# Optimizing a Trainium2 kernel written in Bass

```python
import numpy as np
import jax
import jax.numpy as jnp

def _softmax(x, axis=-1):
    return jax.nn.softmax(x, axis=axis)

def _gelu(x):
    return jax.nn.gelu(x, approximate=True)

def _silu(x):
    return jax.nn.silu(x)

def _sigmoid(x):
    return jax.nn.sigmoid(x)

def _layernorm(x, axis=-1, eps=1e-05):
    m = jnp.mean(x, axis=axis, keepdims=True)
    v = jnp.var(x, axis=axis, keepdims=True)
    return (x - m) / jnp.sqrt(v + eps)

def _scatter_add(tgt, idx, src, axis=0):
    return tgt.at[idx].add(src)

def _segment_sum(src, seg, n):
    return jax.ops.segment_sum(src, seg, n)
kernel_name = 'mk_decoder_postln_d1_seqx_r4_f04095'

def setup_inputs(seed: int=0):
    np.random.seed(seed)
    _w = jnp.asarray

    def _rec_inputs():
        import jax
        import jax.numpy as jnp
        _rk = jax.random.key(seed)
        x = -0.0002928 + 1 * jax.random.normal(jax.random.fold_in(_rk, 1), (16, 128, 256), jnp.float32)
        _lenS = 128 - jax.random.randint(jax.random.fold_in(_rk, 7), (16,), 0, max(1, 128 // 4) + 1, jnp.int32)
        _lenS2 = 128 - jax.random.randint(jax.random.fold_in(_rk, 8), (16,), 0, max(1, 128 // 4) + 1, jnp.int32)
        _ctx_1024P = jax.random.normal(jax.random.fold_in(_rk, 11), (16, 16, 256), jnp.float32)
        _ctx_1024c = jax.random.dirichlet(jax.random.fold_in(_rk, 511), 0.3 * jnp.ones((16,), jnp.float32), (16, 128))
        _ctx_1024t = jnp.einsum('bsk,bkd->bsd', _ctx_1024c, _ctx_1024P)
        _ctx_1024t = _ctx_1024t * jax.lax.rsqrt(jnp.mean(jnp.square(_ctx_1024t)) + 1e-12) * 0.953939
        ctx_1024 = -1.39393e-06 + 0.999914 * (_ctx_1024t + 0.3 * jax.random.normal(jax.random.fold_in(_rk, 611), (16, 128, 256), jnp.float32))
        _validS = jnp.arange(128)[None, :] < _lenS[:, None]
        _validS2 = jnp.arange(128)[None, :] < _lenS2[:, None]
        _causal = jnp.tril(jnp.ones((128, 128), dtype=bool))
        mask_BxS2_ik0 = jnp.where(jnp.broadcast_to(_validS2[:, :], (16, 128)), 0, 1).astype(jnp.int32)
        return (x, ctx_1024, mask_BxS2_ik0)
    x, ctx_1024, mask_BxS2_ik0 = _rec_inputs()

    def _L0_attn_setup():
        import jax, jax.numpy as jnp
        import numpy as np
        HIDDEN = 256
        HEAD_DIM = 64
        N_HEADS = HIDDEN // HEAD_DIM
        BATCH = 2
        SEQ = 512
        ROT_DIM = HEAD_DIM // 2
        THETA = 10000.0
        SCALE_BASE = 512.0
        EPS = 1e-05

        def _layernorm(x, w, b):
            m = jnp.mean(x, axis=-1, keepdims=True)
            v = jnp.mean(jnp.square(x - m), axis=-1, keepdims=True)
            return (x - m) * jax.lax.rsqrt(v + EPS) * w + b

        def _rotate_half(x):
            xs = x.reshape(x.shape[:-1] + (ROT_DIM // 2, 2))
            x1, x2 = (xs[..., 0], xs[..., 1])
            return jnp.stack((-x2, x1), axis=-1).reshape(x.shape)

        def _xpos_rotary(q, k):
            S = q.shape[-2]
            half = jnp.arange(0, ROT_DIM, 2, dtype=jnp.float32)
            inv_freq = 1.0 / THETA ** (half / ROT_DIM)
            t = jnp.arange(S, dtype=jnp.float32)
            freqs = jnp.repeat(t[:, None] * inv_freq, 2, axis=-1)
            scale_vals = (half + 0.4 * ROT_DIM) / (1.4 * ROT_DIM)
            power = (t - S // 2) / SCALE_BASE
            scale = scale_vals[None, :] ** power[:, None]
            scale = jnp.concatenate((scale, scale), axis=-1)
            cos, sin = (jnp.cos(freqs), jnp.sin(freqs))

            def apply(x, sc):
                xl, xr = (x[..., :ROT_DIM], x[..., ROT_DIM:])
                xl = xl * cos * sc + _rotate_half(xl) * sin * sc
                return jnp.concatenate((xl, xr), axis=-1)
            return (apply(q, scale), apply(k, 1.0 / scale))

        def _mish(x):
            return x * jnp.tanh(jax.nn.softplus(x))
        key = jax.random.key(seed)
        ks = jax.random.split(key, 8)

        def lin(k, shape, fan_in):
            b = 1.0 / np.sqrt(fan_in)
            return jax.random.uniform(k, shape, jnp.float32, -b, b)
        return {'x': jax.random.normal(ks[0], (BATCH, SEQ, HIDDEN), jnp.float32), 'ln1_w': jnp.ones((HIDDEN,), jnp.float32), 'ln1_b': jnp.zeros((HIDDEN,), jnp.float32), 'wqkv_w': lin(ks[1], (HIDDEN, 3 * HIDDEN), HIDDEN), 'wg_w': lin(ks[2], (HIDDEN, HIDDEN), HIDDEN), 'wo_w': lin(ks[3], (HIDDEN, HIDDEN), HIDDEN), 'gn_w': jnp.ones((N_HEADS,), jnp.float32), 'gn_b': jnp.zeros((N_HEADS,), jnp.float32), 'ln2_w': jnp.ones((HIDDEN,), jnp.float32), 'ln2_b': jnp.zeros((HIDDEN,), jnp.float32), 'w1_w': lin(ks[4], (HIDDEN, HIDDEN), HIDDEN), 'w1_b': lin(ks[5], (HIDDEN,), HIDDEN), 'w2_w': lin(ks[6], (HIDDEN, HIDDEN), HIDDEN), 'w2_b': lin(ks[7], (HIDDEN,), HIDDEN)}
    _L0_attn_all = _L0_attn_setup()
    _L0_attn_in = {k: v for k, v in _L0_attn_all.items() if k in ('ln1_w', 'ln1_b', 'wqkv_w', 'wg_w', 'wo_w', 'gn_w', 'gn_b', 'ln2_w', 'ln2_b', 'w1_w', 'w1_b', 'w2_w', 'w2_b')}
    del _L0_attn_all

    def _L0_xattn_setup():
        import jax, jax.numpy as jnp
        import numpy as np
        import math
        N_HEAD = 16
        key = jax.random.key(seed)
        ks = jax.random.split(key, 9)
        B, T, D = (2, 512, 256)
        s = 1.0 / math.sqrt(D)
        return {'queries': jax.random.normal(ks[0], (B, T, D), jnp.float32), 'keys': jax.random.normal(ks[1], (B, T, D), jnp.float32), 'key_mask': jax.random.randint(ks[2], (B, T), 0, 2, jnp.int32), 'Wq': jax.random.normal(ks[3], (D, D), jnp.float32) * s, 'bq': jax.random.normal(ks[4], (D,), jnp.float32) * 0.01, 'Wk': jax.random.normal(ks[5], (D, D), jnp.float32) * s, 'bk': jax.random.normal(ks[6], (D,), jnp.float32) * 0.01, 'Wv': jax.random.normal(ks[7], (D, D), jnp.float32) * s, 'bv': jax.random.normal(ks[8], (D,), jnp.float32) * 0.01}
    _L0_xattn_all = _L0_xattn_setup()
    _L0_xattn_in = {k: v for k, v in _L0_xattn_all.items() if k in ('Wq', 'bq', 'Wk', 'bk', 'Wv', 'bv')}
    del _L0_xattn_all

    def _L0_ffn_setup():
        import jax, jax.numpy as jnp
        import numpy as np
        D_MODEL = 256
        HIDDEN = 512
        N_EXPERTS = 8
        TOP_K = 2
        BATCH = 2
        SEQ = 512
        key = jax.random.key(seed)
        ks = jax.random.split(key, 9)
        s = 0.02
        return {'x': jax.random.normal(ks[0], (BATCH, SEQ, D_MODEL), dtype=jnp.float32), 'w_router': jax.random.normal(ks[1], (D_MODEL, N_EXPERTS), dtype=jnp.float32) * s, 'w1': jax.random.normal(ks[2], (N_EXPERTS, D_MODEL, HIDDEN), dtype=jnp.float32) * s, 'w3': jax.random.normal(ks[3], (N_EXPERTS, D_MODEL, HIDDEN), dtype=jnp.float32) * s, 'w2': jax.random.normal(ks[4], (N_EXPERTS, HIDDEN, D_MODEL), dtype=jnp.float32) * s, 'sw1': jax.random.normal(ks[5], (D_MODEL, HIDDEN), dtype=jnp.float32) * s, 'sw3': jax.random.normal(ks[6], (D_MODEL, HIDDEN), dtype=jnp.float32) * s, 'sw2': jax.random.normal(ks[7], (HIDDEN, D_MODEL), dtype=jnp.float32) * s}
    _L0_ffn_all = _L0_ffn_setup()
    _L0_ffn_in = {k: v for k, v in _L0_ffn_all.items() if k in ('w_router', 'w1', 'w3', 'w2', 'sw1', 'sw3', 'sw2')}
    del _L0_ffn_all
    return {'x': x, 'ctx_1024': ctx_1024, 'mask_BxS2_ik0': mask_BxS2_ik0, 'L0_attn_ln1_w': _L0_attn_in['ln1_w'], 'L0_attn_ln1_b': _L0_attn_in['ln1_b'], 'L0_attn_wqkv_w': _L0_attn_in['wqkv_w'], 'L0_attn_wg_w': _L0_attn_in['wg_w'], 'L0_attn_wo_w': _L0_attn_in['wo_w'], 'L0_attn_gn_w': _L0_attn_in['gn_w'], 'L0_attn_gn_b': _L0_attn_in['gn_b'], 'L0_attn_ln2_w': _L0_attn_in['ln2_w'], 'L0_attn_ln2_b': _L0_attn_in['ln2_b'], 'L0_attn_w1_w': _L0_attn_in['w1_w'], 'L0_attn_w1_b': _L0_attn_in['w1_b'], 'L0_attn_w2_w': _L0_attn_in['w2_w'], 'L0_attn_w2_b': _L0_attn_in['w2_b'], 'L0_xattn_Wq': _L0_xattn_in['Wq'], 'L0_xattn_bq': _L0_xattn_in['bq'], 'L0_xattn_Wk': _L0_xattn_in['Wk'], 'L0_xattn_bk': _L0_xattn_in['bk'], 'L0_xattn_Wv': _L0_xattn_in['Wv'], 'L0_xattn_bv': _L0_xattn_in['bv'], 'L0_ffn_w_router': _L0_ffn_in['w_router'], 'L0_ffn_w1': _L0_ffn_in['w1'], 'L0_ffn_w3': _L0_ffn_in['w3'], 'L0_ffn_w2': _L0_ffn_in['w2'], 'L0_ffn_sw1': _L0_ffn_in['sw1'], 'L0_ffn_sw3': _L0_ffn_in['sw3'], 'L0_ffn_sw2': _L0_ffn_in['sw2']}

def reference(x, ctx_1024, mask_BxS2_ik0, L0_attn_ln1_w, L0_attn_ln1_b, L0_attn_wqkv_w, L0_attn_wg_w, L0_attn_wo_w, L0_attn_gn_w, L0_attn_gn_b, L0_attn_ln2_w, L0_attn_ln2_b, L0_attn_w1_w, L0_attn_w1_b, L0_attn_w2_w, L0_attn_w2_b, L0_xattn_Wq, L0_xattn_bq, L0_xattn_Wk, L0_xattn_bk, L0_xattn_Wv, L0_xattn_bv, L0_ffn_w_router, L0_ffn_w1, L0_ffn_w3, L0_ffn_w2, L0_ffn_sw1, L0_ffn_sw3, L0_ffn_sw2):
    import jax
    import jax.numpy as jnp

    def _L0_attn_ref(x, ln1_w, ln1_b, wqkv_w, wg_w, wo_w, gn_w, gn_b, ln2_w, ln2_b, w1_w, w1_b, w2_w, w2_b):
        import jax, jax.numpy as jnp
        import numpy as np
        HIDDEN = 256
        HEAD_DIM = 64
        N_HEADS = HIDDEN // HEAD_DIM
        BATCH = 2
        SEQ = 512
        ROT_DIM = HEAD_DIM // 2
        THETA = 10000.0
        SCALE_BASE = 512.0
        EPS = 1e-05

        def _layernorm(x, w, b):
            m = jnp.mean(x, axis=-1, keepdims=True)
            v = jnp.mean(jnp.square(x - m), axis=-1, keepdims=True)
            return (x - m) * jax.lax.rsqrt(v + EPS) * w + b

        def _rotate_half(x):
            xs = x.reshape(x.shape[:-1] + (ROT_DIM // 2, 2))
            x1, x2 = (xs[..., 0], xs[..., 1])
            return jnp.stack((-x2, x1), axis=-1).reshape(x.shape)

        def _xpos_rotary(q, k):
            S = q.shape[-2]
            half = jnp.arange(0, ROT_DIM, 2, dtype=jnp.float32)
            inv_freq = 1.0 / THETA ** (half / ROT_DIM)
            t = jnp.arange(S, dtype=jnp.float32)
            freqs = jnp.repeat(t[:, None] * inv_freq, 2, axis=-1)
            scale_vals = (half + 0.4 * ROT_DIM) / (1.4 * ROT_DIM)
            power = (t - S // 2) / SCALE_BASE
            scale = scale_vals[None, :] ** power[:, None]
            scale = jnp.concatenate((scale, scale), axis=-1)
            cos, sin = (jnp.cos(freqs), jnp.sin(freqs))

            def apply(x, sc):
                xl, xr = (x[..., :ROT_DIM], x[..., ROT_DIM:])
                xl = xl * cos * sc + _rotate_half(xl) * sin * sc
                return jnp.concatenate((xl, xr), axis=-1)
            return (apply(q, scale), apply(k, 1.0 / scale))

        def _mish(x):
            return x * jnp.tanh(jax.nn.softplus(x))
        B, S, _ = x.shape
        h = _layernorm(x, ln1_w, ln1_b)
        qkv = (h @ wqkv_w).reshape(B, S, N_HEADS, 3 * HEAD_DIM).transpose(0, 2, 1, 3)
        q, k, v = jnp.split(qkv, 3, axis=-1)
        q, k = _xpos_rotary(q, k)
        gamma = 1.0 - 2.0 ** (-5.0 - jnp.arange(N_HEADS, dtype=jnp.float32))
        idx = jnp.arange(S)
        nm = (idx[:, None] - idx[None, :]).astype(jnp.float32)
        decay = jnp.where(nm >= 0, gamma[:, None, None] ** nm, 0.0)
        ret = jnp.einsum('bhsd,bhtd->bhst', q, k) * decay[None]
        ret = jnp.einsum('bhst,bhtd->bhsd', ret, v)
        m = jnp.mean(ret, axis=(2, 3), keepdims=True)
        va = jnp.mean(jnp.square(ret - m), axis=(2, 3), keepdims=True)
        ret = (ret - m) * jax.lax.rsqrt(va + EPS)
        ret = ret * gn_w[None, :, None, None] + gn_b[None, :, None, None]
        y = ret.transpose(0, 2, 1, 3).reshape(B, S, HIDDEN)
        y = _mish(h @ wg_w) * y
        y = y @ wo_w
        y = y + x
        z = _layernorm(y, ln2_w, ln2_b)
        ffn = jax.nn.gelu(z @ w1_w + w1_b, approximate=False) @ w2_w + w2_b
        return ffn + y

    def _L0_xattn_ref(queries, keys, key_mask, Wq, bq, Wk, bk, Wv, bv):
        import jax, jax.numpy as jnp
        import numpy as np
        import math
        N_HEAD = 16
        B, Tq, D = queries.shape
        Tk = keys.shape[1]
        H = N_HEAD
        dk = D // H
        scale = 1.0 / math.sqrt(dk)
        Q = (queries @ Wq.T + bq).reshape(B, Tq, H, dk)
        K = (keys @ Wk.T + bk).reshape(B, Tk, H, dk)
        V = (keys @ Wv.T + bv).reshape(B, Tk, H, dk)
        Qf = Q.transpose(0, 2, 1, 3).reshape(B * H, Tq, dk)
        Kf = K.transpose(0, 2, 1, 3).reshape(B * H, Tk, dk)
        Vf = V.transpose(0, 2, 1, 3).reshape(B * H, Tk, dk)
        scores = jnp.einsum('nqd,nkd->nqk', Qf, Kf) * scale
        km = jnp.tile(key_mask, (H, 1))
        scores = jnp.where(km[:, None, :] == 0, -1000000000.0, scores)
        attn = jax.nn.softmax(scores, axis=-1)
        qm = jnp.tile(key_mask, (H, 1))[:, :, None].astype(attn.dtype)
        attn = attn * qm
        out = jnp.einsum('nqk,nkd->nqd', attn, Vf)
        out = out.reshape(B, H, Tq, dk).transpose(0, 2, 1, 3).reshape(B, Tq, D)
        return out

    def _L0_ffn_ref(x, w_router, w1, w3, w2, sw1, sw3, sw2):
        import jax, jax.numpy as jnp
        import numpy as np
        D_MODEL = 256
        HIDDEN = 512
        N_EXPERTS = 8
        TOP_K = 2
        BATCH = 2
        SEQ = 512
        b, s, d = x.shape
        xf = x.reshape(b * s, d)
        probs = jax.nn.softmax(xf @ w_router, axis=-1)
        top_vals, top_idx = jax.lax.top_k(probs, TOP_K)
        gates = top_vals / jnp.sum(top_vals, axis=-1, keepdims=True)
        onehot = jax.nn.one_hot(top_idx, N_EXPERTS, dtype=xf.dtype)
        cw = jnp.einsum('tk,tke->te', gates, onehot)
        h1 = jnp.einsum('td,edh->eth', xf, w1)
        h3 = jnp.einsum('td,edh->eth', xf, w3)
        y = jnp.einsum('eth,ehd->etd', jax.nn.silu(h1) * h3, w2)
        out = jnp.einsum('etd,te->td', y, cw)
        out = out + jax.nn.silu(xf @ sw1) * (xf @ sw3) @ sw2
        return out.reshape(b, s, d)
    x = _layernorm(x + _L0_attn_ref(x, L0_attn_ln1_w, L0_attn_ln1_b, L0_attn_wqkv_w, L0_attn_wg_w, L0_attn_wo_w, L0_attn_gn_w, L0_attn_gn_b, L0_attn_ln2_w, L0_attn_ln2_b, L0_attn_w1_w, L0_attn_w1_b, L0_attn_w2_w, L0_attn_w2_b), axis=-1)
    x = _layernorm(x + _L0_xattn_ref(x, ctx_1024, mask_BxS2_ik0, L0_xattn_Wq, L0_xattn_bq, L0_xattn_Wk, L0_xattn_bk, L0_xattn_Wv, L0_xattn_bv), axis=-1)
    x = _layernorm(x + _L0_ffn_ref(x, L0_ffn_w_router, L0_ffn_w1, L0_ffn_w3, L0_ffn_w2, L0_ffn_sw1, L0_ffn_sw3, L0_ffn_sw2), axis=-1)
    return x

_drawn_inputs = setup_inputs


def setup_inputs(seed=0):
    import zlib

    import numpy as np

    out = dict(_drawn_inputs(seed))
    spreads = {'L0_attn_ln1_w': (1.0, 0.2),
     'L0_attn_ln1_b': (0.0, 0.421),
     'L0_attn_gn_w': (1.0, 0.6),
     'L0_attn_gn_b': (0.0, 0.8),
     'L0_attn_ln2_w': (1.0, 0.6),
     'L0_attn_ln2_b': (0.0, 0.768)}
    factors = {'L0_attn_w1_b': 8.0,
     'L0_attn_w2_b': 3.134,
     'L0_xattn_bq': 8.0,
     'L0_xattn_bk': 64.0,
     'L0_xattn_bv': 8.0,
     'L0_ffn_w_router': 3.858,
     'L0_ffn_w1': 3.366,
     'L0_ffn_w3': 3.337,
     'L0_ffn_w2': 3.331,
     'L0_ffn_sw1': 3.05,
     'L0_ffn_sw3': 2.989,
     'L0_ffn_sw2': 3.002}
    for name, (base, spread) in spreads.items():
        noise = np.random.default_rng([zlib.crc32(name.encode()), seed]).standard_normal(out[name].shape)
        drawn = base * np.exp(spread * noise) if base else spread * noise
        out[name] = jnp.asarray(drawn.astype(out[name].dtype))
    for name, factor in factors.items():
        out[name] = (out[name] * factor).astype(out[name].dtype)
    return out
```

```python
from contextlib import ExitStack

import numpy as np
import concourse.bass as bass
from concourse import mybir

F32 = mybir.dt.float32
BF16 = mybir.dt.bfloat16
I32 = mybir.dt.int32
U32 = mybir.dt.uint32
ALU = mybir.AluOpType
ACT = mybir.ActivationFunctionType
AX = mybir.AxisListType

P = 128
D = 256
DC = D // P
NB = 16
RH, RD = 4, 64
ROT = 32
XH, XD = 16, 16
NE, HID = 8, 512
HC = HID // P
TOP = 2
BLOCKS = (NB * P * TOP + NE * (P - 1)) // P
HALF = NB // 2
U2 = HALF + BLOCKS
EPS = 1e-5
MASKED = -1e9 * XD ** 0.5
U_MAX = 20.0


def build(nc, a):
    ctx = ExitStack()
    with ctx:
        def sb(name, shape, dt=F32):
            return ctx.enter_context(nc.sbuf_tensor(name, shape, dt))

        def sem(name):
            return ctx.enter_context(nc.semaphore(name))

        bank = [ctx.enter_context(nc.psum_tensor(f"bank{n}", [P, 512], F32)) for n in range(8)]

        X = sb("X", [P, NB, D])
        Y = sb("Y", [P, NB, D])

        def carve(name, *lots):
            whole = sb(name, [P, max(sum(int(np.prod(shape)) for shape in lot) for lot in lots)])
            out = []
            for lot in lots:
                at = 0
                for shape in lot:
                    n = int(np.prod(shape))
                    v = whole[:, at:at + n]
                    if len(shape) == 2:
                        v = v.rearrange("p (a b) -> p a b", a=shape[0])
                    elif len(shape) == 3:
                        v = v.rearrange("p (a b c) -> p a b c", a=shape[0], b=shape[1])
                    out.append(v)
                    at += n
            return out

        (w_qk, w_v, w_g, w_o, w_f1, w_f2, decay,
         xin, xT, sil, hh, hhT, y_st, yg, out_sb, out_t) = carve(
            "weights_a_or_tiles_m",
            [(DC, 2 * D), (DC, D), (DC, D), (DC, D), (DC, D), (DC, D), (RH, P)],
            [(D,), (DC, P), (HID,), (HID,), (HC, P), (D,), (2, TOP, D), (2, D), (D,)])

        (qk, qk_u, qT, k_pad, v, uc, m_e, m_r, m_u, s_dec, yn, yT,
         prob, pT, cxT, x2s) = carve(
            "tiles_a_or_tiles_x",
            [(2, RH, RD), (2 * RH, ROT), (DC, P), (RH, P), (D,), (D,), (D,), (D,), (D,), (RH, P), (D,), (DC, P)],
            [(4, 512), (2, 512), (2 * DC, P), (D,)])

        rot_c, rot_s, hot, pos, pos_e, blk_all = carve(
            "tables_a_or_tiles_r",
            [(2 * RH, RD), (2 * RH, ROT)],
            [(TOP, NB, NE), (NB, NE), (TOP, NB, NE), (BLOCKS, NE)])
        blk = blk_all[0:1, :, :]
        mask_row = Y[:, 0:2, :].rearrange("p b d -> p (b d)").bitcast(I32)

        w_xq = sb("w_xq", [P, DC, D])
        w_xk = sb("w_xk", [P, DC, D])
        w_xv = sb("w_xv", [P, DC, D])
        w_rt = sb("w_rt", [P, DC, NE])
        s_w1 = sb("s_w1", [P, DC, HID])
        s_w3 = sb("s_w3", [P, DC, HID])
        s_w2 = sb("s_w2", [P, HC, D])
        e_w1 = sb("e_w1", [P, DC, NE, HID])
        e_w3 = sb("e_w3", [P, DC, NE, HID])
        e_w2 = sb("e_w2", [P, HC, NE, D])
        cols = sb("cols", [P, 14])
        ln1_w, ln1_b, ln2_w, ln2_b, f1_b, xq_b, xk_b = (cols[:, 2 * n:2 * n + 2] for n in range(7))
        gn = sb("gn", [P, 2, RH])
        f2_b = sb("f2_b", [P, D])
        xv_b = sb("xv_b", [P, D])
        eye = sb("eye", [P, P])
        misc = sb("misc", [P, 2 * P + NE + BLOCKS + 2 + 1])
        avg = misc[:, 0:P]
        before = misc[:, P:2 * P]
        expert_no = misc[:, 2 * P:2 * P + NE]
        block_no = misc[:, 2 * P + NE:2 * P + NE + BLOCKS]
        half_of = misc[:, 2 * P + NE + BLOCKS:2 * P + NE + BLOCKS + 2]
        minus_half = misc[:, 2 * P + NE + BLOCKS + 2:2 * P + NE + BLOCKS + 3]
        mask_col = sb("mask_col", [P, XH], I32)
        mask_add = sb("mask_add", [P, 512], BF16)
        mask_mul = sb("mask_mul", [P, XH])
        ones_bf = sb("ones_bf", [P, P], BF16)
        before_bf = sb("before_bf", [P, P], BF16)
        zero = sb("zero", [P, D])

        tick = sb("tick", [1, 1])
        eps = sb("eps", [P, RH])
        bn = sb("bn", [P, 6])
        mv = sb("mv", [P, 2])
        veps = sb("veps", [P, 1])
        rstd = sb("rstd", [P, 1])
        bn2 = sb("bn2", [P, 6])
        mv2 = sb("mv2", [P, 2])
        veps2 = sb("veps2", [P, 1])
        rstd2 = sb("rstd2", [P, 1])
        h = sb("h", [P, D])
        hT = sb("hT", [P, DC, P])
        gst = sb("gst", [P, RH, 8])
        gsum = sb("gsum", [P, RH, 8])
        gv = sb("gv", [P, 8, RH])
        g_sum2 = sb("g_sum2", [P, RH, 2])
        g_veps = sb("g_veps", [P, RH])
        g_rstd = sb("g_rstd", [P, RH])
        gT = sb("gT", [P, DC, P])
        base_sum = sb("base_sum", [P, D])
        t_out = sb("t_out", [P, D])
        cx = sb("cx", [P, D])
        x1s = sb("x1s", [P, D])
        xqT = sb("xqT", [P, DC, P])
        k_bd = sb("k_bd", [P, DC, 2, P])
        v_tmp = sb("v_tmp", [P, XH, XD])
        v_aug = sb("v_aug", [P, XH, XD + 1])
        s_max = sb("s_max", [P, 4, 4])
        rec = sb("rec", [P, 2, XH])
        x2T = sb("x2T", [P, DC, P])
        logit = sb("logit", [P, NB, NE])
        top = sb("top", [P, NB, 8])
        top_i = sb("top_i", [P, NB, 8], U32)
        top_f = sb("top_f", [P, NB, TOP])
        gate = sb("gate", [P, 3, NB])
        hot_bf = sb("hot_bf", [P, NB, NE], BF16)
        cnt = sb("cnt", [P, 4, NE])
        cnt_i = sb("cnt_i", [P, 2, NE], I32)
        scan = sb("scan", [P, 2, 2 * NE])
        pos_f = sb("pos_f", [P, TOP, NB])
        slot = sb("slot", [P, TOP, NB], U32)
        blk_f = sb("blk_f", [1, 2, BLOCKS])
        blk_e = sb("blk_e", [1, BLOCKS], I32)

        xs = nc.dram_tensor("rows_by_slot", (BLOCKS * P, D), F32, kind="Internal").ap()
        ys = nc.dram_tensor("results_by_slot", (BLOCKS * P, D), F32, kind="Internal").ap()

        S = {}
        for name in """x_first x_second x_rest w_attn w_rest w_cross w_moe consts masks xs_zero ctx_in xin_in
            scattered ys_out gath0 gath1 out0 out1
            setup ln_stat ln_rstd h_ready hT_ps hT_ready qk_ps v_ps g_ps rot_mul rot_done qkT_ps qkT_ready
            s_ps s_dec_ready v_ready clamp_done mish_act mish_done av_ps gn_bn gst_ready gs_ps gs_copy gn_small
            gn_rstd gn_ab yn_step gate_done yT_ps yT_ready o_ps y_sum
            z_stat z_rstd z_ready zT_ps zT_ready f_ps g_ready f2_ps base_done ff_sum x1_stat x1_rstd x1_done
            x1_copy tx_ps cxT_ready xs_ps max_done sub_done exp_done xq_ps xqT_ready xkv_ps kv_done v_moved
            p_ps pT_ready pv_ps l_ps l_done o_step x2_stat x2_rstd x2_done x2_moved x2T_ps x2T_ready
            r_dve r_gate cnt_ps slots_ready experts_ready
            t_ps xT_ready h1_ps h3_ps sil_ready hh_ready hhT_ps hhT_ready y_ps y_taken
            c_step c_stat c_rstd c_done""".split():
            S[name] = sem(name)

        block = ctx.enter_context(nc.Block())

        def row(t, b):
            return t[:, b, :] if isinstance(b, int) else t[:, bass.ds(b, 1), :].rearrange("p a d -> p (a d)")

        def rows(w):
            return w.rearrange("(c p) n -> p c n", p=P)

        @block.sync
        def _(sp):
            x_rows = a["x"].rearrange("b s d -> s b d")
            wqkv = a["wqkv"].rearrange("(c p) (h t d) -> p c h t d", p=P, h=RH, t=3)
            sp.dma_start(X[:, 0, :], x_rows[:, 0, :]).then_inc(S["x_first"], 16)
            sp.dma_start(cols[:], a["cols"]).then_inc(S["consts"], 16)
            sp.dma_start(eye[:], a["eye"]).then_inc(S["consts"], 16)
            for c in range(DC):
                for t in range(2):
                    sp.dma_start(w_qk[:, c, :].rearrange("p (h t d) -> p h t d", h=RH, t=2)[:, :, t, :], wqkv[:, c, :, t, :]).then_inc(S["w_attn"], 16)
                sp.dma_start(w_v[:, c, :].rearrange("p (h d) -> p h d", h=RH), wqkv[:, c, :, 2, :]).then_inc(S["w_attn"], 16)
            sp.dma_start(w_g[:], rows(a["wg"])).then_inc(S["w_attn"], 16)
            sp.dma_start(X[:, 1, :], x_rows[:, 1, :]).then_inc(S["x_second"], 16)
            sp.dma_start(rot_c[:], a["rot_c"]).then_inc(S["consts"], 16)
            sp.dma_start(rot_s[:], a["rot_s"]).then_inc(S["consts"], 16)
            sp.dma_start(decay[:], a["decay"]).then_inc(S["consts"], 16)
            sp.dma_start(misc[:], a["misc"]).then_inc(S["consts"], 16)
            sp.dma_start(X[:, 2:, :], x_rows[:, 2:, :]).then_inc(S["x_rest"], 16)
            sp.dma_start(w_o[:], rows(a["wo"])).then_inc(S["w_rest"], 16)
            for dst, name in ((gn[:, 0, :], "gn_w"), (gn[:, 1, :], "gn_b"), (f2_b[:], "f2_b"), (xv_b[:], "xv_b")):
                src = a[name].rearrange("(a d) -> a d", a=1)
                sp.dma_start(dst, src.to_broadcast([P, src.shape[1]])).then_inc(S["w_rest"], 16)
            sp.dma_start(w_f1[:], rows(a["w_f1"])).then_inc(S["w_rest"], 16)
            sp.dma_start(w_f2[:], rows(a["w_f2"])).then_inc(S["w_rest"], 16)
            for g in range(4):
                sp.dma_start(mask_row[32 * g:32 * g + 1, :], a["mask_row"][g:g + 1, :]).then_inc(S["masks"], 16)
            sp.dma_start(mask_col[:], a["mask_col"]).then_inc(S["masks"], 16)
            sp.dma_start(w_xq[:], rows(a["xq"])).then_inc(S["w_cross"], 16)
            sp.dma_start(w_xk[:], rows(a["xk"])).then_inc(S["w_cross"], 16)
            sp.dma_start(w_xv[:], rows(a["xv"])).then_inc(S["w_cross"], 16)
            sp.dma_start(w_rt[:], rows(a["w_router"])).then_inc(S["w_cross"], 16)
            sp.wait_ge(S["setup"], 1)
            sp.dma_start(xs.rearrange("(p n) d -> p n d", p=P), zero[:].rearrange("p (n d) -> p n d", n=1).to_broadcast([P, BLOCKS, D])).then_inc(S["xs_zero"], 16)
            sp.dma_start(s_w1[:], rows(a["sw1"])).then_inc(S["w_moe"], 16)
            sp.dma_start(s_w3[:], rows(a["sw3"])).then_inc(S["w_moe"], 16)
            sp.dma_start(s_w2[:], rows(a["sw2"])).then_inc(S["w_moe"], 16)
            for dst, name in ((e_w1, "w1"), (e_w3, "w3"), (e_w2, "w2")):
                for e in range(NE):
                    sp.dma_start(dst[:, :, e, :], rows(a[name][e])).then_inc(S["w_moe"], 16)

            def load_ctx(b):
                if not (isinstance(b, int) and b == 0):
                    sp.wait_ge(S["tx_ps"], b)
                sp.dma_start(cx[:], a["ctx"][b, :, :] if isinstance(b, int) else
                     a["ctx"][bass.ds(b, 1), :, :].rearrange("a s d -> (a s) d")).then_inc(S["ctx_in"], 16)

            load_ctx(0)
            with sp.Fori(1, NB) as b:
                load_ctx(b)

            sp.wait_ge(S["x2_moved"], NB)

            def load_shared(u, t):
                if not (isinstance(u, int) and u == 0):
                    sp.wait_ge(S["t_ps"], u)
                sp.dma_start(xin[:], row(X, t)).then_inc(S["xin_in"], 16)

            def load_block(u, k):
                sp.wait_ge(S["t_ps"], u)
                sp.dma_start(xin[:], xs[bass.ds(k * P, P), :]).then_inc(S["xin_in"], 16)

            def store_block(u, k):
                sp.wait_ge(S["y_taken"], u + 1)
                sp.dma_start(ys[bass.ds(k * P, P), :], y_st[:]).then_inc(S["ys_out"], 16)

            def store_out(side, t, n):
                sp.wait_ge(S["c_done"], n)
                dst = a["out"][t, :, :] if isinstance(t, int) else a["out"][bass.ds(t, 1), :, :].rearrange("a s d -> (a s) d")
                sp.dma_start(dst, out_sb[:, side, :]).then_inc(S[f"out{side}"], 16)

            load_shared(0, 0)
            with sp.Fori(1, HALF) as u:
                load_shared(u, u)
            sp.wait_ge(S["scattered"], 16 * TOP * NB)
            load_block(HALF, 0)
            load_block(HALF + 1, 1)
            load_block(HALF + 2, 2)
            with sp.Fori(3, BLOCKS) as k:
                load_block(k + HALF, k)
                store_block(k + (HALF - 3), k - 3)
            load_shared(U2, HALF)
            store_block(U2 - 3, BLOCKS - 3)
            load_shared(U2 + 1, HALF + 1)
            store_block(U2 - 2, BLOCKS - 2)
            load_shared(U2 + 2, HALF + 2)
            store_block(U2 - 1, BLOCKS - 1)
            store_out(0, 0, 1)
            for j in range(1, HALF):
                if j + 2 < HALF:
                    load_shared(U2 + j + 2, HALF + j + 2)
                store_out(0, j, 2 * j)
                store_out(1, HALF + j - 1, 2 * j + 1)
            store_out(1, NB - 1, 2 * HALF)
            sp.wait_ge(S["out0"], 16 * HALF)
            sp.wait_ge(S["out1"], 16 * HALF)

        @block.gpsimd
        def _(pool):
            def rsqrt(b, stat, n_stat, done, var, ve, out):
                pool.wait_ge(S[stat], n_stat)
                if not (isinstance(b, int) and b == 0):
                    pool.wait_ge(S[done], 2 * b)
                pool.tensor_tensor(out=ve, in0=var, in1=eps[:, 0:var.shape[1]], op=ALU.add).then_inc(S[done], 1)
                pool.wait_ge(S[done], 2 * b + 1)
                pool.tensor_tensor(out=out, in0=ve, in1=minus_half.to_broadcast(list(out.shape)), op=ALU.pow)\
                    .then_inc(S[done], 1)

            def ln_rsqrt(b):
                rsqrt(b, "ln_stat", 2 * b + 2, "ln_rstd", mv[:, 1:2], veps[:], rstd[:])

            def gn_rsqrt(b):
                rsqrt(b, "gn_small", 5 * b + 5, "gn_rstd", gv[:, 3, :], g_veps[:], g_rstd[:])

            pool.wait_ge(S["consts"], 96)
            ln_rsqrt(0)
            ln_rsqrt(1)

            def a_step(i):
                if not isinstance(i, int) or 2 <= i:
                    gn_rsqrt(i - 2)
                if not isinstance(i, int) or i + 2 < NB:
                    ln_rsqrt(i + 2)

            a_step(0)
            a_step(1)
            a_step(2)
            with pool.Fori(3, NB - 2) as i:
                a_step(i)
            for i in range(NB - 2, NB + 2):
                a_step(i)

            def z_rsqrt(b):
                rsqrt(b, "z_stat", 2 * b + 2, "z_rstd", mv[:, 1:2], veps[:], rstd[:])

            def x1_rsqrt(b):
                rsqrt(b, "x1_stat", 2 * b + 2, "x1_rstd", mv2[:, 1:2], veps2[:], rstd2[:])

            def base(b):
                if not (isinstance(b, int) and b == 0):
                    pool.wait_ge(S["ff_sum"], b)
                else:
                    pool.wait_ge(S["w_rest"], 112)
                pool.wait_ge(S["y_sum"], b + 1)
                xb, yb = row(X, b), row(Y, b)
                pool.tensor_tensor(out=base_sum[:], in0=xb, in1=yb, op=ALU.add).then_inc(S["base_done"], 1)
                pool.wait_ge(S["base_done"], 2 * b + 1)
                pool.tensor_tensor(out=base_sum[:], in0=base_sum[:], in1=f2_b[:], op=ALU.add)\
                    .then_inc(S["base_done"], 1)

            pool.wait_ge(S["ln_rstd"], 2 * NB)
            z_rsqrt(0)
            z_rsqrt(1)

            def b_step(i):
                if not isinstance(i, int) or i + 2 < NB:
                    z_rsqrt(i + 2)
                if not isinstance(i, int) or 1 <= i <= NB:
                    base(i - 1)
                    x1_rsqrt(i - 1)

            b_step(0)
            b_step(1)
            with pool.Fori(2, NB - 2) as i:
                b_step(i)
            for i in range(NB - 2, NB + 1):
                b_step(i)

            def copy_x1(b):
                if not (isinstance(b, int) and b == 0):
                    pool.wait_ge(S["tx_ps"], b)
                pool.wait_ge(S["x1_copy"], b)
                pool.tensor_tensor(out=x1s[:], in0=row(X, b), in1=zero[:], op=ALU.add).then_inc(S["x1_copy"], 1)

            def move_v(b):
                pool.wait_ge(S["kv_done"], b + 1)
                if not (isinstance(b, int) and b == 0):
                    pool.wait_ge(S["pv_ps"], 4 * b)
                    pool.wait_ge(S["v_moved"], b)
                pool.tensor_tensor(out=v_aug[:, :, 0:XD], in0=v_tmp[:], in1=zero[:].rearrange("p (h d) -> p h d", h=XH),
                                   op=ALU.add).then_inc(S["v_moved"], 1)

            def move_x2(b):
                pool.wait_ge(S["x2_done"], b + 1)
                pool.tensor_tensor(out=row(X, b), in0=x2s[:], in1=zero[:], op=ALU.add).then_inc(S["x2_moved"], 1)

            def x2_rsqrt(b):
                rsqrt(b, "x2_stat", 2 * b + 2, "x2_rstd", mv[:, 1:2], veps[:], rstd[:])

            pool.wait_ge(S["x1_done"], NB)
            pool.tensor_copy(x1s[:], X[:, 0, :]).then_inc(S["x1_copy"], 1)
            pool.wait_ge(S["z_rstd"], 2 * NB)

            def x_step(i):
                static = isinstance(i, int)
                if not static or i >= 2:
                    if not static or i - 2 < NB:
                        x2_rsqrt(i - 2)
                if not static or i + 1 < NB:
                    copy_x1(i + 1)
                if not static or 2 <= i < NB + 2:
                    move_x2(i - 2)
                if not static or i < NB:
                    move_v(i)

            x_step(0)
            x_step(1)
            x_step(2)
            with pool.Fori(3, NB - 1) as i:
                x_step(i)
            for i in range(NB - 1, NB + 2):
                x_step(i)

            pool.wait_ge(S["slots_ready"], 1)
            pool.wait_ge(S["xs_zero"], 16)
            pool.wait_ge(S["x2_moved"], NB)
            for t in range(NB):
                for j in range(TOP):
                    pool.indirect_dma_start(
                        out=xs, out_offset=bass.IndirectOffsetOnAxis(ap=slot[:, j, t:t + 1], axis=0),
                        in_=X[:, t, :], in_offset=None).then_inc(S["scattered"], 16)

            pool.wait_ge(S["ys_out"], 16 * BLOCKS)

            def gather(side, t, n):
                if n > 0:
                    pool.wait_ge(S["c_step"], n)
                for j in range(TOP):
                    pool.indirect_dma_start(
                        out=yg[:, side, j, :], out_offset=None, in_=ys,
                        in_offset=bass.IndirectOffsetOnAxis(ap=slot[:, j, t:t + 1], axis=0))\
                        .then_inc(S[f"gath{side}"], 16)

            def out_rsqrt(n):
                rsqrt(n, "c_stat", 2 * n + 2, "c_rstd", mv[:, 1:2], veps[:], rstd[:])

            pool.wait_ge(S["x2_rstd"], 2 * NB)
            gather(0, 0, 0)
            gather(1, HALF, 0)
            out_rsqrt(0)
            gather(0, 1, 2)
            for j in range(1, HALF):
                out_rsqrt(2 * j - 1)
                if j + 1 < HALF:
                    gather(0, j + 1, 4 * j)
                out_rsqrt(2 * j)
                gather(1, HALF + j, 4 * j + 2)
            out_rsqrt(NB - 1)

        @block.tensor
        def _(pe):
            def mm(out, lhsT, rhs, first, last):
                return pe.matmul(out, lhsT, rhs, start=first, stop=last)

            def turn(bk, at, src, n=DC):
                for c in range(n):
                    t = pe.transpose(bk[:, (at + c) * P:(at + c + 1) * P], src[:, c * P:(c + 1) * P], eye[:])
                return t

            def is_(i, lo, hi):
                return not isinstance(i, int) or lo <= i < hi

            def turn_h(b):
                pe.wait_ge(S["h_ready"], b + 1)
                if is_(b, 1, NB):
                    pe.wait_ge(S["hT_ready"], b)
                if is_(b, 3, NB):
                    pe.wait_ge(S["gs_copy"], b - 2)
                turn(bank[0], 0, h).then_inc(S["hT_ps"], 1)

            def products(b):
                pe.wait_ge(S["hT_ready"], b + 1)
                if is_(b, 1, NB):
                    pe.wait_ge(S["rot_mul"], b)
                for c in range(DC):
                    t = mm(bank[1][:], hT[:, c, :], w_qk[:, c, :], c == 0, c == DC - 1)
                t.then_inc(S["qk_ps"], 1)
                if is_(b, 1, NB):
                    pe.wait_ge(S["mish_done"], b)
                for c in range(DC):
                    t = mm(bank[3][:, 0:D], hT[:, c, :], w_g[:, c, :], c == 0, c == DC - 1)
                t.then_inc(S["g_ps"], 1)
                if is_(b, 1, NB):
                    pe.wait_ge(S["v_ready"], b)
                for c in range(DC):
                    t = mm(bank[2][:, 0:D], hT[:, c, :], w_v[:, c, :], c == 0, c == DC - 1)
                t.then_inc(S["v_ps"], 1)

            def turn_qk(b):
                pe.wait_ge(S["rot_done"], b + 1)
                if is_(b, 1, NB):
                    pe.wait_ge(S["qkT_ready"], b)
                turn(bank[4], 0, qk[:].rearrange("p a h d -> p (a h d)"), 4).then_inc(S["qkT_ps"], 1)

            def scores(b):
                pe.wait_ge(S["qkT_ready"], b + 1)
                if is_(b, 1, NB):
                    pe.wait_ge(S["s_dec_ready"], b)
                for n in range(RH):
                    t = mm(bank[5][:, n * P:(n + 1) * P], k_pad[:, n, :], qT[:, n // 2, :], True, True)
                t.then_inc(S["s_ps"], 1)

            def weighted(b):
                pe.wait_ge(S["s_dec_ready"], b + 1)
                pe.wait_ge(S["v_ready"], b + 1)
                if is_(b, 1, NB):
                    pe.wait_ge(S["yn_step"], 2 * b - 1)
                for n in range(RH):
                    t = mm(bank[6][:, n * RD:(n + 1) * RD], s_dec[:, n, :], v[:, n * RD:(n + 1) * RD], True, True)
                t.then_inc(S["av_ps"], 1)

            def group_sums(b):
                pe.wait_ge(S["gst_ready"], b + 1)
                if is_(b, 1, NB):
                    pe.wait_ge(S["gs_copy"], b)
                pe.wait_ge(S["hT_ready"], b + 3 if not isinstance(b, int) else min(b + 3, NB))
                mm(bank[0][:, 0:RH * 8], avg, gst[:].rearrange("p h e -> p (h e)"), True, True).then_inc(S["gs_ps"], 1)

            def turn_y(b):
                pe.wait_ge(S["gate_done"], b + 1)
                if is_(b, 1, NB):
                    pe.wait_ge(S["y_sum"], b)
                turn(bank[7], 0, yn).then_inc(S["yT_ps"], 1)

            def out_product(b):
                pe.wait_ge(S["yT_ready"], b + 1)
                for c in range(DC):
                    t = mm(bank[7][:, 0:D], yT[:, c, :], w_o[:, c, :], c == 0, c == DC - 1)
                t.then_inc(S["o_ps"], 1)

            def a_step(i):
                if is_(i, 1, NB + 1):
                    scores(i - 1)
                if is_(i, 0, NB):
                    products(i)
                if is_(i, 2, NB + 2):
                    turn_y(i - 2)
                if is_(i, 1, NB + 1):
                    weighted(i - 1)
                if is_(i, 0, NB - 1):
                    turn_h(i + 1)
                if is_(i, 0, NB):
                    turn_qk(i)
                if is_(i, 2, NB + 2):
                    out_product(i - 2)
                if is_(i, 1, NB + 1):
                    group_sums(i - 1)

            pe.wait_ge(S["consts"], 96)
            turn_h(0)
            pe.wait_ge(S["w_attn"], 112)
            a_step(0)
            pe.wait_ge(S["w_rest"], 112)
            a_step(1)
            a_step(2)
            with pe.Fori(3, NB - 1) as i:
                a_step(i)
            for i in range(NB - 1, NB + 2):
                a_step(i)

            def turn_z(b):
                pe.wait_ge(S["z_ready"], b + 1)
                if is_(b, 1, NB):
                    pe.wait_ge(S["zT_ready"], b)
                turn(bank[1], 0, h).then_inc(S["zT_ps"], 1)

            def ff_up(b):
                pe.wait_ge(S["zT_ready"], b + 1)
                if is_(b, 1, NB):
                    pe.wait_ge(S["g_ready"], b)
                for o in range(DC):
                    for c in range(DC):
                        t = mm(bank[4][:, o * P:(o + 1) * P], w_f1[:, c, o * P:(o + 1) * P], hT[:, c, :],
                               c == 0, c == DC - 1)
                t.then_inc(S["f_ps"], 1)

            def ff_down(b):
                pe.wait_ge(S["g_ready"], b + 1)
                if is_(b, 1, NB):
                    pe.wait_ge(S["ff_sum"], b)
                for c in range(DC):
                    t = mm(bank[5][:, 0:D], gT[:, c, :], w_f2[:, c, :], c == 0, c == DC - 1)
                t.then_inc(S["f2_ps"], 1)

            def b_step(i):
                if is_(i, 0, NB):
                    ff_up(i)
                if is_(i, 0, NB - 1):
                    turn_z(i + 1)
                if is_(i, 1, NB + 1):
                    ff_down(i - 1)

            turn_z(0)
            b_step(0)
            b_step(1)
            with pe.Fori(2, NB - 1) as i:
                b_step(i)
            b_step(NB - 1)
            b_step(NB)

            def turn_in(b):
                pe.wait_ge(S["ctx_in"], 16 * (b + 1))
                pe.wait_ge(S["x1_copy"], b + 1)
                if is_(b, 1, NB):
                    pe.wait_ge(S["xqT_ready"], b)
                if is_(b, 3, NB):
                    pe.wait_ge(S["x2T_ready"], b - 2)
                turn(bank[6], 0, cx)
                turn(bank[6], DC, x1s).then_inc(S["tx_ps"], 1)

            def x_scores(b):
                pe.wait_ge(S["xqT_ready"], b + 1)
                pe.wait_ge(S["kv_done"], b + 1)
                for g in range(4):
                    if is_(b, 1, NB):
                        pe.wait_ge(S["sub_done"], 4 * b - 3 + g)
                    lo, hi = 32 * g, 32 * g + 32
                    mm(bank[g][:], ones_bf[lo:lo + 1, :], mask_add[lo:lo + 1, :], True, False)
                    for c in range(DC):
                        t = mm(bank[g][:, c * 256:(c + 1) * 256], xqT[lo:hi, c, :],
                               k_bd[lo:hi, c, :, :].rearrange("p j k -> p (j k)"), False, c == DC - 1)
                    t.then_inc(S["xs_ps"], 1)

            def project(b):
                pe.wait_ge(S["cxT_ready"], b + 1)
                for o in range(DC):
                    for c in range(DC):
                        t = mm(bank[6][:, o * P:(o + 1) * P], w_xq[:, c, o * P:(o + 1) * P], cxT[:, DC + c, :],
                               c == 0, c == DC - 1)
                t.then_inc(S["xq_ps"], 1)
                if is_(b, 2, NB):
                    pe.wait_ge(S["o_step"], 4 * b - 5)
                for o in range(DC):
                    for c in range(DC):
                        mm(bank[7][:, o * P:(o + 1) * P], w_xk[:, c, o * P:(o + 1) * P], cxT[:, c, :],
                           c == 0, c == DC - 1)
                for c in range(DC):
                    t = mm(bank[7][:, D:2 * D], cxT[:, c, :], w_xv[:, c, :], c == 0, c == DC - 1)
                t.then_inc(S["xkv_ps"], 1)

            def turn_p(b, g):
                pe.wait_ge(S["exp_done"], 4 * b + g + 1)
                if is_(b, 1, NB) or g >= 2:
                    pe.wait_ge(S["pT_ready"], 4 * b + g - 1)
                turn(bank[4 + g % 2], 0, prob[:, g, :], 4).then_inc(S["p_ps"], 1)

            def x_out(b, g):
                pe.wait_ge(S["pT_ready"], 4 * b + g + 1)
                pe.wait_ge(S["v_moved"], b + 1)
                if g == 0:
                    pe.wait_ge(S["kv_done"], b + 2 if not isinstance(b, int) else min(b + 2, NB))
                    if is_(b, 1, NB):
                        pe.wait_ge(S["o_step"], 4 * b - 1)
                for s in range(4):
                    n = 8 * (s // 2) + 2 * g + s % 2
                    t = mm(bank[7][:, n * (XD + 1):(n + 1) * (XD + 1)], pT[:, g % 2, s * P:(s + 1) * P],
                           v_aug[:, n, :], True, True)
                t.then_inc(S["pv_ps"], 1)

            def turn_x2(b):
                pe.wait_ge(S["x2_done"], b + 1)
                if is_(b, 1, NB):
                    pe.wait_ge(S["x2T_ready"], b)
                pe.wait_ge(S["xqT_ready"], b + 3 if not isinstance(b, int) else min(b + 3, NB))
                turn(bank[6], 0, x2s).then_inc(S["x2T_ps"], 1)

            def router(b):
                pe.wait_ge(S["x2T_ready"], b + 1)
                for c in range(DC):
                    t = mm(bank[7][:, 480:480 + NE], x2T[:, c, :], w_rt[:, c, :], c == 0, c == DC - 1)
                t.then_inc(S["l_ps"], 1)

            def x_step(i):
                if is_(i, 0, NB):
                    turn_in(i)
                if is_(i, 1, NB + 1):
                    x_scores(i - 1)
                if is_(i, 0, NB):
                    project(i)
                b = i - 1
                if is_(i, 1, NB + 1):
                    turn_p(b, 0)
                    turn_p(b, 1)
                if is_(i, 2, NB + 2):
                    turn_x2(i - 2)
                if is_(i, 1, NB + 1):
                    x_out(b, 0)
                    turn_p(b, 2)
                    x_out(b, 1)
                    turn_p(b, 3)
                    x_out(b, 2)
                    x_out(b, 3)
                if is_(i, 2, NB + 2):
                    if isinstance(i, int) and i == NB + 1:
                        pe.wait_ge(S["o_step"], 4 * NB - 1)
                    router(i - 2)

            pe.wait_ge(S["w_cross"], 64)
            pe.wait_ge(S["setup"], 8)
            x_step(0)
            x_step(1)
            x_step(2)
            with pe.Fori(3, NB) as i:
                x_step(i)
            x_step(NB)
            x_step(NB + 1)

            def counts():
                pe.wait_ge(S["r_dve"], 5)
                flat = hot_bf[:].rearrange("p t e -> p (t e)")
                mm(bank[5][:, 0:NB * NE], before_bf[:], flat, True, False)
                for t in range(NB - 1):
                    n = NB - 1 - t
                    mm(bank[5][:, (t + 1) * NE:NB * NE],
                       ones_bf[:], hot_bf[:, t:t + 1, :].to_broadcast([P, n, NE]), False, t == NB - 2)
                for t in range(NB):
                    m = mm(bank[6][:, 0:NE], ones_bf[:], hot_bf[:, t, :], t == 0, t == NB - 1)
                m.then_inc(S["cnt_ps"], 1)

            def turn_rows(u):
                pe.wait_ge(S["xin_in"], 16 * (u + 1))
                if is_(u, 1, 99):
                    pe.wait_ge(S["xT_ready"], u)
                turn(bank[0], 0, xin).then_inc(S["t_ps"], 1)

            def up(u, w1, w3):
                pe.wait_ge(S["xT_ready"], u + 1)
                if is_(u, 1, 99):
                    pe.wait_ge(S["sil_ready"], u)
                for c in range(DC):
                    t = mm(bank[2][:], xT[:, c, :], w1(c), c == 0, c == DC - 1)
                t.then_inc(S["h1_ps"], 1)
                if is_(u, 1, 99):
                    pe.wait_ge(S["hh_ready"], u)
                for c in range(DC):
                    t = mm(bank[3][:], xT[:, c, :], w3(c), c == 0, c == DC - 1)
                t.then_inc(S["h3_ps"], 1)

            def turn_hidden(u):
                pe.wait_ge(S["hh_ready"], u + 1)
                if is_(u, 1, 99):
                    pe.wait_ge(S["hhT_ready"], u)
                turn(bank[1], 0, hh, HC).then_inc(S["hhT_ps"], 1)

            def down(u, w2):
                pe.wait_ge(S["hhT_ready"], u + 1)
                if is_(u, 1, 99):
                    pe.wait_ge(S["y_taken"], u)
                for c in range(HC):
                    t = mm(bank[4][:, 0:D], hhT[:, c, :], w2(c), c == 0, c == HC - 1)
                t.then_inc(S["y_ps"], 1)

            def up_shared(u):
                up(u, lambda c: s_w1[:, c, :], lambda c: s_w3[:, c, :])

            def down_shared(u):
                down(u, lambda c: s_w2[:, c, :])

            def expert_of(k):
                at = blk_e[:, k:k + 1] if isinstance(k, int) else blk_e[:, bass.ds(k, 1)]
                return pe.value_load(at, min_val=0, max_val=NE - 1)

            def up_block(u, k):
                e = expert_of(k)
                one = bass.ds(e, 1)
                up(u, lambda c: e_w1[:, c, one, :].rearrange("p a n -> p (a n)"),
                   lambda c: e_w3[:, c, one, :].rearrange("p a n -> p (a n)"))

            def down_block(u, k):
                one = bass.ds(expert_of(k), 1)
                down(u, lambda c: e_w2[:, c, one, :].rearrange("p a n -> p (a n)"))

            pe.wait_ge(S["w_moe"], 16 * (3 + 3 * NE))
            counts()
            turn_rows(0)
            turn_rows(1)
            up_shared(0)
            turn_hidden(0)
            turn_rows(2)
            up_shared(1)
            down_shared(0)
            with pe.Fori(2, HALF) as u:
                turn_hidden(u - 1)
                turn_rows(u + 1)
                up_shared(u)
                down_shared(u - 1)
            pe.wait_ge(S["experts_ready"], 1)
            turn_hidden(HALF - 1)
            turn_rows(HALF + 1)
            up_block(HALF, 0)
            down_shared(HALF - 1)
            with pe.Fori(1, BLOCKS) as k:
                turn_hidden(k + (HALF - 1))
                turn_rows(k + (HALF + 1))
                up_block(k + HALF, k)
                down_block(k + (HALF - 1), k - 1)
            turn_hidden(U2 - 1)
            turn_rows(U2 + 1)
            up_shared(U2)
            down_block(U2 - 1, BLOCKS - 1)
            with pe.Fori(U2 + 1, U2 + HALF - 1) as u:
                turn_hidden(u - 1)
                turn_rows(u + 1)
                up_shared(u)
                down_shared(u - 1)
            turn_hidden(U2 + HALF - 2)
            up_shared(U2 + HALF - 1)
            down_shared(U2 + HALF - 2)
            turn_hidden(U2 + HALF - 1)
            down_shared(U2 + HALF - 1)

        @block.scalar
        def _(act):
            def f(out, in_, func, **kw):
                return act.activation(out, in_, func, **kw)

            def is_(i, lo, hi):
                return not isinstance(i, int) or lo <= i < hi

            def take_hT(b, ps, ready, bk, w, bias):
                act.wait_ge(S[ps], b + 1)
                for c in range(DC):
                    t = f(hT[:, c, :], bk[:, c * P:(c + 1) * P], ACT.Identity,
                          scale=w[:, c:c + 1], bias=bias[:, c:c + 1])
                t.then_inc(S[ready], 1)

            def take_h(b):
                take_hT(b, "hT_ps", "hT_ready", bank[0], ln1_w, ln1_b)

            def take_yT(b):
                act.wait_ge(S["yT_ps"], b + 1)
                f(yT[:].rearrange("p c s -> p (c s)"), bank[7][:, 0:D], ACT.Copy).then_inc(S["yT_ready"], 1)

            def take_v(b):
                act.wait_ge(S["v_ps"], b + 1)
                if is_(b, 1, NB):
                    act.wait_ge(S["av_ps"], b)
                f(v[:], bank[2][:, 0:D], ACT.Copy).then_inc(S["v_ready"], 1)

            def take_qkT(b):
                act.wait_ge(S["qkT_ps"], b + 1)
                f(qT[:].rearrange("p c s -> p (c s)"), bank[4][:, 0:D], ACT.Copy)
                for j in range(2):
                    lo, hi = j * RD, (j + 1) * RD
                    t = f(k_pad[lo:hi, j::2, :],
                          bank[4][lo:hi, D:2 * D].rearrange("p (c s) -> p c s", c=DC), ACT.Copy)
                t.then_inc(S["qkT_ready"], 1)

            def take_gs(b):
                act.wait_ge(S["gs_ps"], b + 1)
                if is_(b, 1, NB):
                    act.wait_ge(S["gn_small"], 5 * b)
                f(gsum[:].rearrange("p h e -> p (h e)"), bank[0][:, 0:RH * 8], ACT.Copy).then_inc(S["gs_copy"], 1)

            def mish(b):
                act.wait_ge(S["clamp_done"], b + 1)
                if is_(b, 1, NB):
                    act.wait_ge(S["mish_done"], b)
                    act.wait_ge(S["mish_act"], 4 * b)
                f(m_e[:], uc[:], ACT.Exp).then_inc(S["mish_act"], 1)
                act.wait_ge(S["mish_act"], 4 * b + 1)
                f(m_e[:], m_e[:], ACT.Square, bias=1.0).then_inc(S["mish_act"], 1)
                act.wait_ge(S["mish_act"], 4 * b + 2)
                f(m_r[:], m_e[:], ACT.Ln, bias=1.0).then_inc(S["mish_act"], 1)
                act.wait_ge(S["mish_act"], 4 * b + 3)
                f(m_r[:], m_r[:], ACT.Exp, scale=-1.0).then_inc(S["mish_act"], 1)

            def a_step(i):
                if is_(i, 2, NB + 2):
                    take_yT(i - 2)
                if is_(i, 0, NB):
                    take_v(i)
                if is_(i, 0, NB - 1):
                    take_h(i + 1)
                if is_(i, 0, NB):
                    take_qkT(i)
                if is_(i, 1, NB + 1):
                    take_gs(i - 1)
                if is_(i, 0, NB):
                    mish(i)

            act.wait_ge(S["consts"], 96)
            act.wait_ge(S["setup"], 3)
            take_h(0)
            a_step(0)
            a_step(1)
            with act.Fori(2, NB - 1) as i:
                a_step(i)
            for i in range(NB - 1, NB + 2):
                a_step(i)

            def take_z(b):
                take_hT(b, "zT_ps", "zT_ready", bank[1], ln2_w, ln2_b)

            def gelu(b):
                act.wait_ge(S["f_ps"], b + 1)
                if is_(b, 1, NB):
                    act.wait_ge(S["f2_ps"], b)
                for c in range(DC):
                    t = f(gT[:, c, :], bank[4][:, c * P:(c + 1) * P], ACT.Gelu, bias=f1_b[:, c:c + 1])
                t.then_inc(S["g_ready"], 1)

            def b_step(i):
                if is_(i, 0, NB - 1):
                    take_z(i + 1)
                if is_(i, 0, NB):
                    gelu(i)

            take_z(0)
            b_step(0)
            with act.Fori(1, NB - 1) as i:
                b_step(i)
            gelu(NB - 1)

            def take_in(b):
                act.wait_ge(S["tx_ps"], b + 1)
                f(cxT[:].rearrange("p c s -> p (c s)"), bank[6][:], ACT.Copy).then_inc(S["cxT_ready"], 1)

            def exp(b, g):
                act.wait_ge(S["sub_done"], 4 * b + g + 1)
                f(prob[:, g, :], prob[:, g, :], ACT.Exp, scale=XD ** -0.5).then_inc(S["exp_done"], 1)

            def take_q(b):
                act.wait_ge(S["xq_ps"], b + 1)
                for c in range(DC):
                    t = f(xqT[:, c, :], bank[6][:, c * P:(c + 1) * P], ACT.Identity, bias=xq_b[:, c:c + 1])
                t.then_inc(S["xqT_ready"], 1)

            def take_p(b, g):
                act.wait_ge(S["p_ps"], 4 * b + g + 1)
                f(pT[:, g % 2, :], bank[4 + g % 2][:], ACT.Copy).then_inc(S["pT_ready"], 1)

            def take_x2(b):
                act.wait_ge(S["x2T_ps"], b + 1)
                f(x2T[:].rearrange("p c s -> p (c s)"), bank[6][:, 0:D], ACT.Copy).then_inc(S["x2T_ready"], 1)

            def x_step(i):
                if is_(i, 0, NB):
                    take_in(i)
                if is_(i, 1, NB + 1):
                    for g in range(3):
                        exp(i - 1, g)
                if is_(i, 0, NB):
                    take_q(i)
                if is_(i, 1, NB + 1):
                    exp(i - 1, 3)
                    take_p(i - 1, 0)
                    take_p(i - 1, 1)
                if is_(i, 2, NB + 2):
                    take_x2(i - 2)
                if is_(i, 1, NB + 1):
                    take_p(i - 1, 2)
                    take_p(i - 1, 3)

            x_step(0)
            x_step(1)
            with act.Fori(2, NB) as i:
                x_step(i)
            x_step(NB)
            x_step(NB + 1)

            act.wait_ge(S["r_gate"], 1)
            f(gate[:, 0, :], gate[:, 0, :], ACT.Exp).then_inc(S["r_gate"], 1)


            def take_rows(u):
                act.wait_ge(S["t_ps"], u + 1)
                if is_(u, 1, 99):
                    act.wait_ge(S["h3_ps"], u)
                f(xT[:].rearrange("p c s -> p (c s)"), bank[0][:, 0:D], ACT.Copy).then_inc(S["xT_ready"], 1)

            def silu(u):
                act.wait_ge(S["h1_ps"], u + 1)
                if is_(u, 1, 99):
                    act.wait_ge(S["hh_ready"], u)
                f(sil[:], bank[2][:], ACT.Silu).then_inc(S["sil_ready"], 1)

            def take_block(u, k):
                act.wait_ge(S["y_ps"], u + 1)
                if is_(k, 1, 99):
                    act.wait_ge(S["ys_out"], 16 * k)
                f(y_st[:], bank[4][:, 0:D], ACT.Copy).then_inc(S["y_taken"], 1)

            take_rows(0)
            silu(0)
            take_rows(1)
            with act.Fori(1, HALF + 1) as u:
                silu(u)
                take_rows(u + 1)
            silu(1 + HALF)
            take_rows(2 + HALF)
            take_block(HALF, 0)
            with act.Fori(2, BLOCKS) as k:
                silu(k + HALF)
                take_rows(k + (HALF + 1))
                take_block(k + (HALF - 1), k - 1)
            silu(U2)
            take_rows(U2 + 1)
            take_block(U2 - 1, BLOCKS - 1)
            with act.Fori(U2 + 1, U2 + HALF - 1) as u:
                silu(u)
                take_rows(u + 1)
            silu(U2 + HALF - 1)

        @block.vector
        def _(ve):
            def is_(i, lo, hi):
                return not isinstance(i, int) or lo <= i < hi

            def stats(src, b, name, s6, m2, used):
                if is_(b, 1, NB):
                    ve.wait_ge(S[name], 2 * b)
                    ve.wait_ge(S[used], b)
                ve.bn_stats(s6[:], src).then_inc(S[name], 1)
                ve.wait_ge(S[name], 2 * b + 1)
                ve.memset(tick[:], 0.0)
                ve.bn_aggr(m2[:], s6[:]).then_inc(S[name], 1)

            def normal(dst, src, b, name, m2, r, done):
                ve.wait_ge(S[name], 2 * b + 2)
                ve.tensor_scalar(dst, src, m2[:, 0:1], r[:], ALU.subtract, ALU.mult).then_inc(S[done], 1)

            ve.memset(zero[:], 0.0).then_inc(S["setup"], 1)
            ve.memset(k_pad[:], 0.0).then_inc(S["setup"], 1)
            ve.memset(eps[:], EPS)
            ve.memset(v_aug[:], 1.0).then_inc(S["setup"], 1)
            ve.memset(ones_bf[:], 1.0).then_inc(S["setup"], 1)
            ve.memset(scan[:], 0.0).then_inc(S["setup"], 1)
            ve.wait_ge(S["masks"], 80)
            for g in range(4):
                one = slice(32 * g, 32 * g + 1)
                t = ve.tensor_scalar(mask_add[one, :], mask_row[one, :], 0.0, MASKED, ALU.is_equal, ALU.mult)
            t.then_inc(S["setup"], 1)
            ve.tensor_copy(mask_mul[:], mask_col[:]).then_inc(S["setup"], 1)
            ve.wait_ge(S["consts"], 96)
            ve.tensor_copy(before_bf[:], before).then_inc(S["setup"], 1)
            ve.wait_ge(S["x_first"], 16)

            def ln_stats(b):
                stats(row(X, b), b, "ln_stat", bn, mv, "h_ready")

            def ln_apply(b):
                if is_(b, 1, NB):
                    ve.wait_ge(S["hT_ps"], b)
                normal(h[:], row(X, b), b, "ln_rstd", mv, rstd, "h_ready")

            ln_stats(0)
            ln_apply(0)
            ve.wait_ge(S["x_second"], 16)
            ln_stats(1)
            ve.wait_ge(S["x_rest"], 16)
            ve.wait_ge(S["w_rest"], 112)

            def rotary(b):
                ve.wait_ge(S["qk_ps"], b + 1)
                if is_(b, 1, NB):
                    ve.wait_ge(S["rot_done"], b)
                ps = bank[1][:].rearrange("p (h a d) -> p h a d", h=RH, a=2)
                ve.tensor_tensor(qk[:].rearrange("p a h d -> p h a d"), ps,
                                 rot_c[:].rearrange("p (h a) d -> p h a d", a=2), ALU.mult)
                pairs = bank[1][:].rearrange("p (g d) -> p g d", d=RD)[:, :, 0:ROT]\
                    .rearrange("p g (j t) -> p g j t", t=2)
                u = qk_u[:].rearrange("p g (j t) -> p g j t", t=2)
                s = rot_s[:].rearrange("p g (j t) -> p g j t", t=2)
                ve.tensor_tensor(u[:, :, :, 0], pairs[:, :, :, 1], s[:, :, :, 0], ALU.mult)
                ve.tensor_tensor(u[:, :, :, 1], pairs[:, :, :, 0], s[:, :, :, 1], ALU.mult)\
                    .then_inc(S["rot_mul"], 1)
                ve.wait_ge(S["rot_mul"], b + 1)
                q = qk[:].rearrange("p a h d -> p h a d")[:, :, :, 0:ROT]
                ve.tensor_tensor(q, q, qk_u[:].rearrange("p (h a) d -> p h a d", a=2), ALU.add)\
                    .then_inc(S["rot_done"], 1)

            def clamp(b):
                ve.wait_ge(S["g_ps"], b + 1)
                ve.tensor_scalar(uc[:], bank[3][:, 0:D], U_MAX, None, ALU.min).then_inc(S["clamp_done"], 1)

            def mish(b):
                if is_(b, 1, NB):
                    ve.wait_ge(S["gate_done"], b)
                ve.wait_ge(S["mish_act"], 4 * b + 4)
                ve.scalar_tensor_tensor(m_u[:], m_r[:], -0.5, bank[3][:, 0:D], ALU.add, ALU.mult)\
                    .then_inc(S["mish_done"], 1)

            def decayed(b):
                ve.wait_ge(S["s_ps"], b + 1)
                ve.tensor_tensor(s_dec[:].rearrange("p h s -> p (h s)"), bank[5][:],
                                 decay[:].rearrange("p h s -> p (h s)"), ALU.mult).then_inc(S["s_dec_ready"], 1)

            def gn_stats(b):
                ve.wait_ge(S["av_ps"], b + 1)
                if is_(b, 1, NB):
                    ve.wait_ge(S["gst_ready"], b)
                for n in range(RH):
                    t = ve.bn_stats(gst[:, n, 0:6], bank[6][:, n * RD:(n + 1) * RD])
                t.then_inc(S["gn_bn"], 1)
                ve.wait_ge(S["gn_bn"], b + 1)
                means = gst[:, :, 1:5:3]
                ve.tensor_tensor(gst[:, :, 6:8], means, means, ALU.mult).then_inc(S["gst_ready"], 1)

            def gn_var(b):
                ve.wait_ge(S["gs_copy"], b + 1)
                if is_(b, 1, NB):
                    ve.wait_ge(S["gn_small"], 5 * b)
                    ve.wait_ge(S["gn_ab"], 3 * b)

                ve.tensor_tensor(g_sum2[:], gsum[:, :, 1:3], gsum[:, :, 4:6], ALU.add).then_inc(S["gn_small"], 1)
                ve.tensor_tensor(gv[:, 0, :], gsum[:, :, 6], gsum[:, :, 7], ALU.add).then_inc(S["gn_small"], 1)
                ve.wait_ge(S["gn_small"], 5 * b + 2)
                s0, s1 = g_sum2[:, :, 0], g_sum2[:, :, 1]
                ve.scalar_tensor_tensor(gv[:, 1, :], s0, 0.25, s0, ALU.mult, ALU.mult).then_inc(S["gn_small"], 1)
                ve.wait_ge(S["gn_small"], 5 * b + 3)
                ve.scalar_tensor_tensor(gv[:, 2, :], s1, 1.0 / RD, gv[:, 1, :], ALU.mult, ALU.subtract).then_inc(S["gn_small"], 1)
                ve.wait_ge(S["gn_small"], 5 * b + 4)
                ve.scalar_tensor_tensor(gv[:, 3, :], gv[:, 0, :], 0.5, gv[:, 2, :], ALU.mult, ALU.add)\
                    .then_inc(S["gn_small"], 1)

            def gn_apply(b):
                ve.wait_ge(S["gn_rstd"], 2 * b + 2)
                if is_(b, 1, NB):
                    ve.wait_ge(S["yn_step"], 2 * b)
                A, mA, B = gv[:, 4, :], gv[:, 5, :], gv[:, 6, :]
                ve.tensor_tensor(A, g_rstd[:], gn[:, 0, :], ALU.mult).then_inc(S["gn_ab"], 1)
                ve.wait_ge(S["gn_ab"], 3 * b + 1)
                ve.scalar_tensor_tensor(mA, g_sum2[:, :, 0], 0.5, A, ALU.mult, ALU.mult).then_inc(S["gn_ab"], 1)
                ve.wait_ge(S["gn_ab"], 3 * b + 2)
                ve.tensor_tensor(B, gn[:, 1, :], mA, ALU.subtract).then_inc(S["gn_ab"], 1)
                if is_(b, 1, NB):
                    ve.wait_ge(S["yT_ps"], b)
                y3 = yn[:].rearrange("p (h d) -> p h d", h=RH)

                def wide(v4):
                    return v4.rearrange("p (h a) -> p h a", a=1).to_broadcast([P, RH, RD])

                ve.tensor_tensor(y3, bank[6][:, 0:D].rearrange("p (h d) -> p h d", h=RH), wide(A), ALU.mult)\
                    .then_inc(S["yn_step"], 1)
                ve.wait_ge(S["gn_ab"], 3 * b + 3)
                ve.wait_ge(S["yn_step"], 2 * b + 1)
                ve.tensor_tensor(y3, y3, wide(B), ALU.add).then_inc(S["yn_step"], 1)
                ve.wait_ge(S["yn_step"], 2 * b + 2)
                ve.wait_ge(S["mish_done"], b + 1)
                ve.scalar_tensor_tensor(yn[:], m_u[:], -2.0, yn[:], ALU.mult, ALU.mult).then_inc(S["gate_done"], 1)

            def y_sum(b):
                ve.wait_ge(S["o_ps"], b + 1)
                ve.tensor_tensor(row(Y, b), bank[7][:, 0:D], row(X, b), ALU.add).then_inc(S["y_sum"], 1)

            def a_step(i):
                if is_(i, 2, NB + 2):
                    gn_var(i - 2)
                if is_(i, 1, NB + 1):
                    decayed(i - 1)
                if is_(i, 2, NB + 2):
                    gn_apply(i - 2)
                if is_(i, 1, NB + 1):
                    mish(i - 1)
                if is_(i, 0, NB - 1):
                    ln_apply(i + 1)
                if is_(i, 0, NB):
                    rotary(i)
                    clamp(i)
                if is_(i, 1, NB + 1):
                    gn_stats(i - 1)
                if is_(i, 0, NB - 2):
                    ln_stats(i + 2)
                if is_(i, 2, NB + 2):
                    y_sum(i - 2)

            ve.wait_ge(S["setup"], 8)
            a_step(0)
            a_step(1)
            a_step(2)
            with ve.Fori(3, NB - 2) as i:
                a_step(i)
            for i in range(NB - 2, NB + 2):
                a_step(i)

            def z_stats(b):
                ve.wait_ge(S["y_sum"], b + 1)
                stats(row(Y, b), b, "z_stat", bn, mv, "z_ready")

            def z_apply(b):
                if is_(b, 1, NB):
                    ve.wait_ge(S["zT_ps"], b)
                normal(h[:], row(Y, b), b, "z_rstd", mv, rstd, "z_ready")

            def ff_sum(b):
                ve.wait_ge(S["f2_ps"], b + 1)
                if is_(b, 1, NB):
                    ve.wait_ge(S["x1_done"], b)
                ve.wait_ge(S["base_done"], 2 * b + 2)
                ve.tensor_tensor(t_out[:], bank[5][:, 0:D], base_sum[:], ALU.add).then_inc(S["ff_sum"], 1)
                ve.wait_ge(S["ff_sum"], b + 1)
                stats(t_out[:], b, "x1_stat", bn2, mv2, "x1_done")

            def x1_apply(b):
                normal(row(X, b), t_out[:], b, "x1_rstd", mv2, rstd2, "x1_done")

            def b_step(i):
                if is_(i, 0, NB - 1):
                    z_apply(i + 1)
                if is_(i, 0, NB - 2):
                    z_stats(i + 2)
                if is_(i, 2, NB + 2):
                    x1_apply(i - 2)
                if is_(i, 1, NB + 1):
                    ff_sum(i - 1)

            ve.wait_ge(S["ln_stat"], 2 * NB)
            ve.wait_ge(S["h_ready"], NB)
            z_stats(0)
            z_apply(0)
            z_stats(1)
            b_step(0)
            b_step(1)
            with ve.Fori(2, NB - 2) as i:
                b_step(i)
            for i in range(NB - 2, NB + 2):
                b_step(i)

            def take_logits(b):
                ve.wait_ge(S["l_ps"], b + 1)
                ve.tensor_copy(row(logit, b), bank[7][:, 480:480 + NE]).then_inc(S["l_done"], 1)

            def x_out(b):
                ve.wait_ge(S["pv_ps"], 4 * b + 4)
                if is_(b, 1, NB):
                    ve.wait_ge(S["o_step"], 4 * b)
                    ve.wait_ge(S["x2_done"], b)
                o = bank[7][:, 0:XH * (XD + 1)].rearrange("p (h d) -> p h d", h=XH)
                ve.reciprocal(rec[:, 0, :], o[:, :, XD]).then_inc(S["o_step"], 1)
                ve.wait_ge(S["o_step"], 4 * b + 1)
                ve.tensor_tensor(rec[:, 1, :], rec[:, 0, :], mask_mul[:], ALU.mult).then_inc(S["o_step"], 1)
                ve.wait_ge(S["o_step"], 4 * b + 2)
                ve.tensor_tensor(t_out[:].rearrange("p (h d) -> p h d", h=XH), o[:, :, 0:XD],
                                 rec[:, 1, :].rearrange("p (h a) -> p h a", a=1).to_broadcast([P, XH, XD]),
                                 ALU.mult).then_inc(S["o_step"], 1)
                ve.wait_ge(S["o_step"], 4 * b + 3)
                ve.tensor_tensor(t_out[:], t_out[:], row(X, b), ALU.add).then_inc(S["o_step"], 1)
                ve.wait_ge(S["o_step"], 4 * b + 4)
                stats(t_out[:], b, "x2_stat", bn, mv, "x2_done")

            def x2_apply(b):
                if is_(b, 1, NB):
                    ve.wait_ge(S["x2T_ps"], b)
                    ve.wait_ge(S["x2_moved"], b)
                normal(x2s[:], t_out[:], b, "x2_rstd", mv, rstd, "x2_done")

            def x_max(b, g):
                ve.wait_ge(S["xs_ps"], 4 * b + g + 1)
                if is_(b, 1, NB):
                    ve.wait_ge(S["sub_done"], 4 * b - 3 + g)
                ve.tensor_reduce(s_max[:, g, :], bank[g][:].rearrange("p (s k) -> p s k", s=4), AX.X, ALU.max)\
                    .then_inc(S["max_done"], 1)

            def x_sub(b, g):
                ve.wait_ge(S["max_done"], 4 * b + g + 1)
                ve.tensor_tensor(prob[:, g, :].rearrange("p (s k) -> p s k", s=4),
                                 bank[g][:].rearrange("p (s k) -> p s k", s=4),
                                 s_max[:, g, :].rearrange("p (s a) -> p s a", a=1).to_broadcast([P, 4, P]),
                                 ALU.subtract).then_inc(S["sub_done"], 1)

            def take_kv(b):
                ve.wait_ge(S["xkv_ps"], b + 1)
                if is_(b, 1, NB):
                    ve.wait_ge(S["v_moved"], b)
                for c in range(DC):
                    ve.scalar_tensor_tensor(
                        k_bd[:, c, :, :],
                        bank[7][:, c * P:(c + 1) * P].rearrange("p (a k) -> p a k", a=1).to_broadcast([P, 2, P]),
                        xk_b[:, c:c + 1],
                        half_of.rearrange("p (j a) -> p j a", a=1).to_broadcast([P, 2, P]), ALU.add, ALU.mult)
                ve.tensor_tensor(v_tmp[:].rearrange("p h d -> p (h d)"), bank[7][:, D:2 * D], xv_b[:], ALU.add)\
                    .then_inc(S["kv_done"], 1)

            def x_step(i):
                b = i - 1
                if is_(i, 3, NB + 3):
                    take_logits(i - 3)
                if is_(i, 2, NB + 2):
                    x_out(i - 2)
                if is_(i, 1, NB + 1):
                    x_max(b, 0)
                    x_max(b, 1)
                    x_sub(b, 0)
                if is_(i, 2, NB + 2):
                    x2_apply(i - 2)
                if is_(i, 1, NB + 1):
                    x_max(b, 2)
                    x_sub(b, 1)
                    x_max(b, 3)
                    x_sub(b, 2)
                    x_sub(b, 3)
                if is_(i, 0, NB):
                    take_kv(i)

            ve.wait_ge(S["z_stat"], 2 * NB)
            ve.wait_ge(S["z_ready"], NB)
            ve.wait_ge(S["x1_done"], NB)
            x_step(0)
            x_step(1)
            x_step(2)
            with ve.Fori(3, NB) as i:
                x_step(i)
            for i in range(NB, NB + 3):
                x_step(i)

            ve.wait_ge(S["l_done"], NB)
            for t in range(NB):
                m = ve.max(top[:, t, :], logit[:, t, :])
            m.then_inc(S["r_dve"], 1)
            ve.wait_ge(S["r_dve"], 1)
            for t in range(NB):
                m = ve.max_index(top_i[:, t, :], top[:, t, :], logit[:, t, :])
            m.then_inc(S["r_dve"], 1)
            ve.tensor_tensor(gate[:, 0, :], top[:, :, 1], top[:, :, 0], ALU.subtract).then_inc(S["r_gate"], 1)
            ve.wait_ge(S["r_dve"], 2)
            ve.tensor_copy(top_f[:], top_i[:, :, 0:TOP]).then_inc(S["r_dve"], 1)
            ve.wait_ge(S["r_dve"], 3)
            numbers = expert_no.rearrange("p (a e) -> p a e", a=1).to_broadcast([P, NB, NE])
            for j in range(TOP):
                m = ve.tensor_tensor(hot[:, j, :, :], top_f[:, :, j:j + 1].to_broadcast([P, NB, NE]), numbers,
                                     ALU.is_equal)
            m.then_inc(S["r_dve"], 1)
            ve.wait_ge(S["r_dve"], 4)
            ve.tensor_tensor(hot_bf[:], hot[:, 0, :, :], hot[:, 1, :, :], ALU.add).then_inc(S["r_dve"], 1)
            ve.wait_ge(S["r_gate"], 2)
            ve.tensor_scalar(gate[:, 2, :], gate[:, 0, :], 1.0, None, ALU.add).then_inc(S["r_gate"], 1)
            ve.wait_ge(S["r_gate"], 3)
            ve.reciprocal(gate[:, 1, :], gate[:, 2, :]).then_inc(S["r_gate"], 1)
            ve.wait_ge(S["r_gate"], 4)
            ve.tensor_tensor(gate[:, 2, :], gate[:, 0, :], gate[:, 1, :], ALU.mult).then_inc(S["r_gate"], 1)
            ve.wait_ge(S["cnt_ps"], 1)
            ve.tensor_scalar(cnt_i[:, 0, :], bank[6][:, 0:NE], float(P - 1), None, ALU.add).then_inc(S["r_dve"], 1)
            ve.wait_ge(S["r_dve"], 6)
            ve.tensor_scalar(cnt_i[:, 1, :], cnt_i[:, 0, :], 7, None, ALU.logical_shift_right).then_inc(S["r_dve"], 1)
            ve.wait_ge(S["r_dve"], 7)
            ve.tensor_copy(scan[:, 0, NE:], cnt_i[:, 1, :]).then_inc(S["r_dve"], 1)
            ve.wait_ge(S["r_dve"], 8)
            ve.tensor_tensor(scan[:, 1, NE:], scan[:, 0, NE:], scan[:, 0, NE - 1:2 * NE - 1], ALU.add).then_inc(S["r_dve"], 1)
            ve.wait_ge(S["r_dve"], 9)
            ve.tensor_tensor(scan[:, 0, NE:], scan[:, 1, NE:], scan[:, 1, NE - 2:2 * NE - 2], ALU.add).then_inc(S["r_dve"], 1)
            ve.wait_ge(S["r_dve"], 10)
            ve.tensor_tensor(scan[:, 1, NE:], scan[:, 0, NE:], scan[:, 0, NE - 4:2 * NE - 4], ALU.add).then_inc(S["r_dve"], 1)
            ve.wait_ge(S["r_dve"], 11)
            ve.tensor_copy(cnt[:, 0, :], cnt_i[:, 1, :]).then_inc(S["r_dve"], 1)
            ve.wait_ge(S["r_dve"], 12)
            ve.tensor_tensor(cnt[:, 1, :], scan[:, 1, NE:], cnt[:, 0, :], ALU.subtract).then_inc(S["r_dve"], 1)
            ve.wait_ge(S["r_dve"], 13)
            ve.scalar_tensor_tensor(
                pos[:], cnt[:, 1:2, :].to_broadcast([P, NB, NE]), float(P),
                bank[5][:, 0:NB * NE].rearrange("p (t e) -> p t e", t=NB), ALU.mult, ALU.add).then_inc(S["r_dve"], 1)
            ve.wait_ge(S["r_dve"], 14)
            ve.tensor_tensor(pos_e[:, 0, :, :], hot[:, 0, :, :], pos[:], ALU.mult).then_inc(S["r_dve"], 1)
            ve.wait_ge(S["r_dve"], 15)
            ve.tensor_tensor(pos_e[:, 1, :, :], hot[:, 1, :, :], pos[:], ALU.mult).then_inc(S["r_dve"], 1)
            ve.wait_ge(S["r_dve"], 16)
            ve.tensor_reduce(pos_f[:].rearrange("p j t -> p (j t)"),
                                     pos_e[:].rearrange("p j t e -> p (j t) e"), AX.X, ALU.add).then_inc(S["r_dve"], 1)
            ve.wait_ge(S["r_dve"], 17)
            ve.tensor_copy(slot[:], pos_f[:]).then_inc(S["r_dve"], 1)
            ve.wait_ge(S["r_dve"], 18)
            ve.memset(blk_f[:, 1, :], 0.0).then_inc(S["slots_ready"], 1)
            ve.tensor_tensor(blk[:], scan[0:1, 1:2, NE:].to_broadcast([1, BLOCKS, NE]),
                                    block_no[0:1, :].rearrange("p (b a) -> p b a", a=1).to_broadcast([1, BLOCKS, NE]),
                                    ALU.is_le).then_inc(S["r_dve"], 1)
            ve.wait_ge(S["r_dve"], 19)
            ve.tensor_reduce(blk_f[:, 0, :], blk[:], AX.X, ALU.add).then_inc(S["r_dve"], 1)
            ve.wait_ge(S["r_dve"], 20)
            ve.tensor_scalar(blk_e[:], blk_f[:, 0, :], float(NE - 1), None, ALU.min).then_inc(S["experts_ready"], 1)


            def gated(u):
                ve.wait_ge(S["h3_ps"], u + 1)
                ve.wait_ge(S["sil_ready"], u + 1)
                ve.tensor_tensor(hh[:], bank[3][:], sil[:], ALU.mult).then_inc(S["hh_ready"], 1)

            def take_hidden(u):
                ve.wait_ge(S["hhT_ps"], u + 1)
                ve.tensor_copy(hhT[:].rearrange("p c s -> p (c s)"), bank[1][:]).then_inc(S["hhT_ready"], 1)

            def take_shared(u, t):
                ve.wait_ge(S["y_ps"], u + 1)
                ve.tensor_tensor(row(Y, t), bank[4][:, 0:D], row(X, t), ALU.add).then_inc(S["y_taken"], 1)

            gated(0)
            with ve.Fori(1, HALF) as u:
                take_hidden(u - 1)
                gated(u)
                take_shared(u - 1, u - 1)
            take_hidden(HALF - 1)
            gated(HALF)
            take_shared(HALF - 1, HALF - 1)
            with ve.Fori(HALF + 1, U2 + 1) as u:
                take_hidden(u - 1)
                gated(u)

            gathers = [0, 0]
            stores = [0, 0]

            def combine(n, side, t):
                if n:
                    ve.wait_ge(S["c_done"], n)
                gathers[side] += 16 * TOP
                ve.wait_ge(S[f"gath{side}"], gathers[side])
                ve.wait_ge(S["y_taken"], t + 1 if t < HALF else U2 + t - HALF + 1)
                ve.scalar_tensor_tensor(out_t[:], yg[:, side, 0, :], gate[:, 1, t:t + 1], Y[:, t, :],
                                        ALU.mult, ALU.add).then_inc(S["c_step"], 1)
                ve.wait_ge(S["c_step"], 2 * n + 1)
                ve.scalar_tensor_tensor(out_t[:], yg[:, side, 1, :], gate[:, 2, t:t + 1], out_t[:],
                                        ALU.mult, ALU.add).then_inc(S["c_step"], 1)
                ve.wait_ge(S["c_step"], 2 * n + 2)
                stats(out_t[:], n, "c_stat", bn, mv, "c_done")
                if stores[side]:
                    ve.wait_ge(S[f"out{side}"], stores[side])
                normal(out_sb[:, side, :], out_t[:], n, "c_rstd", mv, rstd, "c_done")
                stores[side] += 16

            ve.wait_ge(S["r_gate"], 5)
            ve.wait_ge(S["x2_stat"], 2 * NB)
            ve.wait_ge(S["x2_done"], NB)
            for j in range(1, HALF + 1):
                u = U2 + j
                take_hidden(u - 1)
                if j < HALF:
                    gated(u)
                if j == 1:
                    combine(0, 0, 0)
                if j < HALF:
                    combine(2 * j - 1, 0, j)
                take_shared(u - 1, HALF + j - 1)
                combine(2 * j if j < HALF else NB - 1, 1, HALF + j - 1)


def tables():
    half = np.arange(0, ROT, 2, dtype=np.float64)
    t = np.arange(P, dtype=np.float64)
    freqs = np.repeat(t[:, None] / 10000.0 ** (half / ROT), 2, axis=-1)
    scale = ((half + 0.4 * ROT) / (1.4 * ROT))[None, :] ** ((t - P // 2) / 512.0)[:, None]
    scale = np.concatenate((scale, scale), axis=-1)
    rot_c = np.ones((P, RH, 2, RD))
    rot_s = np.zeros((P, RH, 2, ROT))
    sign = np.where(np.arange(ROT) % 2 == 0, -1.0, 1.0)
    for n, s in enumerate((scale, 1.0 / scale)):
        rot_c[:, :, n, :ROT] = (np.cos(freqs) * s)[:, None, :]
        rot_s[:, :, n, :] = (np.sin(freqs) * s * sign)[:, None, :]
    gamma = 1.0 - 2.0 ** (-5.0 - np.arange(RH))
    apart = t[None, :] - t[:, None]
    decay = np.where(apart[:, None, :] >= 0, gamma[None, :, None] ** np.maximum(apart, 0)[:, None, :], 0.0)
    misc = np.zeros((P, 2 * P + NE + BLOCKS + 3))
    misc[:, 0:P] = 1.0 / P
    misc[:, P:2 * P] = np.arange(P)[:, None] < np.arange(P)[None, :]
    at = 2 * P
    misc[:, at:at + NE] = np.arange(NE)
    misc[:, at + NE:at + NE + BLOCKS] = np.arange(BLOCKS)
    at += NE + BLOCKS
    misc[:, at:at + 2] = (np.arange(P)[:, None] // XD) % 2 == np.arange(2)[None, :]
    misc[:, at + 2] = -0.5
    f = np.float32
    return {"rot_c": rot_c.reshape(P, 2 * RH, RD).astype(f), "rot_s": rot_s.reshape(P, 2 * RH, ROT).astype(f),
            "decay": decay.astype(f), "misc": misc.astype(f), "eye": np.eye(P, dtype=f)}


def kernel(**inputs):
    import concourse.bacc as _bacc
    from concourse.bass_utils import run_bass_kernel_spmd as _run

    g = {k: np.asarray(v) for k, v in inputs.items()}
    attn, cross, ffn = "L0_attn_", "L0_xattn_", "L0_ffn_"

    def columns(*names):
        return np.concatenate([g[n].reshape(DC, P).T for n in names], axis=1)

    mask = g["mask_BxS2_ik0"]
    order = [8 * c + 2 * r + j for r in range(4) for c in range(2) for j in range(2)]
    arrays = {
        "x": g["x"], "ctx": g["ctx_1024"],
        "wqkv": g[attn + "wqkv_w"], "wg": g[attn + "wg_w"], "wo": g[attn + "wo_w"],
        "w_f1": g[attn + "w1_w"], "w_f2": g[attn + "w2_w"], "f2_b": g[attn + "w2_b"],
        "gn_w": g[attn + "gn_w"], "gn_b": g[attn + "gn_b"],
        "cols": columns(attn + "ln1_w", attn + "ln1_b", attn + "ln2_w", attn + "ln2_b", attn + "w1_b",
                        cross + "bq", cross + "bk"),
        "xq": g[cross + "Wq"].T, "xk": g[cross + "Wk"].T, "xv": g[cross + "Wv"].T, "xv_b": g[cross + "bv"],
        "mask_row": mask[order].reshape(4, 4 * P), "mask_col": mask.T,
        "w_router": g[ffn + "w_router"], "w1": g[ffn + "w1"], "w3": g[ffn + "w3"], "w2": g[ffn + "w2"],
        "sw1": g[ffn + "sw1"], "sw3": g[ffn + "sw3"], "sw2": g[ffn + "sw2"],
    } | tables()
    nc = _bacc.Bacc("TRN2", target_bir_lowering=False, num_devices=1)
    feeds, aps = {}, {}
    for name, value in arrays.items():
        value = np.ascontiguousarray(value)
        feeds[f"in_{name}_dram"] = value
        aps[name] = nc.dram_tensor(f"in_{name}_dram", value.shape, mybir.dt.from_np(value.dtype),
                                   kind="ExternalInput").ap()
    aps["out"] = nc.dram_tensor("out_0_dram", (NB, P, D), F32, kind="ExternalOutput").ap()
    build(nc, aps)
    r = _run(nc, [feeds], core_ids=[0])
    return r.results[0]["out_0_dram"]
```

```python
from contextlib import ExitStack

import numpy as np
import concourse.bass as bass
from concourse import mybir

F32 = mybir.dt.float32
BF16 = mybir.dt.bfloat16
I32 = mybir.dt.int32
U32 = mybir.dt.uint32
ALU = mybir.AluOpType
ACT = mybir.ActivationFunctionType
AX = mybir.AxisListType

P = 128
D = 256
DC = D // P
NB = 16
RH, RD = 4, 64
ROT = 32
XH, XD = 16, 16
NE, HID = 8, 512
HC = HID // P
TOP = 2
BLOCKS = (NB * P * TOP + NE * (P - 1)) // P
HALF = NB // 2
U2 = HALF + BLOCKS
EPS = 1e-5
MASKED = -1e9 * XD ** 0.5
U_MAX = 20.0


def build(nc, a):
    ctx = ExitStack()
    with ctx:
        def sb(name, shape, dt=F32):
            return ctx.enter_context(nc.sbuf_tensor(name, shape, dt))

        def sem(name):
            return ctx.enter_context(nc.semaphore(name))

        bank = [ctx.enter_context(nc.psum_tensor(f"bank{n}", [P, 512], F32)) for n in range(8)]

        X = sb("X", [P, NB, D])
        Y = sb("Y", [P, NB, D])

        def carve(name, *lots):
            whole = sb(name, [P, max(sum(int(np.prod(shape)) for shape in lot) for lot in lots)])
            out = []
            for lot in lots:
                at = 0
                for shape in lot:
                    n = int(np.prod(shape))
                    v = whole[:, at:at + n]
                    if len(shape) == 2:
                        v = v.rearrange("p (a b) -> p a b", a=shape[0])
                    elif len(shape) == 3:
                        v = v.rearrange("p (a b c) -> p a b c", a=shape[0], b=shape[1])
                    out.append(v)
                    at += n
            return out

        (w_qkv, w_g, w_o, w_f1, w_f2, decay,
         xin, xT, sil, hh, hhT, y_st, yg, out_sb, out_t) = carve(
            "weights_a_or_tiles_m",
            [(DC, 3 * D), (DC, D), (DC, D), (DC, D), (DC, D), (RH, P)],
            [(D,), (DC, P), (HID,), (HID,), (HC, P), (D,), (2, TOP, D), (2, D), (D,)])

        (qk, qk_u, qT, k_pad, v, uc, m_e, m_r, m_u, s_dec, yn, yT,
         prob, pT, cxT, x2s) = carve(
            "tiles_a_or_tiles_x",
            [(2, RH, RD), (2 * RH, ROT), (DC, P), (RH, P), (D,), (D,), (D,), (D,), (D,), (RH, P), (D,), (DC, P)],
            [(4, 512), (2, 512), (2 * DC, P), (D,)])

        rot_c, rot_s, hot, pos, pos_e, blk_all = carve(
            "tables_a_or_tiles_r",
            [(2 * RH, RD), (2 * RH, ROT)],
            [(TOP, NB, NE), (NB, NE), (TOP, NB, NE), (BLOCKS, NE)])
        blk = blk_all[0:1, :, :]
        mask_row = Y[:, NB - 2:, :].rearrange("p b d -> p (b d)").bitcast(I32)

        w_xq = sb("w_xq", [P, DC, D])
        w_xk = sb("w_xk", [P, DC, D])
        w_xv = sb("w_xv", [P, DC, D])
        w_rt = sb("w_rt", [P, DC, NE])
        s_w1 = sb("s_w1", [P, DC, HID])
        s_w3 = sb("s_w3", [P, DC, HID])
        s_w2 = sb("s_w2", [P, HC, D])
        e_w1 = sb("e_w1", [P, DC, NE, HID])
        e_w3 = sb("e_w3", [P, DC, NE, HID])
        e_w2 = sb("e_w2", [P, HC, NE, D])
        cols = sb("cols", [P, 14])
        ln1_w, ln1_b, ln2_w, ln2_b, f1_b, xq_b, xk_b = (cols[:, 2 * n:2 * n + 2] for n in range(7))
        gn = sb("gn", [P, 2, RH])
        f2_b = sb("f2_b", [P, D])
        xv_b = sb("xv_b", [P, D])
        eye = sb("eye", [P, P])
        misc = sb("misc", [P, 2 * P + NE + BLOCKS + 2 + 1])
        avg = misc[:, 0:P]
        before = misc[:, P:2 * P]
        expert_no = misc[:, 2 * P:2 * P + NE]
        block_no = misc[:, 2 * P + NE:2 * P + NE + BLOCKS]
        half_of = misc[:, 2 * P + NE + BLOCKS:2 * P + NE + BLOCKS + 2]
        minus_half = misc[:, 2 * P + NE + BLOCKS + 2:2 * P + NE + BLOCKS + 3]
        mask_col = sb("mask_col", [P, XH], I32)
        mask_add = sb("mask_add", [P, 512], BF16)
        mask_mul = sb("mask_mul", [P, XH])
        ones_bf = sb("ones_bf", [P, P], BF16)
        before_bf = sb("before_bf", [P, P], BF16)
        zero = sb("zero", [P, D])

        tick = sb("tick", [1, 4])
        eps = sb("eps", [P, RH])
        bn = sb("bn", [P, 6])
        mv = sb("mv", [P, 2])
        veps = sb("veps", [P, 1])
        rstd = sb("rstd", [P, 1])
        bn2 = sb("bn2", [P, 6])
        veps2 = sb("veps2", [P, 1])
        h = sb("h", [P, D])
        hT = sb("hT", [P, DC, P])
        gst = sb("gst", [P, RH, 8])
        gsum = sb("gsum", [P, RH, 8])
        gv = sb("gv", [P, 8, RH])
        g_sum2 = sb("g_sum2", [P, RH, 2])
        g_veps = sb("g_veps", [P, RH])
        g_rstd = sb("g_rstd", [P, RH])
        gT = sb("gT", [P, 2, DC, P])
        u_raw = sb("u_raw", [P, D])
        z_mv = sb("z_mv", [P, 2, 2])
        z_rs = sb("z_rs", [P, 2, 1])
        x1_mv = sb("x1_mv", [P, 2, 2])
        x1_rs = sb("x1_rs", [P, 2, 1])
        pool_tick = sb("pool_tick", [1, 2])
        t_out = sb("t_out", [P, D])
        cx = sb("cx", [P, D])
        x1s = sb("x1s", [P, D])
        xqT = sb("xqT", [P, DC, P])
        k_bd = sb("k_bd", [P, DC, 2, P])
        v_tmp = sb("v_tmp", [P, XH, XD])
        v_aug = sb("v_aug", [P, XH, XD + 1])
        s_max = sb("s_max", [P, 4, 4])
        rec = sb("rec", [P, 2, XH])
        x2T = sb("x2T", [P, DC, P])
        logit = sb("logit", [P, NB, NE])
        top = sb("top", [P, NB, 8])
        top_i = sb("top_i", [P, NB, 8], U32)
        top_f = sb("top_f", [P, NB, TOP])
        gate = sb("gate", [P, 3, NB])
        hot_bf = sb("hot_bf", [P, NB, NE], BF16)
        cnt = sb("cnt", [P, 4, NE])
        cnt_i = sb("cnt_i", [P, 2, NE], I32)
        scan = sb("scan", [P, 2, 2 * NE])
        pos_f = sb("pos_f", [P, TOP, NB])
        slot = sb("slot", [P, TOP, NB], U32)
        blk_f = sb("blk_f", [1, 2, BLOCKS])
        blk_e = sb("blk_e", [1, BLOCKS], I32)

        xs = nc.dram_tensor("rows_by_slot", (BLOCKS * P, D), F32, kind="Internal").ap()
        ys = nc.dram_tensor("results_by_slot", (BLOCKS * P, D), F32, kind="Internal").ap()

        S = {}
        for name in """x_first x_second x_rest w_attn w_rest w_cross w_moe consts tables masks xs_zero ctx_in xin_in
            scattered ys_out gath0 gath1 out0 out1
            setup ln_stat ln_rstd h_ready hT_ps hT_ready qk_ps v_ps g_ps rot_mul rot_done qkT_ps qkT_ready
            s_ps s_dec_ready v_ready u_ready clamp_done mish_act mish_done av_ps gn_bn gst_ready gs_ps gs_copy gn_small
            gn_rstd gn_ab yn_step gate_done yT_ps yT_ready o_ps y_sum
            z_stat z_rstd z_ready zT_ps zT_ready f_ps g_ready f2_ps base_done ff_sum x1_stat x1_rstd x1_done
            x1_copy tx_ps cxT_ready xs_ps max_done sub_done exp_done xq_ps xqT_ready xk_ps xv_ps k_done xv_done v_moved
            p_ps pT_ready pv_ps l_ps l_done o_step x2_stat x2_rstd x2_done x2_moved x2T_ps x2T_ready
            r_dve r_gate cnt_ps slots_ready experts_ready
            t_ps xT_ready h1_ps h3_ps sil_ready hh_ready hhT_ps hhT_ready y_ps y_taken
            c_step c_stat c_rstd c_done""".split():
            S[name] = sem(name)

        block = ctx.enter_context(nc.Block())

        def row(t, b):
            return t[:, b, :] if isinstance(b, int) else t[:, bass.ds(b, 1), :].rearrange("p a d -> p (a d)")

        def rows(w):
            return w.rearrange("(c p) n -> p c n", p=P)

        @block.sync
        def _(sp):
            x_rows = a["x"].rearrange("b s d -> s b d")
            sp.dma_start(X[:, 0, :], x_rows[:, 0, :]).then_inc(S["x_first"], 16)
            sp.dma_start(misc[:], a["misc"]).then_inc(S["consts"], 16)
            sp.dma_start(eye[:], a["eye"]).then_inc(S["consts"], 16)
            sp.dma_start(cols[:], a["cols"]).then_inc(S["consts"], 16)
            sp.dma_start(w_qkv, rows(a["wqkv"])).then_inc(S["w_attn"], 16)
            sp.dma_start(w_g, rows(a["wg"])).then_inc(S["w_attn"], 16)
            sp.dma_start(X[:, 1, :], x_rows[:, 1, :]).then_inc(S["x_second"], 16)
            sp.dma_start(rot_c, a["rot_c"]).then_inc(S["tables"], 16)
            sp.dma_start(rot_s, a["rot_s"]).then_inc(S["tables"], 16)
            sp.dma_start(decay, a["decay"]).then_inc(S["tables"], 16)
            sp.dma_start(X[:, 2:, :], x_rows[:, 2:, :]).then_inc(S["x_rest"], 16)
            sp.dma_start(w_o[:], rows(a["wo"])).then_inc(S["w_rest"], 16)
            for dst, name in ((gn[:, 0, :], "gn_w"), (gn[:, 1, :], "gn_b"), (f2_b[:], "f2_b"), (xv_b[:], "xv_b")):
                src = a[name].rearrange("(a d) -> a d", a=1)
                sp.dma_start(dst, src.to_broadcast([P, src.shape[1]])).then_inc(S["w_rest"], 16)
            sp.dma_start(w_f1[:], rows(a["w_f1"])).then_inc(S["w_rest"], 16)
            sp.dma_start(w_f2[:], rows(a["w_f2"])).then_inc(S["w_rest"], 16)
            for g in range(4):
                sp.dma_start(mask_row[32 * g:32 * g + 1, :], a["mask_row"][g:g + 1, :]).then_inc(S["masks"], 16)
            sp.dma_start(mask_col[:], a["mask_col"]).then_inc(S["masks"], 16)
            sp.dma_start(w_xq[:], rows(a["xq"])).then_inc(S["w_cross"], 16)
            sp.dma_start(w_xk[:], rows(a["xk"])).then_inc(S["w_cross"], 16)
            sp.dma_start(w_xv[:], rows(a["xv"])).then_inc(S["w_cross"], 16)
            sp.dma_start(w_rt[:], rows(a["w_router"])).then_inc(S["w_cross"], 16)
            sp.wait_ge(S["setup"], 2)
            sp.dma_start(xs.rearrange("(p n) d -> p n d", p=P), zero[:].rearrange("p (n d) -> p n d", n=1).to_broadcast([P, BLOCKS, D])).then_inc(S["xs_zero"], 16)
            sp.dma_start(s_w1[:], rows(a["sw1"])).then_inc(S["w_moe"], 16)
            sp.dma_start(s_w3[:], rows(a["sw3"])).then_inc(S["w_moe"], 16)
            sp.dma_start(s_w2[:], rows(a["sw2"])).then_inc(S["w_moe"], 16)
            for dst, name in ((e_w1, "w1"), (e_w3, "w3"), (e_w2, "w2")):
                for e in range(NE):
                    sp.dma_start(dst[:, :, e, :], rows(a[name][e])).then_inc(S["w_moe"], 16)

            def load_ctx(b):
                if not (isinstance(b, int) and b == 0):
                    sp.wait_ge(S["tx_ps"], b)
                sp.dma_start(cx[:], a["ctx"][b, :, :] if isinstance(b, int) else
                     a["ctx"][bass.ds(b, 1), :, :].rearrange("a s d -> (a s) d")).then_inc(S["ctx_in"], 16)

            load_ctx(0)
            with sp.Fori(1, NB) as b:
                load_ctx(b)

            sp.wait_ge(S["x2_moved"], NB)

            def load_shared(u, t):
                if not (isinstance(u, int) and u == 0):
                    sp.wait_ge(S["t_ps"], u)
                sp.dma_start(xin[:], row(X, t)).then_inc(S["xin_in"], 16)

            def load_block(u, k):
                sp.wait_ge(S["t_ps"], u)
                sp.dma_start(xin[:], xs[bass.ds(k * P, P), :]).then_inc(S["xin_in"], 16)

            def store_block(u, k):
                sp.wait_ge(S["y_taken"], u + 1)
                sp.dma_start(ys[bass.ds(k * P, P), :], y_st[:]).then_inc(S["ys_out"], 16)

            def store_out(side, t, n):
                sp.wait_ge(S["c_done"], n)
                dst = a["out"][t, :, :] if isinstance(t, int) else a["out"][bass.ds(t, 1), :, :].rearrange("a s d -> (a s) d")
                sp.dma_start(dst, out_sb[:, side, :]).then_inc(S[f"out{side}"], 16)

            load_shared(0, 0)
            with sp.Fori(1, HALF) as u:
                load_shared(u, u)
            sp.wait_ge(S["scattered"], 16 * TOP * NB)
            load_block(HALF, 0)
            load_block(HALF + 1, 1)
            load_block(HALF + 2, 2)
            with sp.Fori(3, BLOCKS) as k:
                load_block(k + HALF, k)
                store_block(k + (HALF - 3), k - 3)
            load_shared(U2, HALF)
            store_block(U2 - 3, BLOCKS - 3)
            load_shared(U2 + 1, HALF + 1)
            store_block(U2 - 2, BLOCKS - 2)
            load_shared(U2 + 2, HALF + 2)
            store_block(U2 - 1, BLOCKS - 1)
            store_out(0, 0, 1)
            for j in range(1, HALF):
                if j + 2 < HALF:
                    load_shared(U2 + j + 2, HALF + j + 2)
                store_out(0, j, 2 * j)
                store_out(1, HALF + j - 1, 2 * j + 1)
            store_out(1, NB - 1, 2 * HALF)
            sp.wait_ge(S["out0"], 16 * HALF)
            sp.wait_ge(S["out1"], 16 * HALF)

        @block.gpsimd
        def _(pool):
            def rsqrt(b, stat, n_stat, done, var, ve, out):
                pool.wait_ge(S[stat], n_stat)
                if not (isinstance(b, int) and b == 0):
                    pool.wait_ge(S[done], 2 * b)
                pool.tensor_tensor(out=ve, in0=var, in1=eps[:, 0:var.shape[1]], op=ALU.add).then_inc(S[done], 1)
                pool.wait_ge(S[done], 2 * b + 1)
                pool.tensor_tensor(out=out, in0=ve, in1=minus_half.to_broadcast(list(out.shape)), op=ALU.pow)\
                    .then_inc(S[done], 1)

            def ln_rsqrt(b):
                rsqrt(b, "ln_stat", 2 * b + 2, "ln_rstd", mv[:, 1:2], veps[:], rstd[:])

            def gn_rsqrt(b):
                rsqrt(b, "gn_small", 5 * b + 5, "gn_rstd", gv[:, 3, :], g_veps[:], g_rstd[:])

            def carry(n):
                pool.tensor_tensor(out=pool_tick[:, n:n + 1], in0=eps[0:1, 0:1], in1=eps[0:1, 0:1], op=ALU.add)

            def base(b):
                if isinstance(b, int) and b == 0:
                    pool.wait_ge(S["w_rest"], 112)
                pool.wait_ge(S["y_sum"], b + 1)
                if not (isinstance(b, int) and b == 0):
                    pool.wait_ge(S["base_done"], 2 * b)
                carry(0)
                xb, yb = row(X, b), row(Y, b)
                pool.tensor_tensor(out=xb, in0=xb, in1=yb, op=ALU.add).then_inc(S["base_done"], 1)
                pool.wait_ge(S["base_done"], 2 * b + 1)
                carry(1)
                pool.tensor_tensor(out=xb, in0=xb, in1=f2_b[:], op=ALU.add).then_inc(S["base_done"], 1)

            pool.wait_ge(S["consts"], 48)
            ln_rsqrt(0)
            ln_rsqrt(1)

            def a_step(i):
                if not isinstance(i, int) or 2 <= i < NB + 2:
                    gn_rsqrt(i - 2)
                if not isinstance(i, int) or i + 2 < NB:
                    ln_rsqrt(i + 2)
                if not isinstance(i, int) or i >= 3:
                    base(i - 3)

            a_step(0)
            a_step(1)
            a_step(2)
            a_step(3)
            with pool.Fori(4, NB - 2) as i:
                a_step(i)
            for i in range(NB - 2, NB + 3):
                a_step(i)

            def z_rsqrt(b, odd):
                rsqrt(b, "z_stat", 2 * b + 2, "z_rstd", z_mv[:, odd, 1:2], veps[:], z_rs[:, odd, :])

            def x1_rsqrt(b, odd):
                rsqrt(b, "x1_stat", 2 * b + 2, "x1_rstd", x1_mv[:, odd, 1:2], veps2[:], x1_rs[:, odd, :])

            def b_step(i, odd):
                if not isinstance(i, int) or i + 2 < NB:
                    z_rsqrt(i + 2, odd)
                if not isinstance(i, int) or i >= 1:
                    x1_rsqrt(i - 1, 1 - odd)

            pool.wait_ge(S["ln_rstd"], 2 * NB)
            z_rsqrt(0, 0)
            z_rsqrt(1, 1)
            for i in range(4):
                b_step(i, i % 2)
            with pool.Fori(2, HALF - 1) as pair:
                b_step(pair * 2, 0)
                b_step(pair * 2 + 1, 1)
            for i in range(NB - 2, NB + 1):
                b_step(i, i % 2)

            def copy_x1(b):
                if not (isinstance(b, int) and b == 0):
                    pool.wait_ge(S["tx_ps"], b)
                pool.wait_ge(S["x1_copy"], b)
                pool.tensor_tensor(out=x1s[:], in0=row(X, b), in1=zero[:], op=ALU.add).then_inc(S["x1_copy"], 1)

            def move_v(b):
                pool.wait_ge(S["xv_done"], b + 1)
                if not (isinstance(b, int) and b == 0):
                    pool.wait_ge(S["pv_ps"], 4 * b)
                    pool.wait_ge(S["v_moved"], b)
                pool.tensor_tensor(out=v_aug[:, :, 0:XD], in0=v_tmp[:], in1=zero[:].rearrange("p (h d) -> p h d", h=XH),
                                   op=ALU.add).then_inc(S["v_moved"], 1)

            def move_x2(b):
                pool.wait_ge(S["x2_done"], b + 1)
                pool.tensor_tensor(out=row(X, b), in0=x2s[:], in1=zero[:], op=ALU.add).then_inc(S["x2_moved"], 1)

            def x2_rsqrt(b):
                rsqrt(b, "x2_stat", 2 * b + 2, "x2_rstd", mv[:, 1:2], veps[:], rstd[:])

            pool.wait_ge(S["x1_done"], NB)
            pool.tensor_copy(x1s[:], X[:, 0, :]).then_inc(S["x1_copy"], 1)
            pool.wait_ge(S["x1_rstd"], 2 * NB)

            def x_step(i):
                static = isinstance(i, int)
                if not static or i + 1 < NB:
                    copy_x1(i + 1)
                if not static or 1 <= i < NB + 1:
                    move_v(i - 1)
                if not static or 2 <= i < NB + 2:
                    x2_rsqrt(i - 2)
                    move_x2(i - 2)

            for i in range(3):
                x_step(i)
            with pool.Fori(3, NB - 1) as i:
                x_step(i)
            for i in range(NB - 1, NB + 2):
                x_step(i)

            pool.wait_ge(S["slots_ready"], 1)
            pool.wait_ge(S["xs_zero"], 16)
            pool.wait_ge(S["x2_moved"], NB)
            for t in range(NB):
                for j in range(TOP):
                    pool.indirect_dma_start(
                        out=xs, out_offset=bass.IndirectOffsetOnAxis(ap=slot[:, j, t:t + 1], axis=0),
                        in_=X[:, t, :], in_offset=None).then_inc(S["scattered"], 16)

            pool.wait_ge(S["ys_out"], 16 * BLOCKS)

            def gather(side, t, n):
                if n > 0:
                    pool.wait_ge(S["c_step"], n)
                for j in range(TOP):
                    pool.indirect_dma_start(
                        out=yg[:, side, j, :], out_offset=None, in_=ys,
                        in_offset=bass.IndirectOffsetOnAxis(ap=slot[:, j, t:t + 1], axis=0))\
                        .then_inc(S[f"gath{side}"], 16)

            def out_rsqrt(n):
                rsqrt(n, "c_stat", 2 * n + 2, "c_rstd", mv[:, 1:2], veps[:], rstd[:])

            pool.wait_ge(S["x2_rstd"], 2 * NB)
            gather(0, 0, 0)
            gather(1, HALF, 0)
            out_rsqrt(0)
            gather(0, 1, 2)
            for j in range(1, HALF):
                out_rsqrt(2 * j - 1)
                if j + 1 < HALF:
                    gather(0, j + 1, 4 * j)
                out_rsqrt(2 * j)
                gather(1, HALF + j, 4 * j + 2)
            out_rsqrt(NB - 1)

        @block.tensor
        def _(pe):
            def mm(out, lhsT, rhs, first, last):
                return pe.matmul(out, lhsT, rhs, start=first, stop=last)

            def turn(bk, at, src, n=DC):
                for c in range(n):
                    t = pe.transpose(bk[:, (at + c) * P:(at + c + 1) * P], src[:, c * P:(c + 1) * P], eye[:])
                return t

            def is_(i, lo, hi):
                return not isinstance(i, int) or lo <= i < hi

            def turn_h(b):
                pe.wait_ge(S["h_ready"], b + 1)
                if is_(b, 1, NB):
                    pe.wait_ge(S["hT_ready"], b)
                if is_(b, 3, NB):
                    pe.wait_ge(S["gs_copy"], b - 2)
                turn(bank[0], 0, h).then_inc(S["hT_ps"], 1)

            w_heads = [w_qkv[:, c, :].rearrange("p (h t) -> p h t", h=RH) for c in range(DC)]
            w_qk = [w[:, :, 0:2 * RD] for w in w_heads]
            w_v = [w[:, :, 2 * RD:] for w in w_heads]

            def products(b):
                pe.wait_ge(S["hT_ready"], b + 1)
                if is_(b, 1, NB):
                    pe.wait_ge(S["rot_mul"], b)
                for c in range(DC):
                    t = mm(bank[1][:], hT[:, c, :], w_qk[c], c == 0, c == DC - 1)
                t.then_inc(S["qk_ps"], 1)
                if is_(b, 1, NB):
                    pe.wait_ge(S["u_ready"], b)
                for c in range(DC):
                    t = mm(bank[3][:, 0:D], hT[:, c, :], w_g[:, c, :], c == 0, c == DC - 1)
                t.then_inc(S["g_ps"], 1)
                if is_(b, 1, NB):
                    pe.wait_ge(S["v_ready"], b)
                for c in range(DC):
                    t = mm(bank[2][:, 0:D], hT[:, c, :], w_v[c], c == 0, c == DC - 1)
                t.then_inc(S["v_ps"], 1)

            def turn_qk(b):
                pe.wait_ge(S["rot_done"], b + 1)
                if is_(b, 1, NB):
                    pe.wait_ge(S["qkT_ready"], b)
                turn(bank[4], 0, qk[:].rearrange("p a h d -> p (a h d)"), 4).then_inc(S["qkT_ps"], 1)

            def scores(b):
                pe.wait_ge(S["qkT_ready"], b + 1)
                if is_(b, 1, NB):
                    pe.wait_ge(S["s_dec_ready"], b)
                for n in range(RH):
                    t = mm(bank[5][:, n * P:(n + 1) * P], k_pad[:, n, :], qT[:, n // 2, :], True, True)
                t.then_inc(S["s_ps"], 1)

            def weighted(b):
                pe.wait_ge(S["s_dec_ready"], b + 1)
                pe.wait_ge(S["v_ready"], b + 1)
                if is_(b, 1, NB):
                    pe.wait_ge(S["yn_step"], 2 * b - 1)
                for n in range(RH):
                    t = mm(bank[6][:, n * RD:(n + 1) * RD], s_dec[:, n, :], v[:, n * RD:(n + 1) * RD], True, True)
                t.then_inc(S["av_ps"], 1)

            def group_sums(b):
                pe.wait_ge(S["gst_ready"], b + 1)
                if is_(b, 1, NB):
                    pe.wait_ge(S["gs_copy"], b)
                pe.wait_ge(S["hT_ready"], b + 3 if not isinstance(b, int) else min(b + 3, NB))
                mm(bank[0][:, 0:RH * 8], avg, gst[:].rearrange("p h e -> p (h e)"), True, True).then_inc(S["gs_ps"], 1)

            def turn_y(b):
                pe.wait_ge(S["gate_done"], b + 1)
                if is_(b, 1, NB):
                    pe.wait_ge(S["y_sum"], b)
                turn(bank[7], 0, yn).then_inc(S["yT_ps"], 1)

            def out_product(b):
                pe.wait_ge(S["yT_ready"], b + 1)
                for c in range(DC):
                    t = mm(bank[7][:, 0:D], yT[:, c, :], w_o[:, c, :], c == 0, c == DC - 1)
                t.then_inc(S["o_ps"], 1)

            def a_step(i):
                if is_(i, 0, NB):
                    products(i)
                if is_(i, 1, NB + 1):
                    scores(i - 1)
                if is_(i, 0, NB - 1):
                    turn_h(i + 1)
                if is_(i, 2, NB + 2):
                    turn_y(i - 2)
                if is_(i, 1, NB + 1):
                    weighted(i - 1)
                if is_(i, 2, NB + 2):
                    out_product(i - 2)
                if is_(i, 0, NB):
                    turn_qk(i)
                if is_(i, 1, NB + 1):
                    group_sums(i - 1)

            pe.wait_ge(S["consts"], 48)
            turn_h(0)
            pe.wait_ge(S["w_attn"], 32)
            a_step(0)
            a_step(1)
            pe.wait_ge(S["w_rest"], 112)
            a_step(2)
            with pe.Fori(3, NB - 1) as i:
                a_step(i)
            for i in range(NB - 1, NB + 2):
                a_step(i)

            def turn_z(b):
                pe.wait_ge(S["z_ready"], b + 1)
                if is_(b, 1, NB):
                    pe.wait_ge(S["zT_ready"], b)
                turn(bank[1], 0, h).then_inc(S["zT_ps"], 1)

            def ff_up(b, odd):
                pe.wait_ge(S["zT_ready"], b + 1)
                if is_(b, 2, NB):
                    pe.wait_ge(S["g_ready"], b - 1)
                for o in range(DC):
                    for c in range(DC):
                        t = mm(bank[4 + 2 * odd][:, o * P:(o + 1) * P], w_f1[:, c, o * P:(o + 1) * P], hT[:, c, :],
                               c == 0, c == DC - 1)
                t.then_inc(S["f_ps"], 1)

            def ff_down(b, odd):
                pe.wait_ge(S["g_ready"], b + 1)
                if is_(b, 2, NB):
                    pe.wait_ge(S["ff_sum"], b - 1)
                for c in range(DC):
                    t = mm(bank[5 + 2 * odd][:, 0:D], gT[:, odd, c, :], w_f2[:, c, :], c == 0, c == DC - 1)
                t.then_inc(S["f2_ps"], 1)

            def b_step(i, odd):
                if is_(i, 0, NB):
                    ff_up(i, odd)
                if is_(i, 0, NB - 1):
                    turn_z(i + 1)
                if is_(i, 1, NB + 1):
                    ff_down(i - 1, 1 - odd)

            turn_z(0)
            for i in range(4):
                b_step(i, i % 2)
            with pe.Fori(2, HALF - 1) as pair:
                b_step(pair * 2, 0)
                b_step(pair * 2 + 1, 1)
            for i in range(NB - 2, NB + 1):
                b_step(i, i % 2)

            def turn_in(b):
                pe.wait_ge(S["ctx_in"], 16 * (b + 1))
                pe.wait_ge(S["x1_copy"], b + 1)
                if is_(b, 1, NB):
                    pe.wait_ge(S["xqT_ready"], b)
                turn(bank[6], 0, cx)
                turn(bank[6], DC, x1s).then_inc(S["tx_ps"], 1)

            def x_scores(b, g):
                if g == 0:
                    pe.wait_ge(S["xqT_ready"], b + 1)
                    pe.wait_ge(S["k_done"], b + 1)
                if is_(b, 1, NB) or g >= 2:
                    pe.wait_ge(S["sub_done"], 4 * b + g - 1)
                lo, hi = 32 * g, 32 * g + 32
                mm(bank[g % 2][:], ones_bf[lo:lo + 1, :], mask_add[lo:lo + 1, :], True, False)
                for c in range(DC):
                    t = mm(bank[g % 2][:, c * 256:(c + 1) * 256], xqT[lo:hi, c, :],
                           k_bd[lo:hi, c, :, :].rearrange("p j k -> p (j k)"), False, c == DC - 1)
                t.then_inc(S["xs_ps"], 1)

            def project_q(b):
                pe.wait_ge(S["cxT_ready"], b + 1)
                for o in range(DC):
                    for c in range(DC):
                        t = mm(bank[6][:, o * P:(o + 1) * P], w_xq[:, c, o * P:(o + 1) * P], cxT[:, DC + c, :],
                               c == 0, c == DC - 1)
                t.then_inc(S["xq_ps"], 1)

            def project_k(b):
                if is_(b, 1, NB):
                    pe.wait_ge(S["k_done"], b)
                for o in range(DC):
                    for c in range(DC):
                        t = mm(bank[2][:, o * P:(o + 1) * P], w_xk[:, c, o * P:(o + 1) * P], cxT[:, c, :],
                               c == 0, c == DC - 1)
                t.then_inc(S["xk_ps"], 1)

            def project_v(b):
                if is_(b, 3, NB):
                    pe.wait_ge(S["l_done"], b - 2)
                if is_(b, 1, 3):
                    pe.wait_ge(S["xv_done"], b)
                for c in range(DC):
                    t = mm(bank[7][:, 0:D], cxT[:, c, :], w_xv[:, c, :], c == 0, c == DC - 1)
                t.then_inc(S["xv_ps"], 1)

            def turn_p(b, g):
                pe.wait_ge(S["exp_done"], 4 * b + g + 1)
                if is_(b, 1, NB) or g >= 2:
                    pe.wait_ge(S["pT_ready"], 4 * b + g - 1)
                turn(bank[4 + g % 2], 0, prob[:, g, :], 4).then_inc(S["p_ps"], 1)

            def x_out(b, g):
                pe.wait_ge(S["pT_ready"], 4 * b + g + 1)
                if g == 0:
                    pe.wait_ge(S["v_moved"], b + 1)
                    if is_(b, 1, NB):
                        pe.wait_ge(S["o_step"], 4 * b - 1)
                for s in range(4):
                    n = 8 * (s // 2) + 2 * g + s % 2
                    t = mm(bank[3][:, n * (XD + 1):(n + 1) * (XD + 1)], pT[:, g % 2, s * P:(s + 1) * P],
                           v_aug[:, n, :], True, True)
                t.then_inc(S["pv_ps"], 1)

            def turn_x2(b):
                pe.wait_ge(S["x2_done"], b + 1)
                pe.wait_ge(S["xv_done"], b + 3 if not isinstance(b, int) else min(b + 3, NB))
                if is_(b, 1, NB):
                    pe.wait_ge(S["l_done"], b)
                turn(bank[7], 0, x2s).then_inc(S["x2T_ps"], 1)

            def router(b):
                pe.wait_ge(S["x2T_ready"], b + 1)
                for c in range(DC):
                    t = mm(bank[7][:, 480:480 + NE], x2T[:, c, :], w_rt[:, c, :], c == 0, c == DC - 1)
                t.then_inc(S["l_ps"], 1)

            def x_step(i):
                here, scored, last, ended = is_(i, 0, NB), is_(i, 1, NB + 1), is_(i, 2, NB + 2), is_(i, 3, NB + 3)
                if scored:
                    x_scores(i - 1, 0)
                if here:
                    turn_in(i)
                if last:
                    turn_p(i - 2, 3)
                if ended:
                    turn_x2(i - 3)
                if last:
                    x_out(i - 2, 2)
                if scored:
                    x_scores(i - 1, 1)
                if here:
                    project_q(i)
                if scored:
                    turn_p(i - 1, 0)
                if ended:
                    router(i - 3)
                if last:
                    x_out(i - 2, 3)
                if scored:
                    x_scores(i - 1, 2)
                if here:
                    project_k(i)
                if scored:
                    turn_p(i - 1, 1)
                    x_out(i - 1, 0)
                    x_scores(i - 1, 3)
                if here:
                    project_v(i)
                if scored:
                    turn_p(i - 1, 2)
                    x_out(i - 1, 1)

            pe.wait_ge(S["w_cross"], 64)
            pe.wait_ge(S["setup"], 8)
            for i in range(4):
                x_step(i)
            with pe.Fori(4, NB) as i:
                x_step(i)
            for i in range(NB, NB + 3):
                x_step(i)

            def counts():
                pe.wait_ge(S["r_dve"], 5)
                flat = hot_bf[:].rearrange("p t e -> p (t e)")
                mm(bank[5][:, 0:NB * NE], before_bf[:], flat, True, False)
                for t in range(NB - 1):
                    n = NB - 1 - t
                    mm(bank[5][:, (t + 1) * NE:NB * NE],
                       ones_bf[:], hot_bf[:, t:t + 1, :].to_broadcast([P, n, NE]), False, t == NB - 2)
                for t in range(NB):
                    m = mm(bank[6][:, 0:NE], ones_bf[:], hot_bf[:, t, :], t == 0, t == NB - 1)
                m.then_inc(S["cnt_ps"], 1)

            def turn_rows(u):
                pe.wait_ge(S["xin_in"], 16 * (u + 1))
                if is_(u, 1, 99):
                    pe.wait_ge(S["xT_ready"], u)
                turn(bank[0], 0, xin).then_inc(S["t_ps"], 1)

            def up(u, w1, w3):
                pe.wait_ge(S["xT_ready"], u + 1)
                if is_(u, 1, 99):
                    pe.wait_ge(S["sil_ready"], u)
                for c in range(DC):
                    t = mm(bank[2][:], xT[:, c, :], w1(c), c == 0, c == DC - 1)
                t.then_inc(S["h1_ps"], 1)
                if is_(u, 1, 99):
                    pe.wait_ge(S["hh_ready"], u)
                for c in range(DC):
                    t = mm(bank[3][:], xT[:, c, :], w3(c), c == 0, c == DC - 1)
                t.then_inc(S["h3_ps"], 1)

            def turn_hidden(u):
                pe.wait_ge(S["hh_ready"], u + 1)
                if is_(u, 1, 99):
                    pe.wait_ge(S["hhT_ready"], u)
                turn(bank[1], 0, hh, HC).then_inc(S["hhT_ps"], 1)

            def down(u, w2):
                pe.wait_ge(S["hhT_ready"], u + 1)
                if is_(u, 1, 99):
                    pe.wait_ge(S["y_taken"], u)
                for c in range(HC):
                    t = mm(bank[4][:, 0:D], hhT[:, c, :], w2(c), c == 0, c == HC - 1)
                t.then_inc(S["y_ps"], 1)

            def up_shared(u):
                up(u, lambda c: s_w1[:, c, :], lambda c: s_w3[:, c, :])

            def down_shared(u):
                down(u, lambda c: s_w2[:, c, :])

            def expert_of(k):
                at = blk_e[:, k:k + 1] if isinstance(k, int) else blk_e[:, bass.ds(k, 1)]
                return pe.value_load(at, min_val=0, max_val=NE - 1)

            def up_block(u, k):
                e = expert_of(k)
                one = bass.ds(e, 1)
                up(u, lambda c: e_w1[:, c, one, :].rearrange("p a n -> p (a n)"),
                   lambda c: e_w3[:, c, one, :].rearrange("p a n -> p (a n)"))

            def down_block(u, k):
                one = bass.ds(expert_of(k), 1)
                down(u, lambda c: e_w2[:, c, one, :].rearrange("p a n -> p (a n)"))

            pe.wait_ge(S["w_moe"], 16 * (3 + 3 * NE))
            counts()
            turn_rows(0)
            turn_rows(1)
            up_shared(0)
            turn_hidden(0)
            turn_rows(2)
            up_shared(1)
            down_shared(0)
            with pe.Fori(2, HALF) as u:
                turn_hidden(u - 1)
                turn_rows(u + 1)
                up_shared(u)
                down_shared(u - 1)
            pe.wait_ge(S["experts_ready"], 1)
            turn_hidden(HALF - 1)
            turn_rows(HALF + 1)
            up_block(HALF, 0)
            down_shared(HALF - 1)
            with pe.Fori(1, BLOCKS) as k:
                turn_hidden(k + (HALF - 1))
                turn_rows(k + (HALF + 1))
                up_block(k + HALF, k)
                down_block(k + (HALF - 1), k - 1)
            turn_hidden(U2 - 1)
            turn_rows(U2 + 1)
            up_shared(U2)
            down_block(U2 - 1, BLOCKS - 1)
            with pe.Fori(U2 + 1, U2 + HALF - 1) as u:
                turn_hidden(u - 1)
                turn_rows(u + 1)
                up_shared(u)
                down_shared(u - 1)
            turn_hidden(U2 + HALF - 2)
            up_shared(U2 + HALF - 1)
            down_shared(U2 + HALF - 2)
            turn_hidden(U2 + HALF - 1)
            down_shared(U2 + HALF - 1)

        @block.scalar
        def _(act):
            def f(out, in_, func, **kw):
                return act.activation(out, in_, func, **kw)

            def is_(i, lo, hi):
                return not isinstance(i, int) or lo <= i < hi

            def take_hT(b, ps, ready, bk, w, bias):
                act.wait_ge(S[ps], b + 1)
                for c in range(DC):
                    t = f(hT[:, c, :], bk[:, c * P:(c + 1) * P], ACT.Identity,
                          scale=w[:, c:c + 1], bias=bias[:, c:c + 1])
                t.then_inc(S[ready], 1)

            def take_h(b):
                take_hT(b, "hT_ps", "hT_ready", bank[0], ln1_w, ln1_b)

            def take_yT(b):
                act.wait_ge(S["yT_ps"], b + 1)
                f(yT[:].rearrange("p c s -> p (c s)"), bank[7][:, 0:D], ACT.Copy).then_inc(S["yT_ready"], 1)

            def take_v(b):
                act.wait_ge(S["v_ps"], b + 1)
                if is_(b, 1, NB):
                    act.wait_ge(S["av_ps"], b)
                f(v[:], bank[2][:, 0:D], ACT.Copy).then_inc(S["v_ready"], 1)

            def take_u(b):
                act.wait_ge(S["g_ps"], b + 1)
                if is_(b, 1, NB):
                    act.wait_ge(S["mish_done"], b)
                f(u_raw[:], bank[3][:, 0:D], ACT.Copy).then_inc(S["u_ready"], 1)

            def take_qkT(b):
                act.wait_ge(S["qkT_ps"], b + 1)
                f(qT[:].rearrange("p c s -> p (c s)"), bank[4][:, 0:D], ACT.Copy)
                for j in range(2):
                    lo, hi = j * RD, (j + 1) * RD
                    t = f(k_pad[lo:hi, j::2, :],
                          bank[4][lo:hi, D:2 * D].rearrange("p (c s) -> p c s", c=DC), ACT.Copy)
                t.then_inc(S["qkT_ready"], 1)

            def take_gs(b):
                act.wait_ge(S["gs_ps"], b + 1)
                if is_(b, 1, NB):
                    act.wait_ge(S["gn_small"], 5 * b)
                f(gsum[:].rearrange("p h e -> p (h e)"), bank[0][:, 0:RH * 8], ACT.Copy).then_inc(S["gs_copy"], 1)

            def mish(b):
                act.wait_ge(S["clamp_done"], b + 1)
                if is_(b, 1, NB):
                    act.wait_ge(S["mish_done"], b)
                    act.wait_ge(S["mish_act"], 4 * b)
                f(m_e[:], uc[:], ACT.Exp).then_inc(S["mish_act"], 1)
                act.wait_ge(S["mish_act"], 4 * b + 1)
                f(m_e[:], m_e[:], ACT.Square, bias=1.0).then_inc(S["mish_act"], 1)
                act.wait_ge(S["mish_act"], 4 * b + 2)
                f(m_r[:], m_e[:], ACT.Ln, bias=1.0).then_inc(S["mish_act"], 1)
                act.wait_ge(S["mish_act"], 4 * b + 3)
                f(m_r[:], m_r[:], ACT.Exp, scale=-1.0).then_inc(S["mish_act"], 1)

            def a_step(i):
                if is_(i, 0, NB):
                    take_u(i)
                    take_v(i)
                if is_(i, 0, NB - 1):
                    take_h(i + 1)
                if is_(i, 2, NB + 2):
                    take_yT(i - 2)
                if is_(i, 0, NB):
                    take_qkT(i)
                if is_(i, 1, NB + 1):
                    take_gs(i - 1)
                if is_(i, 0, NB):
                    mish(i)

            act.wait_ge(S["consts"], 48)
            act.wait_ge(S["setup"], 1)
            take_h(0)
            a_step(0)
            a_step(1)
            with act.Fori(2, NB - 1) as i:
                a_step(i)
            for i in range(NB - 1, NB + 2):
                a_step(i)

            def take_z(b):
                take_hT(b, "zT_ps", "zT_ready", bank[1], ln2_w, ln2_b)

            def gelu(b, odd):
                act.wait_ge(S["f_ps"], b + 1)
                if is_(b, 2, NB):
                    act.wait_ge(S["f2_ps"], b - 1)
                for c in range(DC):
                    t = f(gT[:, odd, c, :], bank[4 + 2 * odd][:, c * P:(c + 1) * P], ACT.Gelu, bias=f1_b[:, c:c + 1])
                t.then_inc(S["g_ready"], 1)

            def b_step(i, odd):
                if is_(i, 0, NB):
                    gelu(i, odd)
                if is_(i, 0, NB - 1):
                    take_z(i + 1)

            take_z(0)
            for i in range(4):
                b_step(i, i % 2)
            with act.Fori(2, HALF - 1) as pair:
                b_step(pair * 2, 0)
                b_step(pair * 2 + 1, 1)
            for i in range(NB - 2, NB):
                b_step(i, i % 2)

            def take_in(b):
                act.wait_ge(S["tx_ps"], b + 1)
                f(cxT[:].rearrange("p c s -> p (c s)"), bank[6][:], ACT.Copy).then_inc(S["cxT_ready"], 1)

            def exp(b, g):
                act.wait_ge(S["sub_done"], 4 * b + g + 1)
                f(prob[:, g, :], prob[:, g, :], ACT.Exp, scale=XD ** -0.5).then_inc(S["exp_done"], 1)

            def take_q(b):
                act.wait_ge(S["xq_ps"], b + 1)
                if is_(b, 1, NB):
                    act.wait_ge(S["xs_ps"], 4 * b)
                for c in range(DC):
                    t = f(xqT[:, c, :], bank[6][:, c * P:(c + 1) * P], ACT.Identity, bias=xq_b[:, c:c + 1])
                t.then_inc(S["xqT_ready"], 1)

            def take_p(b, g):
                act.wait_ge(S["p_ps"], 4 * b + g + 1)
                f(pT[:, g % 2, :], bank[4 + g % 2][:], ACT.Copy).then_inc(S["pT_ready"], 1)

            def take_x2(b):
                act.wait_ge(S["x2T_ps"], b + 1)
                f(x2T[:].rearrange("p c s -> p (c s)"), bank[7][:, 0:D], ACT.Copy).then_inc(S["x2T_ready"], 1)

            def x_step(i):
                here, scored, last, ended = is_(i, 0, NB), is_(i, 1, NB + 1), is_(i, 2, NB + 2), is_(i, 3, NB + 3)
                if here:
                    take_in(i)
                if last:
                    take_p(i - 2, 3)
                if ended:
                    take_x2(i - 3)
                if scored:
                    exp(i - 1, 0)
                    take_p(i - 1, 0)
                    exp(i - 1, 1)
                    take_p(i - 1, 1)
                    exp(i - 1, 2)
                if here:
                    take_q(i)
                if scored:
                    take_p(i - 1, 2)
                    exp(i - 1, 3)

            for i in range(4):
                x_step(i)
            with act.Fori(4, NB) as i:
                x_step(i)
            for i in range(NB, NB + 3):
                x_step(i)

            act.wait_ge(S["r_gate"], 1)
            f(gate[:, 0, :], gate[:, 0, :], ACT.Exp).then_inc(S["r_gate"], 1)


            def take_rows(u):
                act.wait_ge(S["t_ps"], u + 1)
                if is_(u, 1, 99):
                    act.wait_ge(S["h3_ps"], u)
                f(xT[:].rearrange("p c s -> p (c s)"), bank[0][:, 0:D], ACT.Copy).then_inc(S["xT_ready"], 1)

            def silu(u):
                act.wait_ge(S["h1_ps"], u + 1)
                if is_(u, 1, 99):
                    act.wait_ge(S["hh_ready"], u)
                f(sil[:], bank[2][:], ACT.Silu).then_inc(S["sil_ready"], 1)

            def take_block(u, k):
                act.wait_ge(S["y_ps"], u + 1)
                if is_(k, 1, 99):
                    act.wait_ge(S["ys_out"], 16 * k)
                f(y_st[:], bank[4][:, 0:D], ACT.Copy).then_inc(S["y_taken"], 1)

            take_rows(0)
            silu(0)
            take_rows(1)
            with act.Fori(1, HALF + 1) as u:
                silu(u)
                take_rows(u + 1)
            silu(1 + HALF)
            take_rows(2 + HALF)
            take_block(HALF, 0)
            with act.Fori(2, BLOCKS) as k:
                silu(k + HALF)
                take_rows(k + (HALF + 1))
                take_block(k + (HALF - 1), k - 1)
            silu(U2)
            take_rows(U2 + 1)
            take_block(U2 - 1, BLOCKS - 1)
            with act.Fori(U2 + 1, U2 + HALF - 1) as u:
                silu(u)
                take_rows(u + 1)
            silu(U2 + HALF - 1)

        @block.vector
        def _(ve):
            def is_(i, lo, hi):
                return not isinstance(i, int) or lo <= i < hi

            def stats(src, b, name, s6, m2, used, tiles=1):
                if is_(b, 1, NB):
                    ve.wait_ge(S[name], 2 * b)
                if is_(b, tiles, NB):
                    ve.wait_ge(S[used], b - (tiles - 1))
                at = 2 * (s6 is bn2)
                ve.memset(tick[:, at:at + 1], 0.0)
                ve.bn_stats(s6[:], src).then_inc(S[name], 1)
                ve.wait_ge(S[name], 2 * b + 1)
                ve.memset(tick[:, at + 1:at + 2], 0.0)
                ve.bn_aggr(m2[:], s6[:]).then_inc(S[name], 1)

            def normal(dst, src, b, name, m2, r, done):
                ve.wait_ge(S[name], 2 * b + 2)
                ve.tensor_scalar(dst, src, m2[:, 0:1], r[:], ALU.subtract, ALU.mult).then_inc(S[done], 1)

            ve.memset(eps[:], EPS)
            ve.memset(k_pad[:], 0.0).then_inc(S["setup"], 1)
            ve.wait_ge(S["x_first"], 16)

            def ln_stats(b):
                stats(row(X, b), b, "ln_stat", bn, mv, "h_ready")

            def ln_apply(b):
                if is_(b, 1, NB):
                    ve.wait_ge(S["hT_ps"], b)
                normal(h[:], row(X, b), b, "ln_rstd", mv, rstd, "h_ready")

            ln_stats(0)
            ln_apply(0)
            ve.memset(zero[:], 0.0).then_inc(S["setup"], 1)
            ve.memset(v_aug[:], 1.0).then_inc(S["setup"], 1)
            ve.memset(ones_bf[:], 1.0).then_inc(S["setup"], 1)
            ve.memset(scan[:], 0.0).then_inc(S["setup"], 1)
            ve.wait_ge(S["consts"], 48)
            ve.tensor_copy(before_bf[:], before).then_inc(S["setup"], 1)
            ve.wait_ge(S["x_second"], 16)
            ln_stats(1)
            ve.wait_ge(S["tables"], 48)

            def rotary(b):
                ve.wait_ge(S["qk_ps"], b + 1)
                if is_(b, 1, NB):
                    ve.wait_ge(S["rot_done"], b)
                ps = bank[1][:].rearrange("p (h a d) -> p h a d", h=RH, a=2)
                ve.tensor_tensor(qk[:].rearrange("p a h d -> p h a d"), ps,
                                 rot_c[:].rearrange("p (h a) d -> p h a d", a=2), ALU.mult)
                pairs = bank[1][:].rearrange("p (g d) -> p g d", d=RD)[:, :, 0:ROT]\
                    .rearrange("p g (j t) -> p g j t", t=2)
                u = qk_u[:].rearrange("p g (j t) -> p g j t", t=2)
                s = rot_s[:].rearrange("p g (j t) -> p g j t", t=2)
                ve.tensor_tensor(u[:, :, :, 0], pairs[:, :, :, 1], s[:, :, :, 0], ALU.mult)
                ve.tensor_tensor(u[:, :, :, 1], pairs[:, :, :, 0], s[:, :, :, 1], ALU.mult)\
                    .then_inc(S["rot_mul"], 1)
                ve.wait_ge(S["rot_mul"], b + 1)
                q = qk[:].rearrange("p a h d -> p h a d")[:, :, :, 0:ROT]
                ve.tensor_tensor(q, q, qk_u[:].rearrange("p (h a) d -> p h a d", a=2), ALU.add)\
                    .then_inc(S["rot_done"], 1)

            def clamp(b):
                ve.wait_ge(S["u_ready"], b + 1)
                ve.tensor_scalar(uc[:], u_raw[:], U_MAX, None, ALU.min).then_inc(S["clamp_done"], 1)

            def mish(b):
                if is_(b, 1, NB):
                    ve.wait_ge(S["gate_done"], b)
                ve.wait_ge(S["mish_act"], 4 * b + 4)
                ve.scalar_tensor_tensor(m_u[:], m_r[:], -0.5, u_raw[:], ALU.add, ALU.mult)\
                    .then_inc(S["mish_done"], 1)

            def decayed(b):
                ve.wait_ge(S["s_ps"], b + 1)
                ve.tensor_tensor(s_dec[:].rearrange("p h s -> p (h s)"), bank[5][:],
                                 decay[:].rearrange("p h s -> p (h s)"), ALU.mult).then_inc(S["s_dec_ready"], 1)

            def gn_stats(b):
                ve.wait_ge(S["av_ps"], b + 1)
                if is_(b, 1, NB):
                    ve.wait_ge(S["gst_ready"], b)
                for n in range(RH):
                    t = ve.bn_stats(gst[:, n, 0:6], bank[6][:, n * RD:(n + 1) * RD])
                t.then_inc(S["gn_bn"], 1)
                ve.wait_ge(S["gn_bn"], b + 1)
                means = gst[:, :, 1:5:3]
                ve.tensor_tensor(gst[:, :, 6:8], means, means, ALU.mult).then_inc(S["gst_ready"], 1)

            def gn_var(b):
                ve.wait_ge(S["gs_copy"], b + 1)
                if is_(b, 1, NB):
                    ve.wait_ge(S["gn_small"], 5 * b)
                    ve.wait_ge(S["gn_ab"], 3 * b)

                ve.tensor_tensor(g_sum2[:], gsum[:, :, 1:3], gsum[:, :, 4:6], ALU.add).then_inc(S["gn_small"], 1)
                ve.tensor_tensor(gv[:, 0, :], gsum[:, :, 6], gsum[:, :, 7], ALU.add).then_inc(S["gn_small"], 1)
                ve.wait_ge(S["gn_small"], 5 * b + 2)
                s0, s1 = g_sum2[:, :, 0], g_sum2[:, :, 1]
                ve.scalar_tensor_tensor(gv[:, 1, :], s0, 0.25, s0, ALU.mult, ALU.mult).then_inc(S["gn_small"], 1)
                ve.wait_ge(S["gn_small"], 5 * b + 3)
                ve.scalar_tensor_tensor(gv[:, 2, :], s1, 1.0 / RD, gv[:, 1, :], ALU.mult, ALU.subtract).then_inc(S["gn_small"], 1)
                ve.wait_ge(S["gn_small"], 5 * b + 4)
                ve.scalar_tensor_tensor(gv[:, 3, :], gv[:, 0, :], 0.5, gv[:, 2, :], ALU.mult, ALU.add)\
                    .then_inc(S["gn_small"], 1)

            def gn_apply(b):
                ve.wait_ge(S["gn_rstd"], 2 * b + 2)
                if is_(b, 1, NB):
                    ve.wait_ge(S["yn_step"], 2 * b)
                A, mA, B = gv[:, 4, :], gv[:, 5, :], gv[:, 6, :]
                ve.tensor_tensor(A, g_rstd[:], gn[:, 0, :], ALU.mult).then_inc(S["gn_ab"], 1)
                ve.wait_ge(S["gn_ab"], 3 * b + 1)
                ve.scalar_tensor_tensor(mA, g_sum2[:, :, 0], 0.5, A, ALU.mult, ALU.mult).then_inc(S["gn_ab"], 1)
                ve.wait_ge(S["gn_ab"], 3 * b + 2)
                ve.tensor_tensor(B, gn[:, 1, :], mA, ALU.subtract).then_inc(S["gn_ab"], 1)
                if is_(b, 1, NB):
                    ve.wait_ge(S["yT_ps"], b)
                y3 = yn[:].rearrange("p (h d) -> p h d", h=RH)

                def wide(v4):
                    return v4.rearrange("p (h a) -> p h a", a=1).to_broadcast([P, RH, RD])

                ve.tensor_tensor(y3, bank[6][:, 0:D].rearrange("p (h d) -> p h d", h=RH), wide(A), ALU.mult)\
                    .then_inc(S["yn_step"], 1)
                ve.wait_ge(S["gn_ab"], 3 * b + 3)
                ve.wait_ge(S["yn_step"], 2 * b + 1)
                ve.tensor_tensor(y3, y3, wide(B), ALU.add).then_inc(S["yn_step"], 1)
                ve.wait_ge(S["yn_step"], 2 * b + 2)
                ve.wait_ge(S["mish_done"], b + 1)
                ve.scalar_tensor_tensor(yn[:], m_u[:], -2.0, yn[:], ALU.mult, ALU.mult).then_inc(S["gate_done"], 1)

            def y_sum(b):
                ve.wait_ge(S["o_ps"], b + 1)
                ve.tensor_tensor(row(Y, b), bank[7][:, 0:D], row(X, b), ALU.add).then_inc(S["y_sum"], 1)

            def a_step(i):
                if is_(i, 2, NB + 2):
                    gn_var(i - 2)
                if is_(i, 0, NB - 1):
                    ln_apply(i + 1)
                if is_(i, 2, NB + 2):
                    gn_apply(i - 2)
                if is_(i, 1, NB + 1):
                    mish(i - 1)
                    decayed(i - 1)
                if is_(i, 0, NB):
                    rotary(i)
                    clamp(i)
                if is_(i, 1, NB + 1):
                    gn_stats(i - 1)
                if is_(i, 0, NB - 2):
                    ln_stats(i + 2)
                if is_(i, 2, NB + 2):
                    y_sum(i - 2)

            for i in range(4):
                if i == 0:
                    ve.wait_ge(S["x_rest"], 16)
                if i == 2:
                    ve.wait_ge(S["w_rest"], 112)
                a_step(i)
                if i == 2:
                    ve.wait_ge(S["masks"], 80)
                    for g in range(4):
                        one = slice(32 * g, 32 * g + 1)
                        t = ve.tensor_scalar(mask_add[one, :], mask_row[one, :], 0.0, MASKED, ALU.is_equal, ALU.mult)
                    t.then_inc(S["setup"], 1)
                    ve.tensor_copy(mask_mul[:], mask_col[:]).then_inc(S["setup"], 1)
                    ve.wait_ge(S["setup"], 8)
            with ve.Fori(4, NB - 2) as i:
                a_step(i)
            for i in range(NB - 2, NB + 2):
                a_step(i)

            def z_stats(b, odd):
                stats(row(Y, b), b, "z_stat", bn, z_mv[:, odd, :], "z_ready", 2)

            def z_apply(b, odd):
                if is_(b, 1, NB):
                    ve.wait_ge(S["zT_ps"], b)
                normal(h[:], row(Y, b), b, "z_rstd", z_mv[:, odd, :], z_rs[:, odd, :], "z_ready")

            def ff_sum(b, odd):
                ve.wait_ge(S["f2_ps"], b + 1)
                ve.wait_ge(S["base_done"], 2 * b + 2)
                xb = row(X, b)
                ve.tensor_tensor(xb, bank[5 + 2 * odd][:, 0:D], xb, ALU.add).then_inc(S["ff_sum"], 1)
                ve.wait_ge(S["ff_sum"], b + 1)
                stats(xb, b, "x1_stat", bn2, x1_mv[:, odd, :], "x1_done", 2)

            def x1_apply(b, odd):
                normal(row(X, b), row(X, b), b, "x1_rstd", x1_mv[:, odd, :], x1_rs[:, odd, :], "x1_done")

            def b_step(i, odd):
                if is_(i, 0, NB - 1):
                    z_apply(i + 1, 1 - odd)
                if is_(i, 0, NB - 2):
                    z_stats(i + 2, odd)
                if is_(i, 2, NB + 2):
                    x1_apply(i - 2, odd)
                if is_(i, 1, NB + 1):
                    ff_sum(i - 1, 1 - odd)

            ve.wait_ge(S["ln_stat"], 2 * NB)
            ve.wait_ge(S["h_ready"], NB)
            ve.wait_ge(S["y_sum"], NB)
            z_stats(0, 0)
            z_stats(1, 1)
            z_apply(0, 0)
            for i in range(4):
                b_step(i, i % 2)
            with ve.Fori(2, HALF - 1) as pair:
                b_step(pair * 2, 0)
                b_step(pair * 2 + 1, 1)
            for i in range(NB - 2, NB + 2):
                b_step(i, i % 2)

            def take_logits(b):
                ve.wait_ge(S["l_ps"], b + 1)
                ve.tensor_copy(row(logit, b), bank[7][:, 480:480 + NE]).then_inc(S["l_done"], 1)

            def x_out(b):
                ve.wait_ge(S["pv_ps"], 4 * b + 4)
                if is_(b, 1, NB):
                    ve.wait_ge(S["o_step"], 4 * b)
                    ve.wait_ge(S["x2_done"], b)
                o = bank[3][:, 0:XH * (XD + 1)].rearrange("p (h d) -> p h d", h=XH)
                ve.reciprocal(rec[:, 0, :], o[:, :, XD]).then_inc(S["o_step"], 1)
                ve.wait_ge(S["o_step"], 4 * b + 1)
                ve.tensor_tensor(rec[:, 1, :], rec[:, 0, :], mask_mul[:], ALU.mult).then_inc(S["o_step"], 1)
                ve.wait_ge(S["o_step"], 4 * b + 2)
                ve.tensor_tensor(t_out[:].rearrange("p (h d) -> p h d", h=XH), o[:, :, 0:XD],
                                 rec[:, 1, :].rearrange("p (h a) -> p h a", a=1).to_broadcast([P, XH, XD]),
                                 ALU.mult).then_inc(S["o_step"], 1)
                ve.wait_ge(S["o_step"], 4 * b + 3)
                ve.tensor_tensor(t_out[:], t_out[:], row(X, b), ALU.add).then_inc(S["o_step"], 1)
                ve.wait_ge(S["o_step"], 4 * b + 4)
                stats(t_out[:], b, "x2_stat", bn, mv, "x2_done")

            def x2_apply(b):
                if is_(b, 1, NB):
                    ve.wait_ge(S["x2T_ps"], b)
                    ve.wait_ge(S["x2_moved"], b)
                normal(x2s[:], t_out[:], b, "x2_rstd", mv, rstd, "x2_done")

            def x_max(b, g):
                ve.wait_ge(S["xs_ps"], 4 * b + g + 1)
                if is_(b, 1, NB):
                    ve.wait_ge(S["sub_done"], 4 * b - 3 + g)
                ve.tensor_reduce(s_max[:, g, :], bank[g % 2][:].rearrange("p (s k) -> p s k", s=4), AX.X, ALU.max)\
                    .then_inc(S["max_done"], 1)

            def x_sub(b, g):
                ve.wait_ge(S["max_done"], 4 * b + g + 1)
                if is_(b, 1, NB):
                    ve.wait_ge(S["p_ps"], 4 * b - 3 + g)
                ve.tensor_tensor(prob[:, g, :].rearrange("p (s k) -> p s k", s=4),
                                 bank[g % 2][:].rearrange("p (s k) -> p s k", s=4),
                                 s_max[:, g, :].rearrange("p (s a) -> p s a", a=1).to_broadcast([P, 4, P]),
                                 ALU.subtract).then_inc(S["sub_done"], 1)

            def take_k(b):
                ve.wait_ge(S["xk_ps"], b + 1)
                if is_(b, 1, NB):
                    ve.wait_ge(S["xs_ps"], 4 * b)
                for c in range(DC):
                    t = ve.scalar_tensor_tensor(
                        k_bd[:, c, :, :],
                        bank[2][:, c * P:(c + 1) * P].rearrange("p (a k) -> p a k", a=1).to_broadcast([P, 2, P]),
                        xk_b[:, c:c + 1],
                        half_of.rearrange("p (j a) -> p j a", a=1).to_broadcast([P, 2, P]), ALU.add, ALU.mult)
                t.then_inc(S["k_done"], 1)

            def take_v(b):
                ve.wait_ge(S["xv_ps"], b + 1)
                if is_(b, 1, NB):
                    ve.wait_ge(S["v_moved"], b)
                ve.tensor_tensor(v_tmp[:].rearrange("p h d -> p (h d)"), bank[7][:, 0:D], xv_b[:], ALU.add)\
                    .then_inc(S["xv_done"], 1)

            def x_step(i):
                here, scored, last, ended = is_(i, 0, NB), is_(i, 1, NB + 1), is_(i, 2, NB + 2), is_(i, 3, NB + 3)
                if scored:
                    x_max(i - 1, 0)
                    x_sub(i - 1, 0)
                    x_max(i - 1, 1)
                    x_sub(i - 1, 1)
                if ended:
                    take_logits(i - 3)
                if last:
                    x_out(i - 2)
                if scored:
                    x_max(i - 1, 2)
                    x_sub(i - 1, 2)
                    x_max(i - 1, 3)
                if here:
                    take_k(i)
                if scored:
                    x_sub(i - 1, 3)
                if last:
                    x2_apply(i - 2)
                if here:
                    take_v(i)

            ve.wait_ge(S["x1_stat"], 2 * NB)
            ve.wait_ge(S["z_ready"], NB)
            ve.wait_ge(S["x1_done"], NB)
            for i in range(4):
                x_step(i)
            with ve.Fori(4, NB) as i:
                x_step(i)
            for i in range(NB, NB + 3):
                x_step(i)

            ve.wait_ge(S["l_done"], NB)
            for t in range(NB):
                m = ve.max(top[:, t, :], logit[:, t, :])
            m.then_inc(S["r_dve"], 1)
            ve.wait_ge(S["r_dve"], 1)
            for t in range(NB):
                m = ve.max_index(top_i[:, t, :], top[:, t, :], logit[:, t, :])
            m.then_inc(S["r_dve"], 1)
            ve.tensor_tensor(gate[:, 0, :], top[:, :, 1], top[:, :, 0], ALU.subtract).then_inc(S["r_gate"], 1)
            ve.wait_ge(S["r_dve"], 2)
            ve.tensor_copy(top_f[:], top_i[:, :, 0:TOP]).then_inc(S["r_dve"], 1)
            ve.wait_ge(S["r_dve"], 3)
            numbers = expert_no.rearrange("p (a e) -> p a e", a=1).to_broadcast([P, NB, NE])
            for j in range(TOP):
                m = ve.tensor_tensor(hot[:, j, :, :], top_f[:, :, j:j + 1].to_broadcast([P, NB, NE]), numbers,
                                     ALU.is_equal)
            m.then_inc(S["r_dve"], 1)
            ve.wait_ge(S["r_dve"], 4)
            ve.tensor_tensor(hot_bf[:], hot[:, 0, :, :], hot[:, 1, :, :], ALU.add).then_inc(S["r_dve"], 1)
            ve.wait_ge(S["r_gate"], 2)
            ve.tensor_scalar(gate[:, 2, :], gate[:, 0, :], 1.0, None, ALU.add).then_inc(S["r_gate"], 1)
            ve.wait_ge(S["r_gate"], 3)
            ve.reciprocal(gate[:, 1, :], gate[:, 2, :]).then_inc(S["r_gate"], 1)
            ve.wait_ge(S["r_gate"], 4)
            ve.tensor_tensor(gate[:, 2, :], gate[:, 0, :], gate[:, 1, :], ALU.mult).then_inc(S["r_gate"], 1)
            ve.wait_ge(S["cnt_ps"], 1)
            ve.tensor_scalar(cnt_i[:, 0, :], bank[6][:, 0:NE], float(P - 1), None, ALU.add).then_inc(S["r_dve"], 1)
            ve.wait_ge(S["r_dve"], 6)
            ve.tensor_scalar(cnt_i[:, 1, :], cnt_i[:, 0, :], 7, None, ALU.logical_shift_right).then_inc(S["r_dve"], 1)
            ve.wait_ge(S["r_dve"], 7)
            ve.tensor_copy(scan[:, 0, NE:], cnt_i[:, 1, :]).then_inc(S["r_dve"], 1)
            ve.wait_ge(S["r_dve"], 8)
            ve.tensor_tensor(scan[:, 1, NE:], scan[:, 0, NE:], scan[:, 0, NE - 1:2 * NE - 1], ALU.add).then_inc(S["r_dve"], 1)
            ve.wait_ge(S["r_dve"], 9)
            ve.tensor_tensor(scan[:, 0, NE:], scan[:, 1, NE:], scan[:, 1, NE - 2:2 * NE - 2], ALU.add).then_inc(S["r_dve"], 1)
            ve.wait_ge(S["r_dve"], 10)
            ve.tensor_tensor(scan[:, 1, NE:], scan[:, 0, NE:], scan[:, 0, NE - 4:2 * NE - 4], ALU.add).then_inc(S["r_dve"], 1)
            ve.wait_ge(S["r_dve"], 11)
            ve.tensor_copy(cnt[:, 0, :], cnt_i[:, 1, :]).then_inc(S["r_dve"], 1)
            ve.wait_ge(S["r_dve"], 12)
            ve.tensor_tensor(cnt[:, 1, :], scan[:, 1, NE:], cnt[:, 0, :], ALU.subtract).then_inc(S["r_dve"], 1)
            ve.wait_ge(S["r_dve"], 13)
            ve.scalar_tensor_tensor(
                pos[:], cnt[:, 1:2, :].to_broadcast([P, NB, NE]), float(P),
                bank[5][:, 0:NB * NE].rearrange("p (t e) -> p t e", t=NB), ALU.mult, ALU.add).then_inc(S["r_dve"], 1)
            ve.wait_ge(S["r_dve"], 14)
            ve.tensor_tensor(pos_e[:, 0, :, :], hot[:, 0, :, :], pos[:], ALU.mult).then_inc(S["r_dve"], 1)
            ve.wait_ge(S["r_dve"], 15)
            ve.tensor_tensor(pos_e[:, 1, :, :], hot[:, 1, :, :], pos[:], ALU.mult).then_inc(S["r_dve"], 1)
            ve.wait_ge(S["r_dve"], 16)
            ve.tensor_reduce(pos_f[:].rearrange("p j t -> p (j t)"),
                                     pos_e[:].rearrange("p j t e -> p (j t) e"), AX.X, ALU.add).then_inc(S["r_dve"], 1)
            ve.wait_ge(S["r_dve"], 17)
            ve.tensor_copy(slot[:], pos_f[:]).then_inc(S["r_dve"], 1)
            ve.wait_ge(S["r_dve"], 18)
            ve.memset(blk_f[:, 1, :], 0.0).then_inc(S["slots_ready"], 1)
            ve.tensor_tensor(blk[:], scan[0:1, 1:2, NE:].to_broadcast([1, BLOCKS, NE]),
                                    block_no[0:1, :].rearrange("p (b a) -> p b a", a=1).to_broadcast([1, BLOCKS, NE]),
                                    ALU.is_le).then_inc(S["r_dve"], 1)
            ve.wait_ge(S["r_dve"], 19)
            ve.tensor_reduce(blk_f[:, 0, :], blk[:], AX.X, ALU.add).then_inc(S["r_dve"], 1)
            ve.wait_ge(S["r_dve"], 20)
            ve.tensor_scalar(blk_e[:], blk_f[:, 0, :], float(NE - 1), None, ALU.min).then_inc(S["experts_ready"], 1)


            def gated(u):
                ve.wait_ge(S["h3_ps"], u + 1)
                ve.wait_ge(S["sil_ready"], u + 1)
                ve.tensor_tensor(hh[:], bank[3][:], sil[:], ALU.mult).then_inc(S["hh_ready"], 1)

            def take_hidden(u):
                ve.wait_ge(S["hhT_ps"], u + 1)
                ve.tensor_copy(hhT[:].rearrange("p c s -> p (c s)"), bank[1][:]).then_inc(S["hhT_ready"], 1)

            def take_shared(u, t):
                ve.wait_ge(S["y_ps"], u + 1)
                ve.tensor_tensor(row(Y, t), bank[4][:, 0:D], row(X, t), ALU.add).then_inc(S["y_taken"], 1)

            gated(0)
            with ve.Fori(1, HALF) as u:
                take_hidden(u - 1)
                gated(u)
                take_shared(u - 1, u - 1)
            take_hidden(HALF - 1)
            gated(HALF)
            take_shared(HALF - 1, HALF - 1)
            with ve.Fori(HALF + 1, U2 + 1) as u:
                take_hidden(u - 1)
                gated(u)

            gathers = [0, 0]
            stores = [0, 0]

            def combine(n, side, t):
                if n:
                    ve.wait_ge(S["c_done"], n)
                gathers[side] += 16 * TOP
                ve.wait_ge(S[f"gath{side}"], gathers[side])
                ve.wait_ge(S["y_taken"], t + 1 if t < HALF else U2 + t - HALF + 1)
                ve.scalar_tensor_tensor(out_t[:], yg[:, side, 0, :], gate[:, 1, t:t + 1], Y[:, t, :],
                                        ALU.mult, ALU.add).then_inc(S["c_step"], 1)
                ve.wait_ge(S["c_step"], 2 * n + 1)
                ve.scalar_tensor_tensor(out_t[:], yg[:, side, 1, :], gate[:, 2, t:t + 1], out_t[:],
                                        ALU.mult, ALU.add).then_inc(S["c_step"], 1)
                ve.wait_ge(S["c_step"], 2 * n + 2)
                stats(out_t[:], n, "c_stat", bn, mv, "c_done")
                if stores[side]:
                    ve.wait_ge(S[f"out{side}"], stores[side])
                normal(out_sb[:, side, :], out_t[:], n, "c_rstd", mv, rstd, "c_done")
                stores[side] += 16

            ve.wait_ge(S["r_gate"], 5)
            ve.wait_ge(S["x2_stat"], 2 * NB)
            ve.wait_ge(S["x2_done"], NB)
            for j in range(1, HALF + 1):
                u = U2 + j
                take_hidden(u - 1)
                if j < HALF:
                    gated(u)
                if j == 1:
                    combine(0, 0, 0)
                if j < HALF:
                    combine(2 * j - 1, 0, j)
                take_shared(u - 1, HALF + j - 1)
                combine(2 * j if j < HALF else NB - 1, 1, HALF + j - 1)


def tables():
    half = np.arange(0, ROT, 2, dtype=np.float64)
    t = np.arange(P, dtype=np.float64)
    freqs = np.repeat(t[:, None] / 10000.0 ** (half / ROT), 2, axis=-1)
    scale = ((half + 0.4 * ROT) / (1.4 * ROT))[None, :] ** ((t - P // 2) / 512.0)[:, None]
    scale = np.concatenate((scale, scale), axis=-1)
    rot_c = np.ones((P, RH, 2, RD))
    rot_s = np.zeros((P, RH, 2, ROT))
    sign = np.where(np.arange(ROT) % 2 == 0, -1.0, 1.0)
    for n, s in enumerate((scale, 1.0 / scale)):
        rot_c[:, :, n, :ROT] = (np.cos(freqs) * s)[:, None, :]
        rot_s[:, :, n, :] = (np.sin(freqs) * s * sign)[:, None, :]
    gamma = 1.0 - 2.0 ** (-5.0 - np.arange(RH))
    apart = t[None, :] - t[:, None]
    decay = np.where(apart[:, None, :] >= 0, gamma[None, :, None] ** np.maximum(apart, 0)[:, None, :], 0.0)
    misc = np.zeros((P, 2 * P + NE + BLOCKS + 3))
    misc[:, 0:P] = 1.0 / P
    misc[:, P:2 * P] = np.arange(P)[:, None] < np.arange(P)[None, :]
    at = 2 * P
    misc[:, at:at + NE] = np.arange(NE)
    misc[:, at + NE:at + NE + BLOCKS] = np.arange(BLOCKS)
    at += NE + BLOCKS
    misc[:, at:at + 2] = (np.arange(P)[:, None] // XD) % 2 == np.arange(2)[None, :]
    misc[:, at + 2] = -0.5
    f = np.float32
    return {"rot_c": rot_c.reshape(P, 2 * RH, RD).astype(f), "rot_s": rot_s.reshape(P, 2 * RH, ROT).astype(f),
            "decay": decay.astype(f), "misc": misc.astype(f), "eye": np.eye(P, dtype=f)}


def kernel(**inputs):
    import concourse.bacc as _bacc
    from concourse.bass_utils import run_bass_kernel_spmd as _run

    g = {k: np.asarray(v) for k, v in inputs.items()}
    attn, cross, ffn = "L0_attn_", "L0_xattn_", "L0_ffn_"

    def columns(*names):
        return np.concatenate([g[n].reshape(DC, P).T for n in names], axis=1)

    mask = g["mask_BxS2_ik0"]
    order = [8 * c + 2 * r + j for r in range(4) for c in range(2) for j in range(2)]
    arrays = {
        "x": g["x"], "ctx": g["ctx_1024"],
        "wqkv": g[attn + "wqkv_w"], "wg": g[attn + "wg_w"], "wo": g[attn + "wo_w"],
        "w_f1": g[attn + "w1_w"], "w_f2": g[attn + "w2_w"], "f2_b": g[attn + "w2_b"],
        "gn_w": g[attn + "gn_w"], "gn_b": g[attn + "gn_b"],
        "cols": columns(attn + "ln1_w", attn + "ln1_b", attn + "ln2_w", attn + "ln2_b", attn + "w1_b",
                        cross + "bq", cross + "bk"),
        "xq": g[cross + "Wq"].T, "xk": g[cross + "Wk"].T, "xv": g[cross + "Wv"].T, "xv_b": g[cross + "bv"],
        "mask_row": mask[order].reshape(4, 4 * P), "mask_col": mask.T,
        "w_router": g[ffn + "w_router"], "w1": g[ffn + "w1"], "w3": g[ffn + "w3"], "w2": g[ffn + "w2"],
        "sw1": g[ffn + "sw1"], "sw3": g[ffn + "sw3"], "sw2": g[ffn + "sw2"],
    } | tables()
    nc = _bacc.Bacc("TRN2", target_bir_lowering=False, num_devices=1)
    feeds, aps = {}, {}
    for name, value in arrays.items():
        value = np.ascontiguousarray(value)
        feeds[f"in_{name}_dram"] = value
        aps[name] = nc.dram_tensor(f"in_{name}_dram", value.shape, mybir.dt.from_np(value.dtype),
                                   kind="ExternalInput").ap()
    aps["out"] = nc.dram_tensor("out_0_dram", (NB, P, D), F32, kind="ExternalOutput").ap()
    build(nc, aps)
    r = _run(nc, [feeds], core_ids=[0])
    return r.results[0]["out_0_dram"]
```

```python
from contextlib import ExitStack

import numpy as np
import concourse.bass as bass
from concourse import mybir

F32 = mybir.dt.float32
BF16 = mybir.dt.bfloat16
I32 = mybir.dt.int32
U32 = mybir.dt.uint32
ALU = mybir.AluOpType
ACT = mybir.ActivationFunctionType
AX = mybir.AxisListType

P = 128
D = 256
DC = D // P
NB = 16
RH, RD = 4, 64
ROT = 32
XH, XD = 16, 16
NE, HID = 8, 512
HC = HID // P
TOP = 2
BLOCKS = (NB * P * TOP + NE * (P - 1)) // P
HALF = NB // 2
FIRST = 9
REST = NB - FIRST
U2 = FIRST + BLOCKS
EPS = 1e-5
MASKED = -1e9 * XD ** 0.5
U_MAX = 20.0


def build(nc, a):
    ctx = ExitStack()
    with ctx:
        def sb(name, shape, dt=F32):
            return ctx.enter_context(nc.sbuf_tensor(name, shape, dt))

        def sem(name):
            return ctx.enter_context(nc.semaphore(name))

        bank = [ctx.enter_context(nc.psum_tensor(f"bank{n}", [P, 512], F32)) for n in range(8)]

        X = sb("X", [P, NB, D])
        Y = sb("Y", [P, NB, D])

        def carve(name, *lots):
            whole = sb(name, [P, max(sum(int(np.prod(shape)) for shape in lot) for lot in lots)])
            out = []
            for lot in lots:
                at = 0
                for shape in lot:
                    n = int(np.prod(shape))
                    v = whole[:, at:at + n]
                    if len(shape) == 2:
                        v = v.rearrange("p (a b) -> p a b", a=shape[0])
                    elif len(shape) == 3:
                        v = v.rearrange("p (a b c) -> p a b c", a=shape[0], b=shape[1])
                    out.append(v)
                    at += n
            return out

        (w_qkv, w_g, w_o, w_f1, w_f2, decay,
         xin, xT, sil, hh, hhT, y_st, out_sb, out_t) = carve(
            "weights_a_or_tiles_m",
            [(DC, 3 * D), (DC, D), (DC, D), (DC, D), (DC, D), (RH, P)],
            [(D,), (DC, P), (HID,), (HID,), (HC, P), (D,), (2, D), (D,)])

        (qk, qk_u, qT, k_pad, v, uc, m_e, m_r, m_u, s_dec, yn, yT,
         prob, pT, cxT, x2s) = carve(
            "tiles_a_or_tiles_x",
            [(2, RH, RD), (2 * RH, ROT), (DC, P), (RH, P), (D,), (D,), (D,), (D,), (D,), (RH, P), (D,), (DC, P)],
            [(4, 512), (2, 512), (2 * DC, P), (D,)])

        rot_c, rot_s, hot, pos, pos_e, blk_all = carve(
            "tables_a_or_tiles_r",
            [(2 * RH, RD), (2 * RH, ROT)],
            [(TOP, NB, NE), (NB, NE), (TOP, NB, NE), (BLOCKS, NE)])
        blk = blk_all[0:1, :, :]
        mask_row = Y[:, NB - 2:, :].rearrange("p b d -> p (b d)").bitcast(I32)

        w_xq = sb("w_xq", [P, DC, D])
        w_xk = sb("w_xk", [P, DC, D])
        w_xv = sb("w_xv", [P, DC, D])
        w_rt = sb("w_rt", [P, DC, NE])
        s_w1 = sb("s_w1", [P, DC, HID])
        s_w3 = sb("s_w3", [P, DC, HID])
        s_w2 = sb("s_w2", [P, HC, D])
        e_w1 = sb("e_w1", [P, DC, NE, HID])
        e_w3 = sb("e_w3", [P, DC, NE, HID])
        e_w2 = sb("e_w2", [P, HC, NE, D])
        cols = sb("cols", [P, 14])
        ln1_w, ln1_b, ln2_w, ln2_b, f1_b, xq_b, xk_b = (cols[:, 2 * n:2 * n + 2] for n in range(7))
        gn = sb("gn", [P, 2, RH])
        f2_b = sb("f2_b", [P, D])
        xv_b = sb("xv_b", [P, D])
        eye = sb("eye", [P, P])
        misc = sb("misc", [P, 2 * P + NE + BLOCKS + 2 + 1])
        avg = misc[:, 0:P]
        before = misc[:, P:2 * P]
        expert_no = misc[:, 2 * P:2 * P + NE]
        block_no = misc[:, 2 * P + NE:2 * P + NE + BLOCKS]
        half_of = misc[:, 2 * P + NE + BLOCKS:2 * P + NE + BLOCKS + 2]
        minus_half = misc[:, 2 * P + NE + BLOCKS + 2:2 * P + NE + BLOCKS + 3]
        mask_col = sb("mask_col", [P, XH], I32)
        mask_add = sb("mask_add", [P, 512], BF16)
        mask_mul = sb("mask_mul", [P, XH])
        ones_bf = sb("ones_bf", [P, P], BF16)
        before_bf = sb("before_bf", [P, P], BF16)
        zero = sb("zero", [P, D])

        tick = sb("tick", [1, 6])
        eps = sb("eps", [P, RH])
        bn = sb("bn", [P, 6])
        mv = sb("mv", [P, 2])
        veps = sb("veps", [P, 1])
        rstd = sb("rstd", [P, 1])
        bn2 = sb("bn2", [P, 6])
        veps2 = sb("veps2", [P, 1])
        h = sb("h", [P, D])
        hT = sb("hT", [P, DC, P])
        gst = sb("gst", [P, RH, 8])
        gsum = sb("gsum", [P, RH, 8])
        gv = sb("gv", [P, 8, RH])
        g_sum2 = sb("g_sum2", [P, RH, 2])
        g_veps = sb("g_veps", [P, RH])
        g_rstd = sb("g_rstd", [P, RH])
        gT = sb("gT", [P, 2, DC, P])
        z_mv = sb("z_mv", [P, 2, 2])
        z_rs = sb("z_rs", [P, 2, 1])
        x1_mv = sb("x1_mv", [P, 2, 2])
        x1_rs = sb("x1_rs", [P, 2, 1])
        pool_tick = sb("pool_tick", [1, 2])
        t_out = sb("t_out", [P, D])
        cx = sb("cx", [P, D])
        x1s = sb("x1s", [P, D])
        u_raw = (t_out, x1s)
        xqT = sb("xqT", [P, DC, P])
        k_bd = sb("k_bd", [P, DC, 2, P])
        v_tmp = sb("v_tmp", [P, XH, XD])
        v_aug = sb("v_aug", [P, XH, XD + 1])
        s_max = sb("s_max", [P, 4, 4])
        rec = sb("rec", [P, 2, XH])
        yg = prob.rearrange("p n (j d) -> p n j d", j=TOP)
        v_pair = (v, v_tmp[:].rearrange("p h d -> p (h d)"))
        m_pair = (m_u, xqT[:].rearrange("p c s -> p (c s)"))
        x2T = sb("x2T", [P, DC, P])
        logit = sb("logit", [P, NE])
        best = sb("best", [P, 8])
        best_at = sb("best_at", [P, 8], U32)
        top = sb("top", [P, NB, TOP])
        top_f = sb("top_f", [P, NB, TOP])
        gate = sb("gate", [P, 3, NB])
        hot_bf = sb("hot_bf", [P, NB, NE], BF16)
        cnt = sb("cnt", [P, 4, NE])
        cnt_i = sb("cnt_i", [P, 2, NE], I32)
        scan = sb("scan", [P, 2, 2 * NE])
        pos_f = sb("pos_f", [P, TOP, NB])
        slot = sb("slot", [P, TOP, NB], U32)
        blk_f = sb("blk_f", [1, 2, BLOCKS])
        blk_e = sb("blk_e", [1, BLOCKS], I32)

        xs = nc.dram_tensor("rows_by_slot", (BLOCKS * P, D), F32, kind="Internal").ap()
        ys = nc.dram_tensor("results_by_slot", (BLOCKS * P, D), F32, kind="Internal").ap()

        S = {}
        for name in """x_first x_second x_rest w_attn w_rest w_cross w_moe consts tables masks xs_zero ctx_in xin_in
            scattered ys_out gath0 gath1 gath2 gath3 out0 out1
            setup ln_stat ln_rstd h_ready hT_ps hT_ready qk_ps gv_ps rot_mul rot_done qkT_ps qkT_ready
            s_ps s_dec_ready v_ready u_ready clamp_done mish_act mish_done av_ps gn_bn gst_ready gs_ps gs_copy gn_small
            gn_rstd gn_ab yn_step gate_done yT_ps yT_ready o_ps y_sum
            z_stat z_rstd z_ready zT_ps zT_ready f_ps g_ready f2_ps base_done ff_sum x1_stat x1_rstd x1_done
            x1_copy tx_ps cxT_ready xs_ps max_done sub_done exp_done xq_ps xqT_ready xk_ps xv_ps k_done xv_done v_moved
            p_ps pT_ready pv_ps l_ps l_done best_done top_done o_step x2_stat x2_rstd x2_done x2_moved x2T_ps x2T_ready
            r_dve r_gate cnt_ps slots_ready experts_ready
            t_ps xT_ready h1_ps h3_ps sil_ready hh_ready hhT_ps hhT_ready y_ps y_taken
            c_step c_stat c_rstd c_done""".split():
            S[name] = sem(name)

        block = ctx.enter_context(nc.Block())

        def row(t, b):
            return t[:, b, :] if isinstance(b, int) else t[:, bass.ds(b, 1), :].rearrange("p a d -> p (a d)")

        def rows(w):
            return w.rearrange("(c p) n -> p c n", p=P)

        @block.sync
        def _(sp):
            x_rows = a["x"].rearrange("b s d -> s b d")
            sp.dma_start(X[:, 0, :], x_rows[:, 0, :]).then_inc(S["x_first"], 16)
            sp.dma_start(misc[:], a["misc"]).then_inc(S["consts"], 16)
            sp.dma_start(eye[:], a["eye"]).then_inc(S["consts"], 16)
            sp.dma_start(cols[:], a["cols"]).then_inc(S["consts"], 16)
            sp.dma_start(w_qkv, rows(a["wqkv"])).then_inc(S["w_attn"], 16)
            sp.dma_start(w_g, rows(a["wg"])).then_inc(S["w_attn"], 16)
            sp.dma_start(X[:, 1, :], x_rows[:, 1, :]).then_inc(S["x_second"], 16)
            sp.dma_start(rot_c, a["rot_c"]).then_inc(S["tables"], 16)
            sp.dma_start(rot_s, a["rot_s"]).then_inc(S["tables"], 16)
            sp.dma_start(decay, a["decay"]).then_inc(S["tables"], 16)
            sp.dma_start(X[:, 2:, :], x_rows[:, 2:, :]).then_inc(S["x_rest"], 16)
            sp.dma_start(w_o[:], rows(a["wo"])).then_inc(S["w_rest"], 16)
            for dst, name in ((gn[:, 0, :], "gn_w"), (gn[:, 1, :], "gn_b"), (f2_b[:], "f2_b"), (xv_b[:], "xv_b")):
                src = a[name].rearrange("(a d) -> a d", a=1)
                sp.dma_start(dst, src.to_broadcast([P, src.shape[1]])).then_inc(S["w_rest"], 16)
            sp.dma_start(w_f1[:], rows(a["w_f1"])).then_inc(S["w_rest"], 16)
            sp.dma_start(w_f2[:], rows(a["w_f2"])).then_inc(S["w_rest"], 16)
            for g in range(4):
                sp.dma_start(mask_row[32 * g:32 * g + 1, :], a["mask_row"][g:g + 1, :]).then_inc(S["masks"], 16)
            sp.dma_start(mask_col[:], a["mask_col"]).then_inc(S["masks"], 16)
            sp.dma_start(w_xq[:], rows(a["xq"])).then_inc(S["w_cross"], 16)
            sp.dma_start(w_xk[:], rows(a["xk"])).then_inc(S["w_cross"], 16)
            sp.dma_start(w_xv[:], rows(a["xv"])).then_inc(S["w_cross"], 16)
            sp.dma_start(w_rt[:], rows(a["w_router"])).then_inc(S["w_cross"], 16)
            sp.wait_ge(S["setup"], 2)
            sp.dma_start(xs.rearrange("(p n) d -> p n d", p=P), zero[:].rearrange("p (n d) -> p n d", n=1).to_broadcast([P, BLOCKS, D])).then_inc(S["xs_zero"], 16)
            sp.dma_start(s_w1[:], rows(a["sw1"])).then_inc(S["w_moe"], 16)
            sp.dma_start(s_w3[:], rows(a["sw3"])).then_inc(S["w_moe"], 16)
            sp.dma_start(s_w2[:], rows(a["sw2"])).then_inc(S["w_moe"], 16)
            for dst, name in ((e_w1, "w1"), (e_w3, "w3"), (e_w2, "w2")):
                for e in range(NE):
                    sp.dma_start(dst[:, :, e, :], rows(a[name][e])).then_inc(S["w_moe"], 16)

            def load_ctx(b):
                if not (isinstance(b, int) and b == 0):
                    sp.wait_ge(S["tx_ps"], b)
                sp.dma_start(cx[:], a["ctx"][b, :, :] if isinstance(b, int) else
                     a["ctx"][bass.ds(b, 1), :, :].rearrange("a s d -> (a s) d")).then_inc(S["ctx_in"], 16)

            load_ctx(0)
            with sp.Fori(1, NB) as b:
                load_ctx(b)

            sp.wait_ge(S["x2_moved"], NB)

            def load_shared(u, t):
                if not (isinstance(u, int) and u == 2):
                    sp.wait_ge(S["t_ps"], u)
                sp.dma_start(xin[:], row(X, t)).then_inc(S["xin_in"], 16)

            def load_block(u, k):
                sp.wait_ge(S["t_ps"], u)
                sp.dma_start(xin[:], xs[bass.ds(k * P, P), :]).then_inc(S["xin_in"], 16)

            def store_block(u, k):
                sp.wait_ge(S["y_taken"], u + 1)
                sp.dma_start(ys[bass.ds(k * P, P), :], y_st[:]).then_inc(S["ys_out"], 16)

            def store_out(side, m):
                sp.wait_ge(S["c_done"], 2 * m + side + 1)
                sp.dma_start(a["out"][HALF * side + m, :, :], out_sb[:, side, :]).then_inc(S[f"out{side}"], 16)

            load_shared(2, 2)
            with sp.Fori(3, FIRST) as u:
                load_shared(u, u)
            sp.wait_ge(S["scattered"], 16 * TOP * NB)
            load_block(FIRST, 0)
            load_block(FIRST + 1, 1)
            load_block(FIRST + 2, 2)
            with sp.Fori(3, BLOCKS) as k:
                load_block(k + FIRST, k)
                store_block(k + (FIRST - 3), k - 3)
            load_shared(U2, FIRST)
            store_block(U2 - 3, BLOCKS - 3)
            load_shared(U2 + 1, FIRST + 1)
            store_block(U2 - 2, BLOCKS - 2)
            load_shared(U2 + 2, FIRST + 2)
            store_block(U2 - 1, BLOCKS - 1)
            for j in range(1, HALF + 2):
                if j + 2 < REST:
                    load_shared(U2 + j + 2, FIRST + j + 2)
                if j >= 2:
                    store_out(0, j - 2)
                    store_out(1, j - 2)
            sp.wait_ge(S["out0"], 16 * HALF)
            sp.wait_ge(S["out1"], 16 * HALF)

        @block.gpsimd
        def _(pool):
            def rsqrt(b, stat, n_stat, done, var, ve, out):
                pool.wait_ge(S[stat], n_stat)
                if not (isinstance(b, int) and b == 0):
                    pool.wait_ge(S[done], 2 * b)
                pool.tensor_tensor(out=ve, in0=var, in1=eps[:, 0:var.shape[1]], op=ALU.add).then_inc(S[done], 1)
                pool.wait_ge(S[done], 2 * b + 1)
                pool.tensor_tensor(out=out, in0=ve, in1=minus_half.to_broadcast(list(out.shape)), op=ALU.pow)\
                    .then_inc(S[done], 1)

            def ln_rsqrt(b):
                rsqrt(b, "ln_stat", 2 * b + 2, "ln_rstd", mv[:, 1:2], veps[:], rstd[:])

            def gn_rsqrt(b):
                rsqrt(b, "gn_small", 5 * b + 5, "gn_rstd", gv[:, 3, :], g_veps[:], g_rstd[:])

            def carry(n):
                pool.tensor_tensor(out=pool_tick[:, n:n + 1], in0=eps[0:1, 0:1], in1=eps[0:1, 0:1], op=ALU.add)

            def base(b):
                if isinstance(b, int) and b == 0:
                    pool.wait_ge(S["w_rest"], 112)
                pool.wait_ge(S["y_sum"], b + 1)
                if not (isinstance(b, int) and b == 0):
                    pool.wait_ge(S["base_done"], 2 * b)
                carry(0)
                xb, yb = row(X, b), row(Y, b)
                pool.tensor_tensor(out=xb, in0=xb, in1=yb, op=ALU.add).then_inc(S["base_done"], 1)
                pool.wait_ge(S["base_done"], 2 * b + 1)
                carry(1)
                pool.tensor_tensor(out=xb, in0=xb, in1=f2_b[:], op=ALU.add).then_inc(S["base_done"], 1)

            pool.wait_ge(S["consts"], 48)
            ln_rsqrt(0)
            ln_rsqrt(1)

            def a_step(i):
                if not isinstance(i, int) or 2 <= i < NB + 2:
                    gn_rsqrt(i - 2)
                if not isinstance(i, int) or i + 2 < NB:
                    ln_rsqrt(i + 2)
                if not isinstance(i, int) or i >= 3:
                    base(i - 3)

            a_step(0)
            a_step(1)
            a_step(2)
            a_step(3)
            with pool.Fori(4, NB - 2) as i:
                a_step(i)
            a_step(NB - 2)

            def z_rsqrt(b, odd):
                rsqrt(b, "z_stat", 2 * b + 2, "z_rstd", z_mv[:, odd, 1:2], veps[:], z_rs[:, odd, :])

            def x1_rsqrt(b, odd):
                rsqrt(b, "x1_stat", 2 * b + 2, "x1_rstd", x1_mv[:, odd, 1:2], veps2[:], x1_rs[:, odd, :])

            def b_step(i, odd):
                if not isinstance(i, int) or i + 3 < NB:
                    z_rsqrt(i + 3, 1 - odd)
                if not isinstance(i, int) or i >= 1:
                    x1_rsqrt(i - 1, 1 - odd)

            def copy_x1(b):
                if not (isinstance(b, int) and b == 0):
                    pool.wait_ge(S["tx_ps"], b)
                pool.wait_ge(S["x1_copy"], b)
                pool.tensor_tensor(out=x1s[:], in0=row(X, b), in1=zero[:], op=ALU.add).then_inc(S["x1_copy"], 1)

            pool.wait_ge(S["ln_rstd"], 2 * NB)
            z_rsqrt(0, 0)
            z_rsqrt(1, 1)
            a_step(NB - 1)
            gn_rsqrt(NB - 2)
            base(NB - 3)
            z_rsqrt(2, 0)
            gn_rsqrt(NB - 1)
            base(NB - 2)
            b_step(0, 0)
            b_step(1, 1)
            base(NB - 1)
            b_step(2, 0)
            b_step(3, 1)
            with pool.Fori(2, HALF - 2) as pair:
                b_step(pair * 2, 0)
                b_step(pair * 2 + 1, 1)
            for i in range(NB - 4, NB + 1):
                if i == NB - 2:
                    pool.wait_ge(S["x1_done"], 1)
                    pool.tensor_copy(x1s[:], X[:, 0, :]).then_inc(S["x1_copy"], 1)
                if i == NB:
                    pool.wait_ge(S["x1_done"], 2)
                    copy_x1(1)
                b_step(i, i % 2)

            def move_v(b):
                pool.wait_ge(S["xv_done"], b + 1)
                if not (isinstance(b, int) and b == 0):
                    pool.wait_ge(S["pv_ps"], 4 * b)
                    pool.wait_ge(S["v_moved"], b)
                pool.tensor_tensor(out=v_aug[:, :, 0:XD], in0=v_tmp[:], in1=zero[:].rearrange("p (h d) -> p h d", h=XH),
                                   op=ALU.add).then_inc(S["v_moved"], 1)

            def move_x2(b):
                pool.wait_ge(S["x2_done"], b + 1)
                pool.tensor_tensor(out=row(X, b), in0=x2s[:], in1=zero[:], op=ALU.add).then_inc(S["x2_moved"], 1)

            def x2_rsqrt(b):
                rsqrt(b, "x2_stat", 2 * b + 2, "x2_rstd", mv[:, 1:2], veps[:], rstd[:])

            pool.wait_ge(S["x1_done"], NB)
            pool.wait_ge(S["x1_rstd"], 2 * NB)

            def x_step(i):
                static = isinstance(i, int)
                if not static or 1 <= i < NB - 1:
                    copy_x1(i + 1)
                if not static or 1 <= i < NB + 1:
                    move_v(i - 1)
                if not static or 2 <= i < NB + 2:
                    x2_rsqrt(i - 2)
                    move_x2(i - 2)

            for i in range(3):
                x_step(i)
            with pool.Fori(3, NB - 1) as i:
                x_step(i)
            for i in range(NB - 1, NB + 2):
                x_step(i)

            pool.wait_ge(S["slots_ready"], 1)
            pool.wait_ge(S["xs_zero"], 16)
            pool.wait_ge(S["x2_moved"], NB)
            for t in range(NB):
                for j in range(TOP):
                    pool.indirect_dma_start(
                        out=xs, out_offset=bass.IndirectOffsetOnAxis(ap=slot[:, j, t:t + 1], axis=0),
                        in_=X[:, t, :], in_offset=None).then_inc(S["scattered"], 16)

            pool.wait_ge(S["ys_out"], 16 * BLOCKS)

            def gather(n):
                if n >= 4:
                    pool.wait_ge(S["c_step"], 2 * (n - 3))
                t = HALF * (n % 2) + n // 2
                for j in range(TOP):
                    pool.indirect_dma_start(
                        out=yg[:, n % 4, j, :], out_offset=None, in_=ys,
                        in_offset=bass.IndirectOffsetOnAxis(ap=slot[:, j, t:t + 1], axis=0))\
                        .then_inc(S[f"gath{n % 4}"], 16)

            def out_rsqrt(m):
                pool.wait_ge(S["c_stat"], 4 * m + 4)
                if m:
                    pool.wait_ge(S["c_rstd"], 2 * m)
                mvs, rs = ((x1_mv, x1_rs), (z_mv, z_rs))[m % 2]
                pool.tensor_tensor(out=g_veps[:, 0:2], in0=mvs[:, :, 1], in1=eps[:, 0:2], op=ALU.add)\
                    .then_inc(S["c_rstd"], 1)
                pool.wait_ge(S["c_rstd"], 2 * m + 1)
                pool.tensor_tensor(out=rs[:, :, 0], in0=g_veps[:, 0:2], in1=minus_half.to_broadcast([P, 2]),
                                   op=ALU.pow).then_inc(S["c_rstd"], 1)

            pool.wait_ge(S["x2_rstd"], 2 * NB)
            pool.wait_ge(S["x1_rstd"], 2 * NB)
            pool.wait_ge(S["p_ps"], 4 * NB)
            for n in range(4):
                gather(n)
            for m in range(HALF):
                if m == 0:
                    out_rsqrt(0)
                if m + 2 < HALF:
                    gather(2 * m + 4)
                if m > 0:
                    out_rsqrt(m)
                if m + 2 < HALF:
                    gather(2 * m + 5)

        @block.tensor
        def _(pe):
            def mm(out, lhsT, rhs, first, last):
                return pe.matmul(out, lhsT, rhs, start=first, stop=last)

            def turn(bk, at, src, n=DC):
                for c in range(n):
                    t = pe.transpose(bk[:, (at + c) * P:(at + c + 1) * P], src[:, c * P:(c + 1) * P], eye[:])
                return t

            def is_(i, lo, hi):
                return not isinstance(i, int) or lo <= i < hi

            def turn_h(b):
                pe.wait_ge(S["h_ready"], b + 1)
                if is_(b, 1, NB):
                    pe.wait_ge(S["hT_ready"], b)
                if is_(b, 3, NB):
                    pe.wait_ge(S["gs_copy"], b - 2)
                turn(bank[0], 0, h).then_inc(S["hT_ps"], 1)

            w_heads = [w_qkv[:, c, :].rearrange("p (h t) -> p h t", h=RH) for c in range(DC)]
            w_qk = [w[:, :, 0:2 * RD] for w in w_heads]
            w_v = [w[:, :, 2 * RD:] for w in w_heads]

            def product_qk(b):
                pe.wait_ge(S["hT_ready"], b + 1)
                if is_(b, 1, NB):
                    pe.wait_ge(S["rot_mul"], b)
                for c in range(DC):
                    t = mm(bank[1][:], hT[:, c, :], w_qk[c], c == 0, c == DC - 1)
                t.then_inc(S["qk_ps"], 1)

            def products_gv(b):
                if is_(b, 1, NB):
                    pe.wait_ge(S["u_ready"], b)
                    pe.wait_ge(S["v_ready"], b)
                for c in range(DC):
                    t = mm(bank[3][:, 0:D], hT[:, c, :], w_g[:, c, :], c == 0, c == DC - 1)
                for c in range(DC):
                    t = mm(bank[3][:, D:2 * D], hT[:, c, :], w_v[c], c == 0, c == DC - 1)
                t.then_inc(S["gv_ps"], 1)

            def turn_qk(b):
                pe.wait_ge(S["rot_done"], b + 1)
                if is_(b, 1, NB):
                    pe.wait_ge(S["qkT_ready"], b)
                turn(bank[4], 0, qk[:].rearrange("p a h d -> p (a h d)"), 4).then_inc(S["qkT_ps"], 1)

            def scores(b):
                pe.wait_ge(S["qkT_ready"], b + 1)
                if is_(b, 1, NB):
                    pe.wait_ge(S["s_dec_ready"], b)
                for n in range(RH):
                    t = mm(bank[5][:, n * P:(n + 1) * P], k_pad[:, n, :], qT[:, n // 2, :], True, True)
                t.then_inc(S["s_ps"], 1)

            def weighted(b, odd):
                pe.wait_ge(S["s_dec_ready"], b + 1)
                pe.wait_ge(S["v_ready"], b + 1)
                if is_(b, 2, NB):
                    pe.wait_ge(S["yn_step"], 2 * b - 3)
                for n in range(RH):
                    t = mm(bank[6 - 4 * odd][:, n * RD:(n + 1) * RD], s_dec[:, n, :], v_pair[odd][:, n * RD:(n + 1) * RD], True, True)
                t.then_inc(S["av_ps"], 1)

            def group_sums(b):
                pe.wait_ge(S["gst_ready"], b + 1)
                if is_(b, 1, NB):
                    pe.wait_ge(S["gs_copy"], b)
                pe.wait_ge(S["hT_ready"], b + 3 if not isinstance(b, int) else min(b + 3, NB))
                mm(bank[0][:, 0:RH * 8], avg, gst[:].rearrange("p h e -> p (h e)"), True, True).then_inc(S["gs_ps"], 1)

            def turn_y(b):
                pe.wait_ge(S["gate_done"], b + 1)
                if is_(b, 1, NB):
                    pe.wait_ge(S["y_sum"], b)
                turn(bank[7], 0, yn).then_inc(S["yT_ps"], 1)

            def out_product(b):
                pe.wait_ge(S["yT_ready"], b + 1)
                for c in range(DC):
                    t = mm(bank[7][:, 0:D], yT[:, c, :], w_o[:, c, :], c == 0, c == DC - 1)
                t.then_inc(S["o_ps"], 1)

            def a_step(i, odd):
                if is_(i, 0, NB):
                    product_qk(i)
                if is_(i, 3, NB + 3):
                    turn_y(i - 3)
                if is_(i, 2, NB + 2):
                    group_sums(i - 2)
                if is_(i, 0, NB):
                    products_gv(i)
                if is_(i, 3, NB + 3):
                    out_product(i - 3)
                if is_(i, 1, NB + 1):
                    scores(i - 1)
                if is_(i, 0, NB - 1):
                    turn_h(i + 1)
                if is_(i, 0, NB):
                    turn_qk(i)
                if is_(i, 1, NB + 1):
                    weighted(i - 1, 1 - odd)

            pe.wait_ge(S["consts"], 48)
            turn_h(0)
            pe.wait_ge(S["w_attn"], 32)
            for i in range(4):
                if i == 3:
                    pe.wait_ge(S["w_rest"], 112)
                a_step(i, i % 2)
            with pe.Fori(2, HALF - 1) as pair:
                a_step(pair * 2, 0)
                a_step(pair * 2 + 1, 1)
            a_step(NB - 2, 0)
            a_step(NB - 1, 1)

            def turn_z(b):
                pe.wait_ge(S["z_ready"], b + 1)
                if is_(b, 1, NB):
                    pe.wait_ge(S["zT_ready"], b)
                turn(bank[1], 0, h).then_inc(S["zT_ps"], 1)

            def ff_up(b, odd):
                pe.wait_ge(S["zT_ready"], b + 1)
                if is_(b, 2, NB):
                    pe.wait_ge(S["g_ready"], b - 1)
                for o in range(DC):
                    for c in range(DC):
                        t = mm(bank[4 + 2 * odd][:, o * P:(o + 1) * P], w_f1[:, c, o * P:(o + 1) * P], hT[:, c, :],
                               c == 0, c == DC - 1)
                t.then_inc(S["f_ps"], 1)

            def ff_down(b, odd):
                pe.wait_ge(S["g_ready"], b + 1)
                if is_(b, 2, NB):
                    pe.wait_ge(S["ff_sum"], b - 1)
                for c in range(DC):
                    t = mm(bank[5 + 2 * odd][:, 0:D], gT[:, odd, c, :], w_f2[:, c, :], c == 0, c == DC - 1)
                t.then_inc(S["f2_ps"], 1)

            def b_step(i, odd):
                if is_(i, 0, NB):
                    ff_up(i, odd)
                if is_(i, 0, NB - 1):
                    turn_z(i + 1)
                if is_(i, 1, NB + 1):
                    ff_down(i - 1, 1 - odd)

            pe.wait_ge(S["rot_done"], NB)
            scores(NB - 1)
            turn_z(0)
            turn_y(NB - 3)
            group_sums(NB - 2)
            pe.wait_ge(S["qkT_ready"], NB)
            ff_up(0, 0)
            weighted(NB - 1, 1)
            out_product(NB - 3)
            turn_z(1)
            turn_y(NB - 2)
            group_sums(NB - 1)
            pe.wait_ge(S["yn_step"], 2 * NB - 3)
            out_product(NB - 2)
            ff_up(1, 1)
            turn_z(2)
            pe.wait_ge(S["s_dec_ready"], NB)
            ff_down(0, 0)
            ff_up(2, 0)
            turn_z(3)
            turn_y(NB - 1)
            out_product(NB - 1)
            pe.wait_ge(S["y_sum"], NB)
            ff_down(1, 1)
            b_step(3, 1)
            with pe.Fori(2, HALF - 1) as pair:
                b_step(pair * 2, 0)
                b_step(pair * 2 + 1, 1)
            for i in range(NB - 2, NB + 1):
                b_step(i, i % 2)

            def turn_in(b):
                pe.wait_ge(S["ctx_in"], 16 * (b + 1))
                pe.wait_ge(S["x1_copy"], b + 1)
                if is_(b, 1, NB):
                    pe.wait_ge(S["xqT_ready"], b)
                turn(bank[6], 0, cx)
                turn(bank[6], DC, x1s).then_inc(S["tx_ps"], 1)

            def x_scores(b, g):
                if g == 0:
                    pe.wait_ge(S["xqT_ready"], b + 1)
                    pe.wait_ge(S["k_done"], b + 1)
                if is_(b, 1, NB) or g >= 2:
                    pe.wait_ge(S["sub_done"], 4 * b + g - 1)
                lo, hi = 32 * g, 32 * g + 32
                mm(bank[g % 2][:], ones_bf[lo:lo + 1, :], mask_add[lo:lo + 1, :], True, False)
                for c in range(DC):
                    t = mm(bank[g % 2][:, c * 256:(c + 1) * 256], xqT[lo:hi, c, :],
                           k_bd[lo:hi, c, :, :].rearrange("p j k -> p (j k)"), False, c == DC - 1)
                t.then_inc(S["xs_ps"], 1)

            def project_q(b):
                pe.wait_ge(S["cxT_ready"], b + 1)
                for o in range(DC):
                    for c in range(DC):
                        t = mm(bank[6][:, o * P:(o + 1) * P], w_xq[:, c, o * P:(o + 1) * P], cxT[:, DC + c, :],
                               c == 0, c == DC - 1)
                t.then_inc(S["xq_ps"], 1)

            def project_k(b):
                if is_(b, 1, NB):
                    pe.wait_ge(S["k_done"], b)
                for o in range(DC):
                    for c in range(DC):
                        t = mm(bank[2][:, o * P:(o + 1) * P], w_xk[:, c, o * P:(o + 1) * P], cxT[:, c, :],
                               c == 0, c == DC - 1)
                t.then_inc(S["xk_ps"], 1)

            def project_v(b):
                if is_(b, 3, NB):
                    pe.wait_ge(S["l_done"], b - 2)
                if isinstance(b, int) and b == 0:
                    pe.wait_ge(S["ff_sum"], NB)
                if is_(b, 1, 3):
                    pe.wait_ge(S["xv_done"], b)
                for c in range(DC):
                    t = mm(bank[7][:, 0:D], cxT[:, c, :], w_xv[:, c, :], c == 0, c == DC - 1)
                t.then_inc(S["xv_ps"], 1)

            def turn_p(b, g):
                pe.wait_ge(S["exp_done"], 4 * b + g + 1)
                if is_(b, 1, NB) or g >= 2:
                    pe.wait_ge(S["pT_ready"], 4 * b + g - 1)
                turn(bank[4 + g % 2], 0, prob[:, g, :], 4).then_inc(S["p_ps"], 1)

            def x_out(b, g):
                pe.wait_ge(S["pT_ready"], 4 * b + g + 1)
                if g == 0:
                    pe.wait_ge(S["v_moved"], b + 1)
                    if is_(b, 1, NB):
                        pe.wait_ge(S["o_step"], 4 * b - 1)
                for s in range(4):
                    n = 8 * (s // 2) + 2 * g + s % 2
                    t = mm(bank[3][:, n * (XD + 1):(n + 1) * (XD + 1)], pT[:, g % 2, s * P:(s + 1) * P],
                           v_aug[:, n, :], True, True)
                t.then_inc(S["pv_ps"], 1)

            def turn_x2(b):
                pe.wait_ge(S["x2_done"], b + 1)
                pe.wait_ge(S["xv_done"], b + 3 if not isinstance(b, int) else min(b + 3, NB))
                if is_(b, 1, NB):
                    pe.wait_ge(S["l_done"], b)
                turn(bank[7], 0, x2s).then_inc(S["x2T_ps"], 1)

            def router(b):
                pe.wait_ge(S["x2T_ready"], b + 1)
                for c in range(DC):
                    t = mm(bank[7][:, 480:480 + NE], x2T[:, c, :], w_rt[:, c, :], c == 0, c == DC - 1)
                t.then_inc(S["l_ps"], 1)

            def x_step(i):
                here, scored, last, ended = is_(i, 0, NB), is_(i, 1, NB + 1), is_(i, 2, NB + 2), is_(i, 3, NB + 3)
                if here and isinstance(i, int) and i == 1:
                    turn_in(i)
                if scored:
                    x_scores(i - 1, 0)
                if here and not (isinstance(i, int) and i == 1):
                    turn_in(i)
                if last:
                    turn_p(i - 2, 3)
                if ended:
                    turn_x2(i - 3)
                if last:
                    x_out(i - 2, 2)
                if scored:
                    x_scores(i - 1, 1)
                if here:
                    project_q(i)
                if scored:
                    turn_p(i - 1, 0)
                if ended:
                    router(i - 3)
                if last:
                    x_out(i - 2, 3)
                if scored:
                    x_scores(i - 1, 2)
                if here:
                    project_k(i)
                if scored:
                    turn_p(i - 1, 1)
                    x_out(i - 1, 0)
                    x_scores(i - 1, 3)
                if here:
                    project_v(i)
                if scored:
                    turn_p(i - 1, 2)
                    x_out(i - 1, 1)

            pe.wait_ge(S["w_cross"], 64)
            pe.wait_ge(S["setup"], 8)
            pe.wait_ge(S["g_ready"], NB)
            for i in range(4):
                x_step(i)
            with pe.Fori(4, NB) as i:
                x_step(i)
            x_step(NB)
            x_step(NB + 1)

            def counts():
                pe.wait_ge(S["r_dve"], 2)
                flat = hot_bf[:].rearrange("p t e -> p (t e)")
                mm(bank[5][:, 0:NB * NE], before_bf[:], flat, True, False)
                for t in range(NB - 1):
                    n = NB - 1 - t
                    mm(bank[5][:, (t + 1) * NE:NB * NE],
                       ones_bf[:], hot_bf[:, t:t + 1, :].to_broadcast([P, n, NE]), False, t == NB - 2)
                for t in range(NB):
                    m = mm(bank[6][:, 0:NE], ones_bf[:], hot_bf[:, t, :], t == 0, t == NB - 1)
                m.then_inc(S["cnt_ps"], 1)

            def turn_rows(u):
                if isinstance(u, int) and u < 2:
                    pe.wait_ge(S["x2_moved"], u + 1)
                else:
                    pe.wait_ge(S["xin_in"], 16 * (u - 1))
                if is_(u, 1, 99):
                    pe.wait_ge(S["xT_ready"], u)
                turn(bank[0], 0, X[:, u, :] if isinstance(u, int) and u < 2 else xin).then_inc(S["t_ps"], 1)

            def up_one(u, w1):
                pe.wait_ge(S["xT_ready"], u + 1)
                if is_(u, 1, 99):
                    pe.wait_ge(S["sil_ready"], u)
                for c in range(DC):
                    t = mm(bank[2][:], xT[:, c, :], w1(c), c == 0, c == DC - 1)
                t.then_inc(S["h1_ps"], 1)

            def up_three(u, w3):
                if is_(u, 1, 99):
                    pe.wait_ge(S["hh_ready"], u)
                else:
                    pe.wait_ge(S["o_step"], 4 * NB - 1)
                for c in range(DC):
                    t = mm(bank[3][:], xT[:, c, :], w3(c), c == 0, c == DC - 1)
                t.then_inc(S["h3_ps"], 1)

            def turn_hidden(u):
                pe.wait_ge(S["hh_ready"], u + 1)
                if is_(u, 1, 99):
                    pe.wait_ge(S["hhT_ready"], u)
                turn(bank[1], 0, hh, HC).then_inc(S["hhT_ps"], 1)

            def down(u, w2):
                pe.wait_ge(S["hhT_ready"], u + 1)
                if is_(u, 1, 99):
                    pe.wait_ge(S["y_taken"], u)
                for c in range(HC):
                    t = mm(bank[4][:, 0:D], hhT[:, c, :], w2(c), c == 0, c == HC - 1)
                t.then_inc(S["y_ps"], 1)

            def up_shared(u):
                up_one(u, lambda c: s_w1[:, c, :])
                up_three(u, lambda c: s_w3[:, c, :])

            def down_shared(u):
                down(u, lambda c: s_w2[:, c, :])

            def expert_of(k):
                at = blk_e[:, k:k + 1] if isinstance(k, int) else blk_e[:, bass.ds(k, 1)]
                return pe.value_load(at, min_val=0, max_val=NE - 1)

            def up_block(u, k):
                e = expert_of(k)
                one = bass.ds(e, 1)
                up_one(u, lambda c: e_w1[:, c, one, :].rearrange("p a n -> p (a n)"))
                up_three(u, lambda c: e_w3[:, c, one, :].rearrange("p a n -> p (a n)"))

            def down_block(u, k):
                one = bass.ds(expert_of(k), 1)
                down(u, lambda c: e_w2[:, c, one, :].rearrange("p a n -> p (a n)"))

            pe.wait_ge(S["w_moe"], 16 * (3 + 3 * NE))
            pe.wait_ge(S["sub_done"], 4 * NB)
            pe.wait_ge(S["k_done"], NB)
            turn_rows(0)
            up_shared(0)
            x_step(NB + 2)
            turn_rows(1)
            turn_hidden(0)
            up_one(1, lambda c: s_w1[:, c, :])
            counts()
            up_three(1, lambda c: s_w3[:, c, :])
            turn_rows(2)
            down_shared(0)
            with pe.Fori(2, FIRST) as u:
                turn_hidden(u - 1)
                turn_rows(u + 1)
                up_shared(u)
                down_shared(u - 1)
            pe.wait_ge(S["experts_ready"], 1)
            turn_hidden(FIRST - 1)
            turn_rows(FIRST + 1)
            up_block(FIRST, 0)
            down_shared(FIRST - 1)
            with pe.Fori(1, BLOCKS) as k:
                turn_hidden(k + (FIRST - 1))
                turn_rows(k + (FIRST + 1))
                up_block(k + FIRST, k)
                down_block(k + (FIRST - 1), k - 1)
            turn_hidden(U2 - 1)
            turn_rows(U2 + 1)
            up_shared(U2)
            down_block(U2 - 1, BLOCKS - 1)
            with pe.Fori(U2 + 1, U2 + REST - 1) as u:
                turn_hidden(u - 1)
                turn_rows(u + 1)
                up_shared(u)
                down_shared(u - 1)
            turn_hidden(U2 + REST - 2)
            up_shared(U2 + REST - 1)
            down_shared(U2 + REST - 2)
            turn_hidden(U2 + REST - 1)
            down_shared(U2 + REST - 1)

        @block.scalar
        def _(act):
            def f(out, in_, func, **kw):
                return act.activation(out, in_, func, **kw)

            def is_(i, lo, hi):
                return not isinstance(i, int) or lo <= i < hi

            def take_hT(b, ps, ready, bk, w, bias):
                act.wait_ge(S[ps], b + 1)
                for c in range(DC):
                    t = f(hT[:, c, :], bk[:, c * P:(c + 1) * P], ACT.Identity,
                          scale=w[:, c:c + 1], bias=bias[:, c:c + 1])
                t.then_inc(S[ready], 1)

            def take_h(b):
                take_hT(b, "hT_ps", "hT_ready", bank[0], ln1_w, ln1_b)

            def take_yT(b):
                act.wait_ge(S["yT_ps"], b + 1)
                f(yT[:].rearrange("p c s -> p (c s)"), bank[7][:, 0:D], ACT.Copy).then_inc(S["yT_ready"], 1)

            def take_v(b, odd):
                act.wait_ge(S["gv_ps"], b + 1)
                if is_(b, 2, NB):
                    act.wait_ge(S["av_ps"], b - 1)
                f(v_pair[odd], bank[3][:, D:2 * D], ACT.Copy).then_inc(S["v_ready"], 1)

            def take_u(b, odd):
                act.wait_ge(S["gv_ps"], b + 1)
                if is_(b, 2, NB):
                    act.wait_ge(S["mish_done"], b - 1)
                f(u_raw[odd][:], bank[3][:, 0:D], ACT.Copy).then_inc(S["u_ready"], 1)

            def take_qkT(b):
                act.wait_ge(S["qkT_ps"], b + 1)
                f(qT[:].rearrange("p c s -> p (c s)"), bank[4][:, 0:D], ACT.Copy)
                for j in range(2):
                    lo, hi = j * RD, (j + 1) * RD
                    t = f(k_pad[lo:hi, j::2, :],
                          bank[4][lo:hi, D:2 * D].rearrange("p (c s) -> p c s", c=DC), ACT.Copy)
                t.then_inc(S["qkT_ready"], 1)

            def take_gs(b):
                act.wait_ge(S["gs_ps"], b + 1)
                if is_(b, 1, NB):
                    act.wait_ge(S["gn_small"], 5 * b)
                f(gsum[:].rearrange("p h e -> p (h e)"), bank[0][:, 0:RH * 8], ACT.Copy).then_inc(S["gs_copy"], 1)

            def mish_first(b):
                act.wait_ge(S["clamp_done"], b + 1)
                if is_(b, 1, NB):
                    act.wait_ge(S["mish_done"], b)
                    act.wait_ge(S["mish_act"], 4 * b)
                f(m_e[:], uc[:], ACT.Exp).then_inc(S["mish_act"], 1)
                act.wait_ge(S["mish_act"], 4 * b + 1)
                f(m_e[:], m_e[:], ACT.Square, bias=1.0).then_inc(S["mish_act"], 1)
                act.wait_ge(S["mish_act"], 4 * b + 2)
                f(m_r[:], m_e[:], ACT.Ln, bias=1.0).then_inc(S["mish_act"], 1)

            def mish_last(b):
                act.wait_ge(S["mish_act"], 4 * b + 3)
                f(m_r[:], m_r[:], ACT.Exp, scale=-1.0).then_inc(S["mish_act"], 1)

            def a_step(i, odd):
                if is_(i, 1, NB + 1):
                    mish_first(i - 1)
                if is_(i, 3, NB + 3):
                    take_yT(i - 3)
                if is_(i, 2, NB + 2):
                    take_gs(i - 2)
                if is_(i, 1, NB + 1):
                    mish_last(i - 1)
                if is_(i, 0, NB):
                    take_u(i, odd)
                if is_(i, 0, NB - 1):
                    take_h(i + 1)
                if is_(i, 0, NB):
                    take_qkT(i)
                    take_v(i, odd)

            act.wait_ge(S["consts"], 48)
            act.wait_ge(S["setup"], 1)
            take_h(0)
            for i in range(4):
                a_step(i, i % 2)
            with act.Fori(2, HALF - 1) as pair:
                a_step(pair * 2, 0)
                a_step(pair * 2 + 1, 1)
            a_step(NB - 2, 0)
            a_step(NB - 1, 1)

            def take_z(b):
                take_hT(b, "zT_ps", "zT_ready", bank[1], ln2_w, ln2_b)

            def gelu(b, odd):
                act.wait_ge(S["f_ps"], b + 1)
                if is_(b, 2, NB):
                    act.wait_ge(S["f2_ps"], b - 1)
                for c in range(DC):
                    t = f(gT[:, odd, c, :], bank[4 + 2 * odd][:, c * P:(c + 1) * P], ACT.Gelu, bias=f1_b[:, c:c + 1])
                t.then_inc(S["g_ready"], 1)

            def b_step(i, odd):
                if is_(i, 0, NB):
                    gelu(i, odd)
                if is_(i, 0, NB - 1):
                    take_z(i + 1)

            take_z(0)
            take_yT(NB - 3)
            take_gs(NB - 2)
            mish_first(NB - 1)
            mish_last(NB - 1)
            gelu(0, 0)
            take_z(1)
            take_yT(NB - 2)
            take_gs(NB - 1)
            gelu(1, 1)
            take_z(2)
            gelu(2, 0)
            take_z(3)
            take_yT(NB - 1)
            b_step(3, 1)
            with act.Fori(2, HALF - 1) as pair:
                b_step(pair * 2, 0)
                b_step(pair * 2 + 1, 1)
            for i in range(NB - 2, NB):
                b_step(i, i % 2)

            def take_in(b):
                act.wait_ge(S["tx_ps"], b + 1)
                f(cxT[:].rearrange("p c s -> p (c s)"), bank[6][:], ACT.Copy).then_inc(S["cxT_ready"], 1)

            def exp(b, g):
                act.wait_ge(S["sub_done"], 4 * b + g + 1)
                f(prob[:, g, :], prob[:, g, :], ACT.Exp, scale=XD ** -0.5).then_inc(S["exp_done"], 1)

            def take_q(b):
                act.wait_ge(S["xq_ps"], b + 1)
                if is_(b, 1, NB):
                    act.wait_ge(S["xs_ps"], 4 * b)
                for c in range(DC):
                    t = f(xqT[:, c, :], bank[6][:, c * P:(c + 1) * P], ACT.Identity, bias=xq_b[:, c:c + 1])
                t.then_inc(S["xqT_ready"], 1)

            def take_p(b, g):
                act.wait_ge(S["p_ps"], 4 * b + g + 1)
                f(pT[:, g % 2, :], bank[4 + g % 2][:], ACT.Copy).then_inc(S["pT_ready"], 1)

            def take_x2(b):
                act.wait_ge(S["x2T_ps"], b + 1)
                f(x2T[:].rearrange("p c s -> p (c s)"), bank[7][:, 0:D], ACT.Copy).then_inc(S["x2T_ready"], 1)

            def x_step(i):
                here, scored, last, ended = is_(i, 0, NB), is_(i, 1, NB + 1), is_(i, 2, NB + 2), is_(i, 3, NB + 3)
                if here:
                    take_in(i)
                if last:
                    take_p(i - 2, 3)
                if ended:
                    take_x2(i - 3)
                if scored:
                    exp(i - 1, 0)
                    take_p(i - 1, 0)
                    exp(i - 1, 1)
                    take_p(i - 1, 1)
                    exp(i - 1, 2)
                if here:
                    take_q(i)
                if scored:
                    take_p(i - 1, 2)
                    exp(i - 1, 3)

            for i in range(4):
                x_step(i)
            with act.Fori(4, NB) as i:
                x_step(i)
            x_step(NB)
            x_step(NB + 1)


            def take_rows(u):
                act.wait_ge(S["t_ps"], u + 1)
                if is_(u, 1, 99):
                    act.wait_ge(S["h3_ps"], u)
                f(xT[:].rearrange("p c s -> p (c s)"), bank[0][:, 0:D], ACT.Copy).then_inc(S["xT_ready"], 1)

            def silu(u):
                act.wait_ge(S["h1_ps"], u + 1)
                if is_(u, 1, 99):
                    act.wait_ge(S["hh_ready"], u)
                f(sil[:], bank[2][:], ACT.Silu).then_inc(S["sil_ready"], 1)

            def take_block(u, k):
                act.wait_ge(S["y_ps"], u + 1)
                if is_(k, 1, 99):
                    act.wait_ge(S["ys_out"], 16 * k)
                f(y_st[:], bank[4][:, 0:D], ACT.Copy).then_inc(S["y_taken"], 1)

            take_rows(0)
            silu(0)
            x_step(NB + 2)
            take_rows(1)
            act.wait_ge(S["r_gate"], 1)
            f(gate[:, 0, :], gate[:, 0, :], ACT.Exp).then_inc(S["r_gate"], 1)
            silu(1)
            take_rows(2)
            with act.Fori(2, FIRST + 1) as u:
                silu(u)
                take_rows(u + 1)
            silu(1 + FIRST)
            take_rows(2 + FIRST)
            take_block(FIRST, 0)
            with act.Fori(2, BLOCKS) as k:
                silu(k + FIRST)
                take_rows(k + (FIRST + 1))
                take_block(k + (FIRST - 1), k - 1)
            silu(U2)
            take_rows(U2 + 1)
            take_block(U2 - 1, BLOCKS - 1)
            with act.Fori(U2 + 1, U2 + REST - 1) as u:
                silu(u)
                take_rows(u + 1)
            silu(U2 + REST - 1)

        @block.vector
        def _(ve):
            def is_(i, lo, hi):
                return not isinstance(i, int) or lo <= i < hi

            def stats(src, b, name, s6, m2, used, tiles=1):
                if is_(b, 1, NB):
                    ve.wait_ge(S[name], 2 * b)
                if is_(b, tiles, NB):
                    ve.wait_ge(S[used], b - (tiles - 1))
                at = 2 * (s6 is bn2)
                ve.memset(tick[:, at:at + 1], 0.0)
                ve.bn_stats(s6[:], src).then_inc(S[name], 1)
                ve.wait_ge(S[name], 2 * b + 1)
                ve.memset(tick[:, at + 1:at + 2], 0.0)
                ve.bn_aggr(m2[:], s6[:]).then_inc(S[name], 1)

            def normal(dst, src, b, name, m2, r, done):
                ve.wait_ge(S[name], 2 * b + 2)
                ve.tensor_scalar(dst, src, m2[:, 0:1], r[:], ALU.subtract, ALU.mult).then_inc(S[done], 1)

            ve.memset(eps[:], EPS)
            ve.memset(k_pad[:], 0.0).then_inc(S["setup"], 1)
            ve.wait_ge(S["x_first"], 16)

            def ln_stats(b):
                if isinstance(b, int) and b == 2:
                    ve.wait_ge(S["x_rest"], 16)
                stats(row(X, b), b, "ln_stat", bn, mv, "h_ready")

            def ln_apply(b):
                if is_(b, 1, NB):
                    ve.wait_ge(S["hT_ps"], b)
                normal(h[:], row(X, b), b, "ln_rstd", mv, rstd, "h_ready")

            ln_stats(0)
            ln_apply(0)
            ve.memset(zero[:], 0.0).then_inc(S["setup"], 1)
            ve.memset(v_aug[:], 1.0).then_inc(S["setup"], 1)
            ve.memset(ones_bf[:], 1.0).then_inc(S["setup"], 1)
            ve.memset(scan[:], 0.0).then_inc(S["setup"], 1)
            ve.wait_ge(S["consts"], 48)
            ve.tensor_copy(before_bf[:], before).then_inc(S["setup"], 1)
            ve.wait_ge(S["x_second"], 16)
            ln_stats(1)
            ve.wait_ge(S["tables"], 48)

            def rotary(b):
                ve.wait_ge(S["qk_ps"], b + 1)
                if is_(b, 1, NB):
                    ve.wait_ge(S["rot_done"], b)
                ps = bank[1][:].rearrange("p (h a d) -> p h a d", h=RH, a=2)
                ve.tensor_tensor(qk[:].rearrange("p a h d -> p h a d"), ps,
                                 rot_c[:].rearrange("p (h a) d -> p h a d", a=2), ALU.mult)
                pairs = bank[1][:].rearrange("p (g d) -> p g d", d=RD)[:, :, 0:ROT]\
                    .rearrange("p g (j t) -> p g j t", t=2)
                u = qk_u[:].rearrange("p g (j t) -> p g j t", t=2)
                s = rot_s[:].rearrange("p g (j t) -> p g j t", t=2)
                ve.tensor_tensor(u[:, :, :, 0], pairs[:, :, :, 1], s[:, :, :, 0], ALU.mult)
                ve.tensor_tensor(u[:, :, :, 1], pairs[:, :, :, 0], s[:, :, :, 1], ALU.mult)\
                    .then_inc(S["rot_mul"], 1)
                ve.wait_ge(S["rot_mul"], b + 1)
                q = qk[:].rearrange("p a h d -> p h a d")[:, :, :, 0:ROT]
                ve.tensor_tensor(q, q, qk_u[:].rearrange("p (h a) d -> p h a d", a=2), ALU.add)\
                    .then_inc(S["rot_done"], 1)

            def clamp(b, odd):
                ve.wait_ge(S["u_ready"], b + 1)
                ve.tensor_scalar(uc[:], u_raw[odd][:], U_MAX, None, ALU.min).then_inc(S["clamp_done"], 1)

            def mish(b, odd):
                if is_(b, 2, NB):
                    ve.wait_ge(S["gate_done"], b - 1)
                ve.wait_ge(S["mish_act"], 4 * b + 4)
                ve.scalar_tensor_tensor(m_pair[odd], m_r[:], -0.5, u_raw[odd][:], ALU.add, ALU.mult)\
                    .then_inc(S["mish_done"], 1)

            def decayed(b):
                ve.wait_ge(S["s_ps"], b + 1)
                ve.tensor_tensor(s_dec[:].rearrange("p h s -> p (h s)"), bank[5][:],
                                 decay[:].rearrange("p h s -> p (h s)"), ALU.mult).then_inc(S["s_dec_ready"], 1)

            def gn_stats(b, odd):
                ve.wait_ge(S["av_ps"], b + 1)
                if is_(b, 1, NB):
                    ve.wait_ge(S["gst_ready"], b)
                for n in range(RH):
                    t = ve.bn_stats(gst[:, n, 0:6], bank[6 - 4 * odd][:, n * RD:(n + 1) * RD])
                t.then_inc(S["gn_bn"], 1)
                ve.wait_ge(S["gn_bn"], b + 1)
                means = gst[:, :, 1:5:3]
                ve.tensor_tensor(gst[:, :, 6:8], means, means, ALU.mult).then_inc(S["gst_ready"], 1)

            def gn_var(b):
                ve.wait_ge(S["gs_copy"], b + 1)
                if is_(b, 1, NB):
                    ve.wait_ge(S["gn_small"], 5 * b)
                    ve.wait_ge(S["gn_ab"], 3 * b)

                ve.tensor_tensor(g_sum2[:], gsum[:, :, 1:3], gsum[:, :, 4:6], ALU.add).then_inc(S["gn_small"], 1)
                ve.tensor_tensor(gv[:, 0, :], gsum[:, :, 6], gsum[:, :, 7], ALU.add).then_inc(S["gn_small"], 1)
                ve.wait_ge(S["gn_small"], 5 * b + 2)
                s0, s1 = g_sum2[:, :, 0], g_sum2[:, :, 1]
                ve.scalar_tensor_tensor(gv[:, 1, :], s0, 0.25, s0, ALU.mult, ALU.mult).then_inc(S["gn_small"], 1)
                ve.wait_ge(S["gn_small"], 5 * b + 3)
                ve.scalar_tensor_tensor(gv[:, 2, :], s1, 1.0 / RD, gv[:, 1, :], ALU.mult, ALU.subtract).then_inc(S["gn_small"], 1)
                ve.wait_ge(S["gn_small"], 5 * b + 4)
                ve.scalar_tensor_tensor(gv[:, 3, :], gv[:, 0, :], 0.5, gv[:, 2, :], ALU.mult, ALU.add)\
                    .then_inc(S["gn_small"], 1)

            def gn_apply(b, odd):
                ve.wait_ge(S["gn_rstd"], 2 * b + 2)
                if is_(b, 1, NB):
                    ve.wait_ge(S["yn_step"], 2 * b)
                A, mA, B = gv[:, 4, :], gv[:, 5, :], gv[:, 6, :]
                ve.tensor_tensor(A, g_rstd[:], gn[:, 0, :], ALU.mult).then_inc(S["gn_ab"], 1)
                ve.wait_ge(S["gn_ab"], 3 * b + 1)
                ve.scalar_tensor_tensor(mA, g_sum2[:, :, 0], 0.5, A, ALU.mult, ALU.mult).then_inc(S["gn_ab"], 1)
                ve.wait_ge(S["gn_ab"], 3 * b + 2)
                ve.tensor_tensor(B, gn[:, 1, :], mA, ALU.subtract).then_inc(S["gn_ab"], 1)
                if is_(b, 1, NB):
                    ve.wait_ge(S["yT_ps"], b)
                y3 = yn[:].rearrange("p (h d) -> p h d", h=RH)

                def wide(v4):
                    return v4.rearrange("p (h a) -> p h a", a=1).to_broadcast([P, RH, RD])

                ve.tensor_tensor(y3, bank[6 - 4 * odd][:, 0:D].rearrange("p (h d) -> p h d", h=RH), wide(A), ALU.mult)\
                    .then_inc(S["yn_step"], 1)
                ve.wait_ge(S["gn_ab"], 3 * b + 3)
                ve.wait_ge(S["yn_step"], 2 * b + 1)
                ve.tensor_tensor(y3, y3, wide(B), ALU.add).then_inc(S["yn_step"], 1)
                ve.wait_ge(S["yn_step"], 2 * b + 2)
                ve.wait_ge(S["mish_done"], b + 1)
                ve.scalar_tensor_tensor(yn[:], m_pair[odd], -2.0, yn[:], ALU.mult, ALU.mult).then_inc(S["gate_done"], 1)

            def y_sum(b):
                ve.wait_ge(S["o_ps"], b + 1)
                ve.tensor_tensor(row(Y, b), bank[7][:, 0:D], row(X, b), ALU.add).then_inc(S["y_sum"], 1)

            def a_step(i, odd):
                if is_(i, 0, NB):
                    rotary(i)
                if is_(i, 2, NB + 2):
                    gn_var(i - 2)
                if is_(i, 0, NB - 1):
                    ln_apply(i + 1)
                if is_(i, 0, NB):
                    clamp(i, odd)
                if is_(i, 3, NB + 3):
                    y_sum(i - 3)
                if is_(i, 1, NB + 1):
                    decayed(i - 1)
                    mish(i - 1, 1 - odd)
                if is_(i, 0, NB - 2):
                    ln_stats(i + 2)
                if is_(i, 2, NB + 2):
                    gn_apply(i - 2, odd)
                if is_(i, 1, NB + 1):
                    gn_stats(i - 1, 1 - odd)

            for i in range(4):
                if i == 2:
                    ve.wait_ge(S["w_rest"], 112)
                a_step(i, i % 2)
                if i == 2:
                    ve.wait_ge(S["masks"], 80)
                    for g in range(4):
                        one = slice(32 * g, 32 * g + 1)
                        t = ve.tensor_scalar(mask_add[one, :], mask_row[one, :], 0.0, MASKED, ALU.is_equal, ALU.mult)
                    t.then_inc(S["setup"], 1)
                    ve.tensor_copy(mask_mul[:], mask_col[:]).then_inc(S["setup"], 1)
                    ve.wait_ge(S["setup"], 8)
            with ve.Fori(2, HALF - 1) as pair:
                a_step(pair * 2, 0)
                a_step(pair * 2 + 1, 1)
            a_step(NB - 2, 0)

            def z_stats(b, odd):
                stats(row(Y, b), b, "z_stat", bn, z_mv[:, odd, :], "z_ready", 2)

            def z_apply(b, odd):
                if is_(b, 1, NB):
                    ve.wait_ge(S["zT_ps"], b)
                normal(h[:], row(Y, b), b, "z_rstd", z_mv[:, odd, :], z_rs[:, odd, :], "z_ready")

            def ff_sum(b, odd):
                ve.wait_ge(S["f2_ps"], b + 1)
                ve.wait_ge(S["base_done"], 2 * b + 2)
                xb = row(X, b)
                ve.tensor_tensor(xb, bank[5 + 2 * odd][:, 0:D], xb, ALU.add).then_inc(S["ff_sum"], 1)
                ve.wait_ge(S["ff_sum"], b + 1)
                stats(xb, b, "x1_stat", bn2, x1_mv[:, odd, :], "x1_done", 2)

            def x1_apply(b, odd):
                normal(row(X, b), row(X, b), b, "x1_rstd", x1_mv[:, odd, :], x1_rs[:, odd, :], "x1_done")

            def b_step(i, odd):
                if is_(i, 0, NB - 2):
                    z_apply(i + 2, odd)
                if is_(i, 0, NB - 3):
                    z_stats(i + 3, 1 - odd)
                if is_(i, 1, NB + 1):
                    ff_sum(i - 1, 1 - odd)
                if is_(i, 2, NB + 2):
                    x1_apply(i - 2, odd)

            ve.wait_ge(S["ln_stat"], 2 * NB)
            ve.wait_ge(S["h_ready"], NB)
            ve.wait_ge(S["y_sum"], 3)
            z_stats(0, 0)
            z_stats(1, 1)
            a_step(NB - 1, 1)
            ve.wait_ge(S["hT_ps"], NB)
            z_apply(0, 0)
            decayed(NB - 1)
            gn_var(NB - 2)
            z_apply(1, 1)
            z_stats(2, 0)
            y_sum(NB - 3)
            gn_apply(NB - 2, 0)
            mish(NB - 1, 1)
            gn_stats(NB - 1, 1)
            gn_var(NB - 1)
            z_apply(2, 0)
            y_sum(NB - 2)
            gn_apply(NB - 1, 1)
            z_stats(3, 1)
            b_step(1, 1)
            y_sum(NB - 1)
            ve.wait_ge(S["y_sum"], NB)
            b_step(2, 0)
            b_step(3, 1)
            with ve.Fori(2, HALF - 2) as pair:
                b_step(pair * 2, 0)
                b_step(pair * 2 + 1, 1)
            for i in range(NB - 4, NB + 1):
                b_step(i, i % 2)

            def take_logits(b):
                ve.wait_ge(S["l_ps"], b + 1)
                if is_(b, 1, NB):
                    ve.wait_ge(S["best_done"], 2 * b)
                ve.tensor_copy(logit[:], bank[7][:, 480:480 + NE]).then_inc(S["l_done"], 1)

            def sort(b):
                ve.wait_ge(S["l_done"], b + 1)
                if is_(b, 1, NB):
                    ve.wait_ge(S["top_done"], b)
                ve.memset(tick[:, 4:5], 0.0)
                ve.max(best[:], logit[:]).then_inc(S["best_done"], 1)

            def find(b):
                ve.wait_ge(S["best_done"], 2 * b + 1)
                ve.memset(tick[:, 5:6], 0.0)
                ve.max_index(best_at[:], best[:], logit[:]).then_inc(S["best_done"], 1)

            def keep(b):
                ve.wait_ge(S["best_done"], 2 * b + 2)
                ve.tensor_copy(row(top, b), best[:, 0:TOP])
                ve.tensor_copy(row(top_f, b), best_at[:, 0:TOP]).then_inc(S["top_done"], 1)

            def x_out(b):
                ve.wait_ge(S["pv_ps"], 4 * b + 4)
                if is_(b, 1, NB):
                    ve.wait_ge(S["o_step"], 4 * b)
                    ve.wait_ge(S["x2_done"], b)
                o = bank[3][:, 0:XH * (XD + 1)].rearrange("p (h d) -> p h d", h=XH)
                ve.reciprocal(rec[:, 0, :], o[:, :, XD]).then_inc(S["o_step"], 1)
                ve.wait_ge(S["o_step"], 4 * b + 1)
                ve.tensor_tensor(rec[:, 1, :], rec[:, 0, :], mask_mul[:], ALU.mult).then_inc(S["o_step"], 1)
                ve.wait_ge(S["o_step"], 4 * b + 2)
                ve.tensor_tensor(t_out[:].rearrange("p (h d) -> p h d", h=XH), o[:, :, 0:XD],
                                 rec[:, 1, :].rearrange("p (h a) -> p h a", a=1).to_broadcast([P, XH, XD]),
                                 ALU.mult).then_inc(S["o_step"], 1)
                ve.wait_ge(S["o_step"], 4 * b + 3)
                ve.tensor_tensor(t_out[:], t_out[:], row(X, b), ALU.add).then_inc(S["o_step"], 1)
                ve.wait_ge(S["o_step"], 4 * b + 4)
                stats(t_out[:], b, "x2_stat", bn, mv, "x2_done")

            def x2_apply(b):
                if is_(b, 1, NB):
                    ve.wait_ge(S["x2T_ps"], b)
                    ve.wait_ge(S["x2_moved"], b)
                normal(x2s[:], t_out[:], b, "x2_rstd", mv, rstd, "x2_done")

            def x_max(b, g):
                ve.wait_ge(S["xs_ps"], 4 * b + g + 1)
                if is_(b, 1, NB):
                    ve.wait_ge(S["sub_done"], 4 * b - 3 + g)
                ve.tensor_reduce(s_max[:, g, :], bank[g % 2][:].rearrange("p (s k) -> p s k", s=4), AX.X, ALU.max)\
                    .then_inc(S["max_done"], 1)

            def x_sub(b, g):
                ve.wait_ge(S["max_done"], 4 * b + g + 1)
                if is_(b, 1, NB):
                    ve.wait_ge(S["p_ps"], 4 * b - 3 + g)
                ve.tensor_tensor(prob[:, g, :].rearrange("p (s k) -> p s k", s=4),
                                 bank[g % 2][:].rearrange("p (s k) -> p s k", s=4),
                                 s_max[:, g, :].rearrange("p (s a) -> p s a", a=1).to_broadcast([P, 4, P]),
                                 ALU.subtract).then_inc(S["sub_done"], 1)

            def take_k(b):
                ve.wait_ge(S["xk_ps"], b + 1)
                if is_(b, 1, NB):
                    ve.wait_ge(S["xs_ps"], 4 * b)
                for c in range(DC):
                    t = ve.scalar_tensor_tensor(
                        k_bd[:, c, :, :],
                        bank[2][:, c * P:(c + 1) * P].rearrange("p (a k) -> p a k", a=1).to_broadcast([P, 2, P]),
                        xk_b[:, c:c + 1],
                        half_of.rearrange("p (j a) -> p j a", a=1).to_broadcast([P, 2, P]), ALU.add, ALU.mult)
                t.then_inc(S["k_done"], 1)

            def take_v(b):
                ve.wait_ge(S["xv_ps"], b + 1)
                if is_(b, 1, NB):
                    ve.wait_ge(S["v_moved"], b)
                ve.tensor_tensor(v_tmp[:].rearrange("p h d -> p (h d)"), bank[7][:, 0:D], xv_b[:], ALU.add)\
                    .then_inc(S["xv_done"], 1)

            def x_step(i):
                here, scored, last, ended = is_(i, 0, NB), is_(i, 1, NB + 1), is_(i, 2, NB + 2), is_(i, 3, NB + 3)
                if scored:
                    x_max(i - 1, 0)
                    x_sub(i - 1, 0)
                    x_max(i - 1, 1)
                    x_sub(i - 1, 1)
                if ended:
                    take_logits(i - 3)
                if last:
                    x_out(i - 2)
                if ended:
                    sort(i - 3)
                if scored:
                    x_max(i - 1, 2)
                    x_sub(i - 1, 2)
                    x_max(i - 1, 3)
                if ended:
                    find(i - 3)
                if here:
                    take_k(i)
                if scored:
                    x_sub(i - 1, 3)
                if ended:
                    keep(i - 3)
                if last:
                    x2_apply(i - 2)
                if here:
                    take_v(i)

            x_step(0)
            x1_apply(NB - 1, 1)
            ve.wait_ge(S["x1_stat"], 2 * NB)
            ve.wait_ge(S["z_ready"], NB)
            ve.wait_ge(S["x1_done"], NB)
            for i in range(1, 4):
                x_step(i)
            with ve.Fori(4, NB) as i:
                x_step(i)
            x_step(NB)
            x_step(NB + 1)

            def gated(u):
                ve.wait_ge(S["h3_ps"], u + 1)
                ve.wait_ge(S["sil_ready"], u + 1)
                ve.tensor_tensor(hh[:], bank[3][:], sil[:], ALU.mult).then_inc(S["hh_ready"], 1)

            def take_hidden(u):
                ve.wait_ge(S["hhT_ps"], u + 1)
                ve.tensor_copy(hhT[:].rearrange("p c s -> p (c s)"), bank[1][:]).then_inc(S["hhT_ready"], 1)

            def take_shared(u, t):
                ve.wait_ge(S["y_ps"], u + 1)
                ve.tensor_tensor(row(Y, t), bank[4][:, 0:D], row(X, t), ALU.add).then_inc(S["y_taken"], 1)

            gated(0)
            x_step(NB + 2)
            take_hidden(0)

            ve.wait_ge(S["top_done"], NB)
            ve.tensor_tensor(gate[:, 0, :], top[:, :, 1], top[:, :, 0], ALU.subtract).then_inc(S["r_gate"], 1)
            numbers = expert_no.rearrange("p (a e) -> p a e", a=1).to_broadcast([P, NB, NE])
            for j in range(TOP):
                m = ve.tensor_tensor(hot[:, j, :, :], top_f[:, :, j:j + 1].to_broadcast([P, NB, NE]), numbers,
                                     ALU.is_equal)
            m.then_inc(S["r_dve"], 1)
            ve.wait_ge(S["r_dve"], 1)
            ve.tensor_tensor(hot_bf[:], hot[:, 0, :, :], hot[:, 1, :, :], ALU.add).then_inc(S["r_dve"], 1)
            ve.wait_ge(S["r_gate"], 2)
            ve.tensor_scalar(gate[:, 2, :], gate[:, 0, :], 1.0, None, ALU.add).then_inc(S["r_gate"], 1)
            ve.wait_ge(S["r_gate"], 3)
            ve.reciprocal(gate[:, 1, :], gate[:, 2, :]).then_inc(S["r_gate"], 1)
            ve.wait_ge(S["r_gate"], 4)
            ve.tensor_tensor(gate[:, 2, :], gate[:, 0, :], gate[:, 1, :], ALU.mult).then_inc(S["r_gate"], 1)
            ve.wait_ge(S["cnt_ps"], 1)
            ve.tensor_scalar(cnt_i[:, 0, :], bank[6][:, 0:NE], float(P - 1), None, ALU.add).then_inc(S["r_dve"], 1)
            ve.wait_ge(S["r_dve"], 3)
            ve.tensor_scalar(cnt_i[:, 1, :], cnt_i[:, 0, :], 7, None, ALU.logical_shift_right).then_inc(S["r_dve"], 1)
            ve.wait_ge(S["r_dve"], 4)
            ve.tensor_copy(scan[:, 0, NE:], cnt_i[:, 1, :]).then_inc(S["r_dve"], 1)
            ve.wait_ge(S["r_dve"], 5)
            ve.tensor_tensor(scan[:, 1, NE:], scan[:, 0, NE:], scan[:, 0, NE - 1:2 * NE - 1], ALU.add).then_inc(S["r_dve"], 1)
            ve.wait_ge(S["r_dve"], 6)
            ve.tensor_tensor(scan[:, 0, NE:], scan[:, 1, NE:], scan[:, 1, NE - 2:2 * NE - 2], ALU.add).then_inc(S["r_dve"], 1)
            ve.wait_ge(S["r_dve"], 7)
            ve.tensor_tensor(scan[:, 1, NE:], scan[:, 0, NE:], scan[:, 0, NE - 4:2 * NE - 4], ALU.add).then_inc(S["r_dve"], 1)
            ve.wait_ge(S["r_dve"], 8)
            ve.tensor_copy(cnt[:, 0, :], cnt_i[:, 1, :]).then_inc(S["r_dve"], 1)
            ve.wait_ge(S["r_dve"], 9)
            ve.tensor_tensor(cnt[:, 1, :], scan[:, 1, NE:], cnt[:, 0, :], ALU.subtract).then_inc(S["r_dve"], 1)
            ve.wait_ge(S["r_dve"], 10)
            ve.scalar_tensor_tensor(
                pos[:], cnt[:, 1:2, :].to_broadcast([P, NB, NE]), float(P),
                bank[5][:, 0:NB * NE].rearrange("p (t e) -> p t e", t=NB), ALU.mult, ALU.add).then_inc(S["r_dve"], 1)
            ve.wait_ge(S["r_dve"], 11)
            ve.tensor_tensor(pos_e[:, 0, :, :], hot[:, 0, :, :], pos[:], ALU.mult).then_inc(S["r_dve"], 1)
            ve.wait_ge(S["r_dve"], 12)
            ve.tensor_tensor(pos_e[:, 1, :, :], hot[:, 1, :, :], pos[:], ALU.mult).then_inc(S["r_dve"], 1)
            ve.wait_ge(S["r_dve"], 13)
            ve.tensor_reduce(pos_f[:].rearrange("p j t -> p (j t)"),
                                     pos_e[:].rearrange("p j t e -> p (j t) e"), AX.X, ALU.add).then_inc(S["r_dve"], 1)
            ve.wait_ge(S["r_dve"], 14)
            ve.tensor_copy(slot[:], pos_f[:]).then_inc(S["r_dve"], 1)
            ve.wait_ge(S["r_dve"], 15)
            ve.memset(blk_f[:, 1, :], 0.0).then_inc(S["slots_ready"], 1)
            gated(1)
            ve.tensor_tensor(blk[:], scan[0:1, 1:2, NE:].to_broadcast([1, BLOCKS, NE]),
                                    block_no[0:1, :].rearrange("p (b a) -> p b a", a=1).to_broadcast([1, BLOCKS, NE]),
                                    ALU.is_le).then_inc(S["r_dve"], 1)
            ve.wait_ge(S["r_dve"], 16)
            ve.tensor_reduce(blk_f[:, 0, :], blk[:], AX.X, ALU.add).then_inc(S["r_dve"], 1)
            ve.wait_ge(S["r_dve"], 17)
            ve.tensor_scalar(blk_e[:], blk_f[:, 0, :], float(NE - 1), None, ALU.min).then_inc(S["experts_ready"], 1)

            take_shared(0, 0)
            with ve.Fori(2, FIRST) as u:
                take_hidden(u - 1)
                gated(u)
                take_shared(u - 1, u - 1)
            take_hidden(FIRST - 1)
            gated(FIRST)
            take_shared(FIRST - 1, FIRST - 1)
            with ve.Fori(FIRST + 1, U2 + 1) as u:
                take_hidden(u - 1)
                gated(u)

            def combine(m):
                mvs = (x1_mv, z_mv)[m % 2]
                for side in range(2):
                    n, t = 2 * m + side, HALF * side + m
                    total = (out_t, t_out[:])[side]
                    if m:
                        ve.wait_ge(S["c_done"], n - 1)
                    ve.wait_ge(S[f"gath{n % 4}"], 16 * TOP * (n // 4 + 1))
                    ve.wait_ge(S["y_taken"], t + 1 if t < FIRST else BLOCKS + t + 1)
                    ve.scalar_tensor_tensor(total, yg[:, n % 4, 0, :], gate[:, 1, t:t + 1], Y[:, t, :],
                                            ALU.mult, ALU.add).then_inc(S["c_step"], 1)
                    ve.wait_ge(S["c_step"], 2 * n + 1)
                    ve.scalar_tensor_tensor(total, yg[:, n % 4, 1, :], gate[:, 2, t:t + 1], total,
                                            ALU.mult, ALU.add).then_inc(S["c_step"], 1)
                    ve.wait_ge(S["c_step"], 2 * n + 2)
                    stats(total, n, "c_stat", bn, mvs[:, side, :], "c_done", 4)

            def finish(m):
                mvs, rs = ((x1_mv, x1_rs), (z_mv, z_rs))[m % 2]
                ve.wait_ge(S["c_rstd"], 2 * m + 2)
                for side in range(2):
                    if m:
                        ve.wait_ge(S[f"out{side}"], 16 * m)
                    ve.tensor_scalar(out_sb[:, side, :], (out_t, t_out[:])[side], mvs[:, side, 0:1], rs[:, side, :],
                                     ALU.subtract, ALU.mult).then_inc(S["c_done"], 1)

            ve.wait_ge(S["r_gate"], 5)
            ve.wait_ge(S["x2_stat"], 2 * NB)
            ve.wait_ge(S["x2_done"], NB)
            for j in range(1, HALF + 2):
                u = U2 + j
                if j <= REST:
                    take_hidden(u - 1)
                if 2 <= j < REST + 2:
                    take_shared(u - 2, FIRST + j - 2)
                if j >= 2:
                    combine(j - 2)
                if j < REST:
                    gated(u)
                if j >= 2:
                    finish(j - 2)


def tables():
    half = np.arange(0, ROT, 2, dtype=np.float64)
    t = np.arange(P, dtype=np.float64)
    freqs = np.repeat(t[:, None] / 10000.0 ** (half / ROT), 2, axis=-1)
    scale = ((half + 0.4 * ROT) / (1.4 * ROT))[None, :] ** ((t - P // 2) / 512.0)[:, None]
    scale = np.concatenate((scale, scale), axis=-1)
    rot_c = np.ones((P, RH, 2, RD))
    rot_s = np.zeros((P, RH, 2, ROT))
    sign = np.where(np.arange(ROT) % 2 == 0, -1.0, 1.0)
    for n, s in enumerate((scale, 1.0 / scale)):
        rot_c[:, :, n, :ROT] = (np.cos(freqs) * s)[:, None, :]
        rot_s[:, :, n, :] = (np.sin(freqs) * s * sign)[:, None, :]
    gamma = 1.0 - 2.0 ** (-5.0 - np.arange(RH))
    apart = t[None, :] - t[:, None]
    decay = np.where(apart[:, None, :] >= 0, gamma[None, :, None] ** np.maximum(apart, 0)[:, None, :], 0.0)
    misc = np.zeros((P, 2 * P + NE + BLOCKS + 3))
    misc[:, 0:P] = 1.0 / P
    misc[:, P:2 * P] = np.arange(P)[:, None] < np.arange(P)[None, :]
    at = 2 * P
    misc[:, at:at + NE] = np.arange(NE)
    misc[:, at + NE:at + NE + BLOCKS] = np.arange(BLOCKS)
    at += NE + BLOCKS
    misc[:, at:at + 2] = (np.arange(P)[:, None] // XD) % 2 == np.arange(2)[None, :]
    misc[:, at + 2] = -0.5
    f = np.float32
    return {"rot_c": rot_c.reshape(P, 2 * RH, RD).astype(f), "rot_s": rot_s.reshape(P, 2 * RH, ROT).astype(f),
            "decay": decay.astype(f), "misc": misc.astype(f), "eye": np.eye(P, dtype=f)}


def kernel(**inputs):
    import concourse.bacc as _bacc
    from concourse.bass_utils import run_bass_kernel_spmd as _run

    g = {k: np.asarray(v) for k, v in inputs.items()}
    attn, cross, ffn = "L0_attn_", "L0_xattn_", "L0_ffn_"

    def columns(*names):
        return np.concatenate([g[n].reshape(DC, P).T for n in names], axis=1)

    mask = g["mask_BxS2_ik0"]
    order = [8 * c + 2 * r + j for r in range(4) for c in range(2) for j in range(2)]
    arrays = {
        "x": g["x"], "ctx": g["ctx_1024"],
        "wqkv": g[attn + "wqkv_w"], "wg": g[attn + "wg_w"], "wo": g[attn + "wo_w"],
        "w_f1": g[attn + "w1_w"], "w_f2": g[attn + "w2_w"], "f2_b": g[attn + "w2_b"],
        "gn_w": g[attn + "gn_w"], "gn_b": g[attn + "gn_b"],
        "cols": columns(attn + "ln1_w", attn + "ln1_b", attn + "ln2_w", attn + "ln2_b", attn + "w1_b",
                        cross + "bq", cross + "bk"),
        "xq": g[cross + "Wq"].T, "xk": g[cross + "Wk"].T, "xv": g[cross + "Wv"].T, "xv_b": g[cross + "bv"],
        "mask_row": mask[order].reshape(4, 4 * P), "mask_col": mask.T,
        "w_router": g[ffn + "w_router"], "w1": g[ffn + "w1"], "w3": g[ffn + "w3"], "w2": g[ffn + "w2"],
        "sw1": g[ffn + "sw1"], "sw3": g[ffn + "sw3"], "sw2": g[ffn + "sw2"],
    } | tables()
    nc = _bacc.Bacc("TRN2", target_bir_lowering=False, num_devices=1)
    feeds, aps = {}, {}
    for name, value in arrays.items():
        value = np.ascontiguousarray(value)
        feeds[f"in_{name}_dram"] = value
        aps[name] = nc.dram_tensor(f"in_{name}_dram", value.shape, mybir.dt.from_np(value.dtype),
                                   kind="ExternalInput").ap()
    aps["out"] = nc.dram_tensor("out_0_dram", (NB, P, D), F32, kind="ExternalOutput").ap()
    build(nc, aps)
    r = _run(nc, [feeds], core_ids=[0])
    return r.results[0]["out_0_dram"]
```
